# Optimizing a Trainium2 kernel written in Bass

```python
import numpy as np
import jax
import jax.numpy as jnp

def _softmax(x, axis=-1):
    return jax.nn.softmax(x, axis=axis)

def _gelu(x):
    return jax.nn.gelu(x, approximate=True)

def _silu(x):
    return jax.nn.silu(x)

def _sigmoid(x):
    return jax.nn.sigmoid(x)

def _layernorm(x, axis=-1, eps=1e-05):
    m = jnp.mean(x, axis=axis, keepdims=True)
    v = jnp.var(x, axis=axis, keepdims=True)
    return (x - m) / jnp.sqrt(v + eps)

def _scatter_add(tgt, idx, src, axis=0):
    return tgt.at[idx].add(src)

def _segment_sum(src, seg, n):
    return jax.ops.segment_sum(src, seg, n)
kernel_name = 'mk_seq_preln_d1_jaxref_r4_3ba65b'

def setup_inputs(seed: int=0):
    np.random.seed(seed)
    _w = jnp.asarray

    def _L0_attn_setup():
        import jax, jax.numpy as jnp
        import numpy as np
        D_MODEL = 256
        N_HEADS = 16
        HEAD_DIM = D_MODEL // N_HEADS
        D_FF = 1024
        WINDOW = 128
        LN_EPS = 1e-05
        NEG_INF = jnp.finfo(jnp.float32).min

        def layer_norm(x, w, b):
            mu = jnp.mean(x, axis=-1, keepdims=True)
            var = jnp.mean(jnp.square(x - mu), axis=-1, keepdims=True)
            return (x - mu) * jax.lax.rsqrt(var + LN_EPS) * w + b
        key = jax.random.key(seed)
        ks = jax.random.split(key, 12)
        B, L, D = (2, 512, D_MODEL)
        s = 1.0 / np.sqrt(D)
        inp = {'x': jax.random.normal(ks[0], (B, L, D), jnp.float32), 'Wq': jax.random.normal(ks[1], (D, D), jnp.float32) * s, 'bq': jnp.zeros((D,), jnp.float32), 'Wk': jax.random.normal(ks[2], (D, D), jnp.float32) * s, 'bk': jnp.zeros((D,), jnp.float32), 'Wv': jax.random.normal(ks[3], (D, D), jnp.float32) * s, 'bv': jnp.zeros((D,), jnp.float32), 'Wo': jax.random.normal(ks[4], (D, D), jnp.float32) * s, 'bo': jnp.zeros((D,), jnp.float32), 'W1': jax.random.normal(ks[5], (D, D_FF), jnp.float32) * s, 'b1': jnp.zeros((D_FF,), jnp.float32), 'W2': jax.random.normal(ks[6], (D_FF, D), jnp.float32) * (1.0 / np.sqrt(D_FF)), 'b2': jnp.zeros((D,), jnp.float32), 'ln1_w': jnp.ones((D,), jnp.float32), 'ln1_b': jnp.zeros((D,), jnp.float32), 'ln2_w': jnp.ones((D,), jnp.float32), 'ln2_b': jnp.zeros((D,), jnp.float32)}
        return inp
    _L0_attn_in = _L0_attn_setup()

    def _L0_ffn_setup():
        import math
        import jax, jax.numpy as jnp
        import numpy as np
        D_CONTENT = 256
        D_POSITION = 32
        NUM_TILES = 8
        BATCH = 8
        SEQ = 512

        def make_pe(seq_len, d_pos):
            pos = jnp.arange(seq_len, dtype=jnp.float32)[:, None]
            div = jnp.exp(jnp.arange(0, d_pos, 2, dtype=jnp.float32) * (-math.log(10000.0) / d_pos))
            ang = pos * div
            pe = jnp.zeros((seq_len, d_pos), dtype=jnp.float32)
            pe = pe.at[:, 0::2].set(jnp.sin(ang))
            pe = pe.at[:, 1::2].set(jnp.cos(ang))
            return pe
        key = jax.random.key(seed)
        k1, k2, k3, k4 = jax.random.split(key, 4)
        x = jax.random.normal(k1, (BATCH, SEQ, D_CONTENT), dtype=jnp.float32)
        tile_sigs = jax.random.normal(k2, (NUM_TILES, D_POSITION), dtype=jnp.float32)
        lim = 1.0 / math.sqrt(D_CONTENT)
        W = jax.random.uniform(k3, (NUM_TILES, D_CONTENT, D_CONTENT), minval=-lim, maxval=lim, dtype=jnp.float32)
        b = jax.random.uniform(k4, (NUM_TILES, D_CONTENT), minval=-lim, maxval=lim, dtype=jnp.float32)
        return {'x': x, 'tile_sigs': tile_sigs, 'W': W, 'b': b}
    _L0_ffn_in = _L0_ffn_setup()
    _d = {'L0_attn_x': _L0_attn_in['x'], 'L0_attn_Wq': _L0_attn_in['Wq'], 'L0_attn_bq': _L0_attn_in['bq'], 'L0_attn_Wk': _L0_attn_in['Wk'], 'L0_attn_bk': _L0_attn_in['bk'], 'L0_attn_Wv': _L0_attn_in['Wv'], 'L0_attn_bv': _L0_attn_in['bv'], 'L0_attn_Wo': _L0_attn_in['Wo'], 'L0_attn_bo': _L0_attn_in['bo'], 'L0_attn_W1': _L0_attn_in['W1'], 'L0_attn_b1': _L0_attn_in['b1'], 'L0_attn_W2': _L0_attn_in['W2'], 'L0_attn_b2': _L0_attn_in['b2'], 'L0_attn_ln1_w': _L0_attn_in['ln1_w'], 'L0_attn_ln1_b': _L0_attn_in['ln1_b'], 'L0_attn_ln2_w': _L0_attn_in['ln2_w'], 'L0_attn_ln2_b': _L0_attn_in['ln2_b'], 'L0_ffn_tile_sigs': _L0_ffn_in['tile_sigs'], 'L0_ffn_W': _L0_ffn_in['W'], 'L0_ffn_b': _L0_ffn_in['b']}
    _x0 = _d['L0_attn_x']
    _d['L0_attn_x'] = jax.random.normal(jax.random.fold_in(jax.random.key(seed), 1), (32, 512, 256), dtype=_x0.dtype)
    del _x0
    return _d

def reference(L0_attn_x, L0_attn_Wq, L0_attn_bq, L0_attn_Wk, L0_attn_bk, L0_attn_Wv, L0_attn_bv, L0_attn_Wo, L0_attn_bo, L0_attn_W1, L0_attn_b1, L0_attn_W2, L0_attn_b2, L0_attn_ln1_w, L0_attn_ln1_b, L0_attn_ln2_w, L0_attn_ln2_b, L0_ffn_tile_sigs, L0_ffn_W, L0_ffn_b):

    def _L0_attn_ref(x, Wq, bq, Wk, bk, Wv, bv, Wo, bo, W1, b1, W2, b2, ln1_w, ln1_b, ln2_w, ln2_b):
        import jax, jax.numpy as jnp
        import numpy as np
        D_MODEL = 256
        N_HEADS = 16
        HEAD_DIM = D_MODEL // N_HEADS
        D_FF = 1024
        WINDOW = 128
        LN_EPS = 1e-05
        NEG_INF = jnp.finfo(jnp.float32).min

        def layer_norm(x, w, b):
            mu = jnp.mean(x, axis=-1, keepdims=True)
            var = jnp.mean(jnp.square(x - mu), axis=-1, keepdims=True)
            return (x - mu) * jax.lax.rsqrt(var + LN_EPS) * w + b
        B, L, D = x.shape
        i = jnp.arange(L)[:, None]
        j = jnp.arange(L)[None, :]
        band = (j > i) | (i - j > WINDOW)
        bias = jnp.where(band, NEG_INF, 0.0).astype(x.dtype)
        h = layer_norm(x, ln1_w, ln1_b)
        q = (h @ Wq + bq).reshape(B, L, N_HEADS, HEAD_DIM)
        k = (h @ Wk + bk).reshape(B, L, N_HEADS, HEAD_DIM)
        v = (h @ Wv + bv).reshape(B, L, N_HEADS, HEAD_DIM)
        scale = 1.0 / np.sqrt(HEAD_DIM)
        scores = jnp.einsum('blhd,bmhd->bhlm', q, k) * scale + bias
        attn = jax.nn.softmax(scores, axis=-1)
        ctx = jnp.einsum('bhlm,bmhd->blhd', attn, v).reshape(B, L, D)
        x = x + ctx @ Wo + bo
        h2 = layer_norm(x, ln2_w, ln2_b)
        x = x + jax.nn.gelu(h2 @ W1 + b1) @ W2 + b2
        return x

    def _L0_ffn_ref(x, tile_sigs, W, b):
        import math
        import jax, jax.numpy as jnp
        import numpy as np
        D_CONTENT = 256
        D_POSITION = 32
        NUM_TILES = 8
        BATCH = 8
        SEQ = 512

        def make_pe(seq_len, d_pos):
            pos = jnp.arange(seq_len, dtype=jnp.float32)[:, None]
            div = jnp.exp(jnp.arange(0, d_pos, 2, dtype=jnp.float32) * (-math.log(10000.0) / d_pos))
            ang = pos * div
            pe = jnp.zeros((seq_len, d_pos), dtype=jnp.float32)
            pe = pe.at[:, 0::2].set(jnp.sin(ang))
            pe = pe.at[:, 1::2].set(jnp.cos(ang))
            return pe
        B, S, D = x.shape
        P = tile_sigs.shape[1]
        pe = make_pe(S, P)
        scores = jnp.einsum('sp,tp->st', pe, jnp.sign(tile_sigs))
        idx = jnp.argmax(scores, axis=-1)
        y_all = jnp.einsum('bsd,tod->bsto', x, W) + b
        idx4 = jnp.broadcast_to(idx[None, :, None, None], (B, S, 1, D))
        out = jnp.take_along_axis(y_all, idx4, axis=2)[:, :, 0]
        return out
    x = L0_attn_x
    x = x + _L0_attn_ref(_layernorm(x, axis=-1), L0_attn_Wq, L0_attn_bq, L0_attn_Wk, L0_attn_bk, L0_attn_Wv, L0_attn_bv, L0_attn_Wo, L0_attn_bo, L0_attn_W1, L0_attn_b1, L0_attn_W2, L0_attn_b2, L0_attn_ln1_w, L0_attn_ln1_b, L0_attn_ln2_w, L0_attn_ln2_b)
    x = x + _L0_ffn_ref(_layernorm(x, axis=-1), L0_ffn_tile_sigs, L0_ffn_W, L0_ffn_b)
    return x

_drawn_inputs = setup_inputs


def setup_inputs(seed=0):
    import zlib

    import numpy as np

    out = dict(_drawn_inputs(seed))
    spreads = {'L0_attn_bq': (0.0, 0.765),
     'L0_attn_bk': (0.0, 0.8),
     'L0_attn_bv': (0.0, 0.1),
     'L0_attn_bo': (0.0, 0.1),
     'L0_attn_b1': (0.0, 0.1),
     'L0_attn_b2': (0.0, 0.1),
     'L0_attn_ln1_w': (1.0, 0.2),
     'L0_attn_ln1_b': (0.0, 0.1),
     'L0_attn_ln2_w': (1.0, 0.2),
     'L0_attn_ln2_b': (0.0, 0.1)}
    factors = {'L0_ffn_b': 3.473}
    for name, (base, spread) in spreads.items():
        noise = np.random.default_rng([zlib.crc32(name.encode()), seed]).standard_normal(out[name].shape)
        drawn = base * np.exp(spread * noise) if base else spread * noise
        out[name] = jnp.asarray(drawn.astype(out[name].dtype))
    for name, factor in factors.items():
        out[name] = (out[name] * factor).astype(out[name].dtype)
    return out
```

```python
from contextlib import ExitStack
import math

import numpy as np

import concourse.bass as bass
from concourse import mybir

F32 = mybir.dt.float32
F32R = mybir.dt.float32r
I32 = mybir.dt.int32
U32 = mybir.dt.uint32
ALU = mybir.AluOpType
ACT = mybir.ActivationFunctionType
AX_X = mybir.AxisListType.X

P = 128
NB, L, D = 32, 512, 256
NT = L // P
KD = D // P
NH, HD = 16, 16
NPAIR = NH // 2
DFF = 1024
NM = DFF // P
NE, DPOS = 8, 32
WINDOW = 128
EPS = 1e-5
SCALE = 1.0 / math.sqrt(HD)
MASKED = -3.0e38
LOWEST = float(np.finfo(np.float32).min)
VW = HD + 1

SLOTS = P // NB
HALF = 4
NGROUP = -(-((L + NE * (SLOTS - 1)) // SLOTS) // (2 * HALF)) * 2 * HALF
NCOL = NGROUP + 2 * HALF
EMPTY = float(1 << 20)

Q_STACK = ("hi", "lo", "hi")
K_STACK = ("hi", "hi", "lo")
MAX_ROW = 3 * HD


def shape_constants():
    r = np.arange(P)
    parts = {}
    parts["ident"] = np.eye(P)
    q, k = r[:, None], r[None, :]
    parts["mask"] = np.concatenate([np.where(k >= q, 0.0, MASKED), np.where(k <= q, 0.0, MASKED)], 1)
    for name, stack, part in (("sel_qh", Q_STACK, "hi"), ("sel_ql", Q_STACK, "lo"),
                              ("sel_kh", K_STACK, "hi"), ("sel_kl", K_STACK, "lo")):
        m = np.zeros((P, NPAIR // KD, P))
        for p in range(NPAIR // KD):
            for par in range(2):
                for c in range(3):
                    if stack[c] == part:
                        for d in range(HD):
                            m[2 * HD * p + HD * par + d, p, 64 * par + HD * c + d] = 1.0
        parts[name] = m.reshape(P, -1)
    kcol = np.zeros((P, 1))
    for par in range(2):
        kcol[64 * par + MAX_ROW:64 * par + MAX_ROW + 2] = -1.0
    parts["minus_one_rows"] = kcol
    parts["before"] = (q < k).astype(np.float32)
    parts["ones"] = np.ones((P, P))
    parts["group_iota"] = np.broadcast_to(np.arange(NCOL), (P, NCOL))
    parts["slot_of_row"] = np.broadcast_to(r % SLOTS, (P, P))
    parts["first_row"] = (L * (r // SLOTS))[:, None]
    parts["position_plus_1"] = r[:, None] + P * np.arange(NT)[None, :] + 1
    parts["expert_rank"] = np.broadcast_to(NE - np.arange(NE), (P, NT, NE)).reshape(P, -1)
    pos = np.arange(L, dtype=np.float32)[:, None]
    div = np.exp((np.arange(0, DPOS, 2, dtype=np.float32) *
                  np.float32(-math.log(10000.0) / DPOS)).astype(np.float64)).astype(np.float32)
    ang = pos * div
    code = np.zeros((L, DPOS), np.float32)
    code[:, 0::2], code[:, 1::2] = np.sin(ang), np.cos(ang)
    codeT = np.zeros((P, L))
    codeT[:DPOS] = code.T
    parts["position_code"] = codeT
    at, cols = {}, 0
    for name, a in parts.items():
        at[name] = (cols, cols + a.shape[1])
        cols += a.shape[1]
    return np.ascontiguousarray(np.concatenate(list(parts.values()), 1).astype(np.float32)), at


def build(nc, x, Wq, bq, Wk, bk, Wv, bv, Wo, bo, W1, b1, W2, b2, ln1_w, ln1_b, ln2_w, ln2_b,
          sigs, We, be, consts, at, scratch, out):
    ctx = ExitStack()
    with ctx:
        def sb(name, shape, dt=F32):
            return ctx.enter_context(nc.sbuf_tensor(name, shape, dt))

        def sem(name):
            return ctx.enter_context(nc.semaphore(name))

        score_bank = [ctx.enter_context(nc.psum_tensor(f"score_bank{i}", [P, 512], F32)) for i in range(4)]
        ffn_bank = [ctx.enter_context(nc.psum_tensor(f"ffn_bank{i}", [P, 512], F32)) for i in range(2)]
        mix_bank = [ctx.enter_context(nc.psum_tensor(f"mix_bank{i}", [P, 512], F32)) for i in range(2)]
        select_bank = [ffn_bank[0], ffn_bank[1], score_bank[0], score_bank[1]]

        ident = sb("ident", [P, P])
        mask = sb("mask", [P, 2 * P])
        sel = {n: sb(n, [P, NPAIR // KD, P], F32R) for n in ("sel_qh", "sel_ql", "sel_kh", "sel_kl")}
        minus_one_rows = sb("minus_one_rows", [P, 1])
        wqkv_h = sb("wqkv_h", [P, KD, 3 * D], F32R)
        wqkv_l = sb("wqkv_l", [P, KD, 3 * D], F32R)
        wo_h = sb("wo_h", [P, KD, D], F32R)
        wo_l = sb("wo_l", [P, KD, D], F32R)
        w1_h = sb("w1_h", [P, KD, DFF], F32R)
        w1_l = sb("w1_l", [P, KD, DFF], F32R)
        w2 = sb("w2", [P, NM, D])
        qk_bias = sb("qk_bias", [P, 4])
        b1_col = sb("b1_col", [P, NM])
        ln_col = sb("ln_col", [P, 4, KD])
        bv_row = sb("bv_row", [P, D])
        bo_row = sb("bo_row", [P, D])
        b2_row = sb("b2_row", [P, D])
        minus_half = sb("minus_half", [P, NT])

        x_in = sb("x_in", [P, NT, D])
        normed = sb("normed", [P, NT, D])
        x1 = sb("x1", [P, NT, D])
        x_b2 = sb("x_b2", [P, NT, D])
        x2 = sb("x2", [P, NT, D])
        y = sb("y", [P, NT, D])
        ctxn = y
        nT_h = sb("nT_h", [P, KD, L], F32R)
        nT_l = sb("nT_l", [P, KD, L], F32R)
        qk_h = sb("qk_h", [P, 2, L], F32R)
        qk_l = sb("qk_l", [P, 2, L], F32R)
        q_pad = sb("q_pad", [P, NPAIR, 2, L], F32R)
        k_stack = sb("k_stack", [P, NPAIR, L], F32R)
        v_ones = sb("v_ones", [P, NT, NH * VW + HD])
        probs = sb("probs", [P, 4, 7 * 2 * P])
        ctxT = sb("ctxT", [P, 4, L])
        cn_h = sb("cn_h", [P, KD, L], F32R)
        cn_l = sb("cn_l", [P, KD, L], F32R)
        hidden = sb("hidden", [P, NM, L])
        maxT = sb("maxT", [16, L])
        row_max = sb("row_max", [P, NT, NH])
        max_parts = sb("max_parts", [P, NT, 2, 2, 2, 4])
        max_hi = sb("max_hi", [P, NT, 2, 2, 4], F32R)
        inv_sum = sb("inv_sum", [P, NT, NH])
        stats1 = sb("stats1", [P, NT, 6])
        mv1 = sb("mv1", [P, NT, 2])
        stats2 = sb("stats2", [P, NT, 6])
        mv2 = sb("mv2", [P, NT, 2])
        lnt = sb("lnt", [P, 8, NT])
        lnt2 = sb("lnt2", [P, 4, NT])
        row_index = sb("row_index", [P, NCOL], I32)
        gather_rows = [sb(f"gather_rows{i}", [P, HALF], I32) for i in range(2)]
        scatter_rows = [sb(f"scatter_rows{i}", [P, HALF], I32) for i in range(2)]
        group_expert = sb("group_expert", [P, NCOL], I32)
        assert NH * VW + HD >= (NH - 1) * VW + 32

        staged = probs[:, :, :].rearrange("p a b -> p (a b)")
        stage2 = hidden[:, :, :].rearrange("p a b -> p (a b)")
        wqkv_raw = staged[:, 0:KD * 3 * D].rearrange("p (k n) -> p k n", k=KD)
        wo_raw = staged[:, 1536:1536 + KD * D].rearrange("p (k n) -> p k n", k=KD)
        w1_raw = staged[:, 2048:2048 + KD * DFF].rearrange("p (k n) -> p k n", k=KD)
        route = staged[:, 4096:4096 + 1024]
        ncst = consts.shape[1]
        cst = stage2[:, 0:ncst]
        assert ncst <= NM * L

        def const(name):
            return cst[:, at[name][0]:at[name][1]]

        LEAD = 1
        loaded = sem("loaded")
        zeroed = sem("zeroed")
        dve_step = sem("dve_step")
        pool_step = sem("pool_step")
        setup_mm = sem("setup_mm")
        setup_dve = sem("setup_dve")
        ready = sem("ready")
        PER = {}

        def counted(name, n):
            s = sem(name)
            PER[id(s)] = n
            return s

        x_loaded = counted("x_loaded", 16)
        x_used = counted("x_used", 1)
        mv1_ready = counted("mv1_ready", 1)
        n1_ready = counted("n1_ready", 1)
        x1_ready = counted("x1_ready", 1)
        nT_ready = counted("nT_ready", KD)
        nTh_done = counted("nTh_done", KD)
        nTl_done = counted("nTl_done", KD)
        qk_ready = counted("qk_ready", 4)
        qkh_done = counted("qkh_done", 4)
        qkl_done = counted("qkl_done", 4)
        v_ready = counted("v_ready", 2)
        v_done = counted("v_done", 2)
        sel_ready = counted("sel_ready", 2 * NPAIR)
        qsel_done = counted("qsel_done", NPAIR)
        ksel_done = counted("ksel_done", NPAIR)
        s_ready = counted("s_ready", NH)
        max_done = counted("max_done", NH)
        parts_done = counted("parts_done", 2)
        maxT_ready = counted("maxT_ready", 2)
        maxT_done = counted("maxT_done", 2)
        max_rows = [counted(f"max_rows{i}", 64) for i in range(2)]
        sT_ready = counted("sT_ready", NPAIR * NT)
        exp_done = counted("exp_done", NPAIR * NT)
        probs_ready = counted("probs_ready", NPAIR)
        ctx_ready = counted("ctx_ready", 4)
        ctx_saved = counted("ctx_saved", 4)
        ctxq_ready = counted("ctxq_ready", NT)
        ctxn_done = counted("ctxn_done", NT)
        cT_ready = counted("cT_ready", KD)
        cTh_done = counted("cTh_done", KD)
        cTl_done = counted("cTl_done", KD)
        attn_ready = counted("attn_ready", 2)
        x2_done = counted("x2_done", 2)
        mv2_ready = counted("mv2_ready", 1)
        n2_ready = counted("n2_ready", 1)
        residual_ready = counted("residual_ready", 1)
        n2T_ready = counted("n2T_ready", KD)
        n2Th_done = counted("n2Th_done", KD)
        n2Tl_done = counted("n2Tl_done", KD)
        up_ready = counted("up_ready", NM)
        gelu_done = counted("gelu_done", NM)
        down_ready = counted("down_ready", 2)
        y_done = counted("y_done", 2)
        y_stored = counted("y_stored", 16)
        y_free = sem("y_free")
        inv_step = counted("inv_step", NT)
        bn2_step = counted("bn2_step", NT)
        bn1_step = counted("bn1_step", NT)
        maxhi_step = counted("maxhi_step", 4)
        LN1_STEPS, LN2_STEPS, X1_STEPS = 7, 3, 1
        ln1_step = counted("ln1_step", LN1_STEPS)
        ln2_step = counted("ln2_step", LN2_STEPS)
        x1_step = counted("x1_step", X1_STEPS)
        norm_scale = counted("norm_scale", 1)
        sign_done = sem("sign_done")

        def until(eng, s, b, k):
            eng.wait_ge(s, b * PER[id(s)] + k)

        passed = {"DVE": sem("passed_by_dve"), "Pool": sem("passed_by_pool")}

        def apart(eng, name):
            eng.sem_inc(passed[name], 1)

        p2_weights = sem("p2_weights")
        p2_gather_rows = sem("p2_gather_rows")
        p2_scatter_rows = sem("p2_scatter_rows")
        p2_raw = sem("p2_raw")
        p2_tr = sem("p2_tr")
        p2_hi = sem("p2_hi")
        p2_gather = [sem(f"p2_gather{i}") for i in range(2)]
        p2_stats = sem("p2_stats")
        p2_bn = sem("p2_bn")
        p2_mv = sem("p2_mv")
        p2_rstd = sem("p2_rstd")
        p2_pool = sem("p2_pool")
        p2_norm = sem("p2_norm")
        p2_nT = sem("p2_nT")
        p2_nTh = sem("p2_nTh")
        p2_nTl = sem("p2_nTl")
        p2_y = sem("p2_y")
        p2_out = sem("p2_out")
        p2_scatter = [sem(f"p2_scatter{i}") for i in range(2)]
        p2_bias = sem("p2_bias")

        HL = NE * KD * D
        we_raw = staged[:, 0:HL].rearrange("p (e o d) -> p e o d", e=NE, o=KD)
        pads = q_pad[:, :, :, :].rearrange("p a b c -> p (a b c)")
        we_h = pads[:, 0:HL].rearrange("p (e k o) -> p e k o", e=NE, k=KD)
        we_l = pads[:, HL:2 * HL].rearrange("p (e k o) -> p e k o", e=NE, k=KD)
        stacks = k_stack[:, :, :].rearrange("p a b -> p (a b)")
        bias_h = stacks[0:1, 0:NE * D].rearrange("p (e o) -> p e o", e=NE)
        bias_l = stacks[0:1, NE * D:2 * NE * D].rearrange("p (e o) -> p e o", e=NE)
        bias_raw = ctxT[0:1, :, :].rearrange("p a b -> p (a b)")
        one_row = sb("one_row", [1, P], F32R)
        rows_in = [x_in, x1]
        rows_out = [y, x2]
        p2_banks = [ffn_bank, score_bank[0:2]]
        p2_T = [(nT_h, nT_l), (cn_h, cn_l)]
        NHALF = NGROUP // HALF

        b_wide = route[:, 16:16 + KD * P].rearrange("p (k n) -> p k n", k=KD)
        at_small = 16 + KD * P
        r_score, r_cand, r_onehot = (route[:, at_small + i:at_small + i + NT * NE]
                                     .rearrange("p (c e) -> p c e", e=NE) for i in (0, 32, 64))
        r_small = route[:, at_small + 96:at_small + 108].rearrange("p (a c) -> p a c", c=NT)
        r_groups = route[:, at_small + 108:at_small + 116]
        r_start = route[:, at_small + 116:at_small + 124]
        r_gexp = route[:, at_small + 124:at_small + 124 + NCOL]
        r_tmp = route[:, at_small + 272:at_small + 272 + NCOL]
        r_int = sb("r_int", [P, 8], I32)
        r_row = staged[:, 5120:5120 + NT * P].rearrange("p (c n) -> p c n", c=NT)
        r_group = staged[:, 5632:5632 + NT * NCOL].rearrange("p (c n) -> p c n", c=NT)

        def col(v, n):
            return v.rearrange("(m p) -> p m", p=P)

        NLOAD = 19
        x_rows = x.rearrange("b (t p) d -> b p t d", p=P)
        y_rows = scratch.rearrange("(b t p) d -> b p t d", t=NT, p=P)

        block = ctx.enter_context(nc.Block())

        @block.sync
        def _(sp):
            sp.dma_start(cst, consts).then_inc(loaded, 16)
            sp.dma_start(wqkv_raw[:, :, 0:D], Wq.rearrange("(k p) n -> p k n", p=P)).then_inc(loaded, 16)
            sp.dma_start(wqkv_raw[:, :, D:2 * D], Wk.rearrange("(k p) n -> p k n", p=P)).then_inc(loaded, 16)
            sp.dma_start(wqkv_raw[:, :, 2 * D:], Wv.rearrange("(k p) n -> p k n", p=P)).then_inc(loaded, 16)
            sp.dma_start(wo_raw, Wo.rearrange("(k p) n -> p k n", p=P)).then_inc(loaded, 16)
            sp.dma_start(w1_raw, W1.rearrange("(k p) n -> p k n", p=P)).then_inc(loaded, 16)
            sp.dma_start(w2[:, :, :], W2.rearrange("(k p) n -> p k n", p=P)).then_inc(loaded, 16)
            sp.dma_start(qk_bias[:, 0:2], col(bq, 2), allow_slow_non_contiguous=True).then_inc(loaded, 16)
            sp.dma_start(qk_bias[:, 2:4], col(bk, 2), allow_slow_non_contiguous=True).then_inc(loaded, 16)
            sp.dma_start(b1_col[:, :], col(b1, NM), allow_slow_non_contiguous=True).then_inc(loaded, 16)
            for i, v in enumerate((ln1_w, ln1_b, ln2_w, ln2_b)):
                sp.dma_start(ln_col[:, i, :], col(v, KD), allow_slow_non_contiguous=True).then_inc(loaded, 16)
            for row, v in ((bv_row, bv), (bo_row, bo), (b2_row, b2)):
                sp.dma_start(row[:, :], v.partition_broadcast(P)).then_inc(loaded, 16)
            sp.dma_start(route[0:DPOS, 0:NE], sigs.rearrange("t p -> p t"), allow_slow_non_contiguous=True).then_inc(loaded, 16)
            sp.dma_start(x_in[:, :, :], x_rows[0]).then_inc(x_loaded, 16)
            sp.dma_start(ident[:, :], consts[:, at["ident"][0]:at["ident"][1]]).then_inc(loaded, 16)

            def attention(b, ahead):
                if ahead:
                    until(sp, x_used, b, 1)
                    sp.dma_start(x_in[:, :, :], x_rows[b + 1]).then_inc(x_loaded, 16)
                for half in range(2):
                    until(sp, maxT_done, b, half + 1)
                    for par in range(2):
                        for part in range(2):
                            row = 64 * par + MAX_ROW + part
                            src = 8 * par + 4 * part
                            sp.dma_start(
                                q_pad[row:row + 1, 4 * half:4 * half + 4, par, :].bitcast(F32),
                                maxT[src:src + 4, :],
                            ).then_inc(max_rows[half], 16)

            def finish(c):
                until(sp, y_done, c, 2)
                sp.dma_start(y_rows[c], y[:, :, :]).then_inc(y_stored, 16)
                until(sp, y_stored, c, 16)
                sp.sem_inc(y_free, 1)

            sp.sem_inc(y_free, LEAD)
            attention(0, True)
            with sp.Fori(1, NB - 1) as b:
                attention(b, True)
                finish(b - 1)
            attention(NB - 1, False)
            finish(NB - 2)
            finish(NB - 1)

            until(sp, y_done, NB - 1, 2)
            sp.dma_start(staged[:, 0:NE * KD * D].rearrange("p (e o d) -> p e o d", e=NE, o=KD),
                         We.rearrange("e (o p) d -> p e o d", p=P)).then_inc(p2_raw, 16)
            sp.dma_start(bias_raw, be.rearrange("(a e) o -> a (e o)", a=1)).then_inc(p2_raw, 16)

        @block.gpsimd
        def _(pool):
            nc.gpsimd.memset(v_ones[:, :, :], 0.0).then_inc(pool_step, 1)
            nc.gpsimd.memset(minus_half[:, :], -0.5).then_inc(pool_step, 1)
            nc.gpsimd.memset(one_row[:, :].bitcast(F32), 1.0).then_inc(pool_step, 1)
            nc.gpsimd.memset(q_pad[:, :, :, :].bitcast(F32), 0.0).then_inc(pool_step, 1)
            pool.wait_ge(pool_step, 1)
            nc.gpsimd.memset(v_ones[:, :, 0:NH * VW].rearrange("p t (h w) -> p t h w", w=VW)[:, :, :, 0:1],
                             1.0).then_inc(pool_step, 1)
            pool.wait_ge(pool_step, 5)
            nc.gpsimd.memset(lnt2[:, 3, :], 0.0).then_inc(ready, 1)
            pool.wait_ge(loaded, 16 * NLOAD)

            def rsqrt_step(done, dst, src, tmp, step, at_step):
                nc.gpsimd.tensor_scalar(tmp, src, EPS, 1.0, ALU.add, ALU.mult).then_inc(step, 1)
                done(at_step)
                nc.gpsimd.tensor_tensor(dst, tmp, minus_half[:, :], ALU.pow).then_inc(step, 1)
                done(at_step + 1)

            def norm1(b):
                until(pool, mv1_ready, b, 1)
                apart(pool, "Pool")
                if isinstance(b, int) and b == 0:
                    pass
                else:
                    until(pool, nT_ready, b - 1, KD)
                    apart(pool, "Pool")

                def done(k):
                    until(pool, ln1_step, b, k)
                    apart(pool, "Pool")

                neg_mean, r, t, r1 = lnt[:, 0, :], lnt[:, 1, :], lnt[:, 2, :], lnt[:, 3, :]
                var = mv1[:, :, 1]
                nc.gpsimd.tensor_scalar(neg_mean, mv1[:, :, 0], -1.0, 0.0, ALU.mult, ALU.add).then_inc(ln1_step, 1)
                rsqrt_step(done, r, var, lnt[:, 4, :], ln1_step, 2)
                nc.gpsimd.tensor_tensor(t, var, r, ALU.mult).then_inc(ln1_step, 1)
                done(4)
                nc.gpsimd.tensor_tensor(lnt[:, 5, :], t, r, ALU.mult).then_inc(ln1_step, 1)
                done(5)
                nc.gpsimd.tensor_scalar(lnt[:, 6, :], lnt[:, 5, :], EPS, 1.0, ALU.add, ALU.mult).then_inc(ln1_step, 1)
                done(6)
                nc.gpsimd.tensor_tensor(r1, lnt[:, 6, :], minus_half[:, :], ALU.pow).then_inc(ln1_step, 1)
                done(7)
                nc.gpsimd.tensor_tensor(lnt[:, 7, :], r, r1, ALU.mult).then_inc(norm_scale, 1)
                until(pool, norm_scale, b, 1)
                apart(pool, "Pool")
                for t_ in range(NT):
                    last = nc.gpsimd.tensor_scalar(normed[:, t_, :], x_in[:, t_, :], neg_mean[:, t_:t_ + 1],
                                                   lnt[:, 7, t_:t_ + 1], ALU.add, ALU.mult)
                last.then_inc(n1_ready, 1)

            def norm2(c):
                until(pool, mv2_ready, c, 1)
                apart(pool, "Pool")

                def done(k):
                    until(pool, ln2_step, c, k)
                    apart(pool, "Pool")

                neg_mean, r = lnt2[:, 0, :], lnt2[:, 1, :]
                nc.gpsimd.tensor_scalar(neg_mean, mv2[:, :, 0], -1.0, 0.0, ALU.mult, ALU.add).then_inc(ln2_step, 1)
                rsqrt_step(done, r, mv2[:, :, 1], lnt2[:, 2, :], ln2_step, 2)
                for t in range(NT):
                    last = nc.gpsimd.tensor_scalar(normed[:, t, :], x2[:, t, :], neg_mean[:, t:t + 1],
                                                   r[:, t:t + 1], ALU.add, ALU.mult)
                last.then_inc(n2_ready, 1)
                until(pool, n2_ready, c, 1)
                apart(pool, "Pool")
                nc.gpsimd.tensor_tensor(x2[:, :, :], x2[:, :, :], x_b2[:, :, :], ALU.add).then_inc(residual_ready, 1)

            def residuals(b):
                for t in range(NT):
                    last = nc.gpsimd.tensor_scalar(x1[:, t, :], x_in[:, t, :], lnt[:, 0, t:t + 1],
                                                   lnt[:, 1, t:t + 1], ALU.add, ALU.mult)
                last.then_inc(x1_step, 1)
                if not (isinstance(b, int) and b == 0):
                    until(pool, residual_ready, b - 1, 1)
                    apart(pool, "Pool")
                for t in range(NT):
                    last = nc.gpsimd.tensor_tensor(x_b2[:, t, :], x_in[:, t, :], b2_row[:, :], ALU.add)
                last.then_inc(x_used, 1)
                until(pool, x1_step, b, 1)
                apart(pool, "Pool")
                for t in range(NT):
                    last = nc.gpsimd.tensor_tensor(x1[:, t, :], x1[:, t, :], bo_row[:, :], ALU.add)
                last.then_inc(x1_ready, 1)

            def masks(b):
                for p in range(NPAIR):
                    until(pool, exp_done, b, NT * (p + 1))
                    apart(pool, "Pool")
                    blocks = probs[:, p % 4, 0:12 * P].rearrange("p (a h q) -> p a h q", h=2, q=P)
                    same, after = blocks[:, :, 0, :], blocks[:, :, 1, :]
                    last = probs[:, p % 4, 12 * P:14 * P].rearrange("p (a q) -> p a q", q=P)
                    for part, n, sign in ((same, 6, 1), (last, 2, 1), (after, 6, -1)):
                        done = nc.gpsimd.affine_select(
                            out=part, in_=part, compare_op=ALU.is_ge, fill=0.0,
                            base=0 if sign == 1 else WINDOW - P, pattern=[[0, n], [sign, P]],
                            channel_multiplier=-sign)
                    done.then_inc(probs_ready, 1)

            norm1(0)
            residuals(0)
            norm1(1)
            masks(0)
            with pool.Fori(1, NB - 1) as b:
                norm2(b - 1)
                residuals(b)
                norm1(b + 1)
                masks(b)
            norm2(NB - 2)
            residuals(NB - 1)
            masks(NB - 1)
            norm2(NB - 1)

            def rows_of(n, table, step):
                nc.gpsimd.tensor_copy(table[:, :], row_index[:, bass.ds(n * HALF, HALF)]).then_inc(step, 1)
                pool.wait_ge(step, n + 1)
                apart(pool, "Pool")

            def gather(n, half):
                rows_of(n, gather_rows[half], p2_gather_rows)
                for s in range(HALF):
                    nc.gpsimd.indirect_dma_start(
                        rows_in[half][:, s, :], None, scratch,
                        bass.IndirectOffsetOnAxis(ap=gather_rows[half][:, s:s + 1].bitcast(U32), axis=0),
                        bounds_check=NB * L - 1, oob_is_err=False).then_inc(p2_gather[half], 16)

            def scatter(n, half):
                pool.wait_ge(p2_out, 2 * n + 2)
                apart(pool, "Pool")
                rows_of(n, scatter_rows[half], p2_scatter_rows)
                for s in range(HALF):
                    nc.gpsimd.indirect_dma_start(
                        out, bass.IndirectOffsetOnAxis(ap=scatter_rows[half][:, s:s + 1].bitcast(U32), axis=0),
                        rows_out[half][:, s, :], None,
                        bounds_check=NB * L - 1, oob_is_err=False).then_inc(p2_scatter[half], 16)

            def norm3(n, half):
                pool.wait_ge(p2_mv, n + 1)
                apart(pool, "Pool")
                neg_mean, r, t = lnt2[:, 0, :], lnt2[:, 1, :], lnt2[:, 2, :]
                nc.gpsimd.tensor_scalar(neg_mean, mv2[:, :, 0], -1.0, 0.0, ALU.mult, ALU.add).then_inc(p2_pool, 1)
                nc.gpsimd.tensor_scalar(t, mv2[:, :, 1], EPS, 1.0, ALU.add, ALU.mult).then_inc(p2_pool, 1)
                pool.wait_ge(p2_pool, 3 * n + 2)
                apart(pool, "Pool")
                nc.gpsimd.tensor_tensor(r, t, minus_half[:, :], ALU.pow).then_inc(p2_pool, 1)
                pool.wait_ge(p2_pool, 3 * n + 3)
                apart(pool, "Pool")
                pool.wait_ge(p2_nT, LEAD + KD * n)
                apart(pool, "Pool")
                for s in range(HALF):
                    last = nc.gpsimd.tensor_scalar(normed[:, s, :], rows_in[half][:, s, :], neg_mean[:, s:s + 1],
                                                   r[:, s:s + 1], ALU.add, ALU.mult)
                last.then_inc(p2_norm, 1)

            until(pool, y_stored, NB - 1, 16)
            apart(pool, "Pool")
            pool.sem_inc(p2_norm, LEAD)
            gather(0, 0)
            with pool.Fori(0, NHALF, 2) as n:
                norm3(n, 0)
                gather(n + 1, 1)
                scatter(n, 0)
                norm3(n + 1, 1)
                gather(n + 2, 0)
                scatter(n + 1, 1)
            pool.wait_ge(p2_scatter[0], 16 * HALF * (NHALF // 2))
            pool.wait_ge(p2_scatter[1], 16 * HALF * (NHALF // 2))
            pool.wait_ge(p2_gather[0], 16 * HALF * (NHALF // 2 + 1))

        @block.scalar
        def _(act):
            act.wait_ge(loaded, 16 * NLOAD)
            nc.scalar.activation(route[0:DPOS, 8:16], route[0:DPOS, 0:NE], ACT.Sign).then_inc(sign_done, 1)
            act.wait_ge(ready, 2)

            def round_banks(c, ready_sem, dst, done_sem):
                for k in range(KD):
                    until(act, ready_sem, c, k + 1)
                    nc.scalar.activation(dst[:, k, :], mix_bank[k][:, :], ACT.Copy).then_inc(done_sem, 1)

            def qk_hi(b, g):
                for i in range(2):
                    until(act, qk_ready, b, 2 * g + i + 1)
                    nc.scalar.activation(qk_h[:, i, :], ffn_bank[i][:, :], ACT.Identity,
                                         bias=qk_bias[:, 2 * i + g:2 * i + g + 1]).then_inc(qkh_done, 1)

            def q_stacks(b, g):
                for p in range(4 * g, 4 * g + 4):
                    until(act, sel_ready, b, 2 * p + 1)
                    bank = select_bank[(2 * p) % 4]
                    nc.scalar.activation(q_pad[0:64, p, 0, :], bank[0:64, :], ACT.Copy)
                    nc.scalar.activation(q_pad[64:P, p, 1, :], bank[64:P, :], ACT.Copy).then_inc(qsel_done, 1)

            def gelu(c, m):
                until(act, up_ready, c, m + 1)
                nc.scalar.activation(hidden[:, m, :], ffn_bank[m % 2][:, :], ACT.Gelu_apprx_tanh,
                                     bias=b1_col[:, m:m + 1]).then_inc(gelu_done, 1)

            def max_out(b, half):
                until(act, maxT_ready, b, half + 1)
                if half == 1:
                    until(act, max_rows[0], b, 64)
                nc.scalar.activation(maxT[:, :], mix_bank[half][0:16, :], ACT.Copy).then_inc(maxT_done, 1)

            def exps(b, p):
                for kc in range(NT):
                    until(act, sT_ready, b, NT * p + kc + 1)
                    if kc == 0 and p >= 4 and p % 2 == 0:
                        until(act, ctx_ready, b, p // 2 - 1)
                    n = 4 * P if kc < NT - 1 else 2 * P
                    nc.scalar.activation(probs[:, p % 4, 4 * P * kc:4 * P * kc + n], score_bank[kc][:, 0:n],
                                         ACT.Exp, scale=SCALE).then_inc(exp_done, 1)

            def save_ctx(b, g):
                until(act, ctx_ready, b, g + 1)
                nc.scalar.activation(ctxT[:, g, :], mix_bank[g % 2][:, :], ACT.Copy).then_inc(ctx_saved, 1)

            def iteration(b, c):
                if b is not None:
                    round_banks(b, nT_ready, nT_h, nTh_done)
                    qk_hi(b, 0)
                if c is not None:
                    round_banks(c, cT_ready, cn_h, cTh_done)
                if b is not None:
                    q_stacks(b, 0)
                    qk_hi(b, 1)
                    q_stacks(b, 1)
                if c is not None:
                    round_banks(c, n2T_ready, cn_h, n2Th_done)
                for m in range(NM):
                    if c is not None:
                        gelu(c, m)
                    if b is not None and m == 2:
                        max_out(b, 0)
                if b is not None:
                    max_out(b, 1)
                    for p in range(NPAIR):
                        exps(b, p)
                        if p in (4, 6):
                            save_ctx(b, (p - 4) // 2)
                    save_ctx(b, 2)
                    save_ctx(b, 3)

            iteration(0, None)
            with act.Fori(1, NB - 1) as b:
                iteration(b, b - 1)
            iteration(NB - 1, NB - 2)
            iteration(None, NB - 1)

            for i in range(8):
                act.wait_ge(p2_tr, i + 1)
                dst = we_h.rearrange("p e k o -> p (e k o)")[:, 512 * i:512 * i + 512]
                nc.scalar.activation(dst, score_bank[i % 4][:, :], ACT.Copy).then_inc(p2_hi, 1)
            with act.Fori(0, NHALF, 2) as n0:
                for half in range(2):
                    n = n0 + half
                    for k in range(KD):
                        act.wait_ge(p2_nT, LEAD + n * KD + k + 1)
                        nc.scalar.activation(p2_T[half][0][:, k, :], mix_bank[k][:, :], ACT.Copy)\
                            .then_inc(p2_nTh, 1)

        @block.vector
        def _(dve):
            steps = [0]

            def link(ins):
                steps[0] += 1
                ins.then_inc(dve_step, 1)
                dve.wait_ge(dve_step, steps[0])

            dve.wait_ge(loaded, 16 * NLOAD)
            for k in range(KD):
                last = nc.vector.tensor_scalar(b_wide[:, k, :], const("ones"), ln_col[:, 1, k:k + 1], None, ALU.mult)
            last.then_inc(setup_dve, 1)
            for n in sel:
                nc.vector.tensor_copy(sel[n][:, :, :], const(n).rearrange("p (a b) -> p a b", b=P))
            nc.vector.tensor_copy(mask[:, :], const("mask"))
            nc.vector.tensor_copy(minus_one_rows[:, :], const("minus_one_rows"))
            for k in range(KD):
                nc.vector.tensor_scalar(wqkv_h[:, k, :], wqkv_raw[:, k, :], ln_col[:, 0, k:k + 1], None, ALU.mult)
                link(nc.vector.tensor_scalar(w1_h[:, k, :], w1_raw[:, k, :], ln_col[:, 2, k:k + 1], None, ALU.mult))
                nc.vector.scalar_tensor_tensor(wqkv_l[:, k, :], wqkv_raw[:, k, :], ln_col[:, 0, k:k + 1],
                                               wqkv_h[:, k, :].bitcast(F32), ALU.mult, ALU.subtract)
                link(nc.vector.scalar_tensor_tensor(w1_l[:, k, :], w1_raw[:, k, :], ln_col[:, 2, k:k + 1],
                                                    w1_h[:, k, :].bitcast(F32), ALU.mult, ALU.subtract))
            link(nc.vector.tensor_copy(wo_h[:, :, :], wo_raw))
            nc.vector.tensor_tensor(wo_l[:, :, :], wo_raw, wo_h[:, :, :].bitcast(F32), ALU.subtract)
            dve.wait_ge(setup_mm, 1)
            nc.vector.tensor_tensor(qk_bias[:, :], score_bank[0][:, 0:4], qk_bias[:, :], ALU.add)
            nc.vector.tensor_tensor(b1_col[:, :], score_bank[1][:, 0:NM], b1_col[:, :], ALU.add)
            nc.vector.tensor_tensor(bv_row[:, :], score_bank[2][:, 0:D], bv_row[:, :], ALU.add)

            def spread(a):
                return a.unsqueeze(2).broadcast_to([P, NT, NE])

            rank3 = const("expert_rank").rearrange("p (c e) -> p c e", e=NE)
            link(nc.vector.tensor_copy(r_score, score_bank[3][:, 0:NT * NE].rearrange("p (c e) -> p c e", e=NE)))
            link(nc.vector.tensor_reduce(r_small[:, 0, :], r_score, AX_X, ALU.max))
            link(nc.vector.tensor_tensor(r_cand, r_score, spread(r_small[:, 0, :]), ALU.is_equal))
            link(nc.vector.tensor_tensor(r_cand, r_cand, rank3, ALU.mult))
            link(nc.vector.tensor_reduce(r_small[:, 1, :], r_cand, AX_X, ALU.max))
            nc.vector.tensor_tensor(r_onehot, r_cand, spread(r_small[:, 1, :]), ALU.is_equal).then_inc(setup_dve, 1)
            dve.wait_ge(setup_mm, 2)
            nc.vector.tensor_copy(r_score, score_bank[0][:, 0:NT * NE].rearrange("p (c e) -> p c e", e=NE))
            link(nc.vector.tensor_scalar(r_int[:, 0:NE], score_bank[1][:, 0:NE], float(SLOTS - 1), None, ALU.add))
            link(nc.vector.tensor_scalar(r_int[:, 0:NE], r_int[:, 0:NE], SLOTS.bit_length() - 1, None,
                                         ALU.arith_shift_right))
            nc.vector.tensor_copy(r_groups, r_int[:, 0:NE])
            link(nc.vector.memset(r_start, 0.0))
            for e in range(NE - 1):
                link(nc.vector.tensor_tensor(r_start[:, e + 1:e + 2], r_start[:, e:e + 1], r_groups[:, e:e + 1],
                                             ALU.add))
            link(nc.vector.memset(r_gexp, 0.0))
            for e in range(1, NE):
                link(nc.vector.scalar_tensor_tensor(r_gexp, const("group_iota"), r_start[:, e:e + 1], r_gexp,
                                                    ALU.is_ge, ALU.add))
            nc.vector.tensor_copy(group_expert[:, :], r_gexp)
            link(nc.vector.tensor_scalar(r_start, r_start, float(SLOTS), None, ALU.mult))
            link(nc.vector.tensor_tensor(r_score, r_score, r_start.unsqueeze(1).broadcast_to([P, NT, NE]), ALU.add))
            link(nc.vector.tensor_tensor(r_score, r_score, r_onehot, ALU.mult))
            link(nc.vector.tensor_reduce(r_small[:, 0, :], r_score, AX_X, ALU.add))
            link(nc.vector.tensor_copy(r_int[:, 0:NT], r_small[:, 0, :]))
            link(nc.vector.tensor_scalar(r_int[:, NT:2 * NT], r_int[:, 0:NT], SLOTS.bit_length() - 1, None,
                                         ALU.arith_shift_right))
            link(nc.vector.tensor_copy(r_small[:, 1, :], r_int[:, NT:2 * NT]))
            link(nc.vector.scalar_tensor_tensor(r_small[:, 2, :], r_small[:, 1, :], -float(SLOTS), r_small[:, 0, :],
                                                ALU.mult, ALU.add))
            for c in range(NT):
                nc.vector.tensor_scalar(r_row[:, c, :], const("slot_of_row"), r_small[:, 2, c:c + 1], None,
                                        ALU.is_equal)
                last = nc.vector.tensor_scalar(r_group[:, c, :], const("group_iota"), r_small[:, 1, c:c + 1],
                                               const("position_plus_1")[:, c:c + 1], ALU.is_equal, ALU.mult)
            last.then_inc(setup_dve, 1)
            dve.wait_ge(setup_mm, 3)
            nc.vector.tensor_scalar(r_gexp, score_bank[2][:, 0:NCOL], 0.0, EMPTY, ALU.is_equal, ALU.mult)
            link(nc.vector.tensor_scalar(r_tmp, score_bank[2][:, 0:NCOL], const("first_row"), -1.0, ALU.add, ALU.add))
            link(nc.vector.tensor_tensor(row_index[:, :], r_gexp, r_tmp, ALU.add))
            nc.vector.memset(max_parts[:, :, :, :, :, :], 0.0).then_inc(ready, 1)
            dve.wait_ge(ready, 2)

            def stats(b):
                until(dve, x_loaded, b, 16)
                for t in range(NT):
                    nc.vector.bn_stats(stats1[:, t, :], x_in[:, t, :]).then_inc(bn1_step, 1)
                if not (isinstance(b, int) and b == 0):
                    until(dve, n1_ready, b - 1, 1)
                for t in range(NT):
                    until(dve, bn1_step, b, t + 1)
                    apart(dve, "DVE")
                    last = nc.vector.bn_aggr(mv1[:, t, :], stats1[:, t, :])
                last.then_inc(mv1_ready, 1)

            def rest_of_banks(c, hi, hi_done, lo, lo_done):
                for k in range(KD):
                    until(dve, hi_done, c, k + 1)
                    nc.vector.tensor_tensor(lo[:, k, :], mix_bank[k][:, :], hi[:, k, :].bitcast(F32), ALU.subtract)\
                        .then_inc(lo_done, 1)

            def normalise(c):
                dve.wait_ge(y_free, LEAD + c)
                for t in range(NT):
                    until(dve, ctxq_ready, c, t + 1)
                    heads = score_bank[t][:, :].rearrange("p (h w) -> p h w", w=32)
                    nc.vector.reciprocal(inv_sum[:, t, :].unsqueeze(2), heads[:, :, 0:1]).then_inc(inv_step, 1)
                for t in range(NT):
                    heads = score_bank[t][:, :].rearrange("p (h w) -> p h w", w=32)
                    until(dve, inv_step, c, t + 1)
                    nc.vector.tensor_tensor(ctxn[:, t, :].rearrange("p (h d) -> p h d", d=HD), heads[:, :, 1:VW],
                                            inv_sum[:, t, :].unsqueeze(2).broadcast_to([P, NH, HD]), ALU.mult)\
                        .then_inc(ctxn_done, 1)

            def qk_lo(b, g):
                for i in range(2):
                    until(dve, qkh_done, b, 2 * g + i + 1)
                    nc.vector.scalar_tensor_tensor(qk_l[:, i, :], ffn_bank[i][:, :],
                                                   qk_bias[:, 2 * i + g:2 * i + g + 1],
                                                   qk_h[:, i, :].bitcast(F32), ALU.add, ALU.subtract)\
                        .then_inc(qkl_done, 1)

            def values(b):
                for u in range(2):
                    until(dve, v_ready, b, u + 1)
                    for s in range(2):
                        t = 2 * u + s
                        dst = v_ones[:, t, 0:NH * VW].rearrange("p (h w) -> p h w", w=VW)[:, :, 1:VW]
                        last = nc.vector.tensor_tensor(
                            dst, ffn_bank[u][:, D * s:D * s + D].rearrange("p (h d) -> p h d", d=HD),
                            bv_row[:, :].rearrange("p (h d) -> p h d", d=HD), ALU.add)
                    last.then_inc(v_done, 1)

            def after_attention(c):
                for u in range(2):
                    until(dve, x1_ready, c, 1)
                    until(dve, attn_ready, c, u + 1)
                    nc.vector.tensor_tensor(x2[:, 2 * u:2 * u + 2, :].rearrange("p t d -> p (t d)"),
                                            score_bank[2 + u][:, :],
                                            x1[:, 2 * u:2 * u + 2, :].rearrange("p t d -> p (t d)"), ALU.add)\
                        .then_inc(x2_done, 1)
                for t in range(NT):
                    until(dve, x2_done, c, t // 2 + 1)
                    nc.vector.bn_stats(stats2[:, t, :], x2[:, t, :]).then_inc(bn2_step, 1)
                for t in range(NT):
                    until(dve, bn2_step, c, t + 1)
                    apart(dve, "DVE")
                    last = nc.vector.bn_aggr(mv2[:, t, :], stats2[:, t, :])
                last.then_inc(mv2_ready, 1)

            def k_stacks(b, g):
                for p in range(4 * g, 4 * g + 4):
                    until(dve, sel_ready, b, 2 * p + 2)
                    nc.vector.tensor_scalar(k_stack[:, p, :], select_bank[(2 * p + 1) % 4][:, :],
                                            minus_one_rows[:, 0:1], None, ALU.add).then_inc(ksel_done, 1)

            def head_max(b, h):
                until(dve, s_ready, b, h + 1)
                apart(dve, "DVE")
                for t in range(NT):
                    bank = score_bank[2 * (h % 2) + t // 2]
                    c0 = 2 * P * (t % 2)
                    lo = P if t == 0 else 0
                    block_ = bank[:, c0 + lo:c0 + 2 * P]
                    last = nc.vector.tensor_tensor_reduce(
                        out=block_, in0=block_, in1=mask[:, lo:2 * P],
                        scale=1.0, scalar=LOWEST, op0=ALU.add, op1=ALU.max, accum_out=row_max[:, t, h:h + 1])
                last.then_inc(max_done, 1)

            def max_split(b, half):
                until(dve, max_done, b, 8 * half + 8)
                src = row_max[:, :, 8 * half:8 * half + 8].rearrange("p t (j a) -> p t a j", a=2)
                for par in range(2):
                    nc.vector.tensor_copy(max_hi[:, :, half, par, :], src[:, :, par, :]).then_inc(maxhi_step, 1)
                for par in range(2):
                    until(dve, maxhi_step, b, 2 * half + par + 1)
                    hi = max_hi[:, :, half, par, :].bitcast(F32)
                    nc.vector.tensor_copy(max_parts[:, :, half, par, 0, :], hi)
                    last = nc.vector.tensor_tensor(max_parts[:, :, half, par, 1, :], src[:, :, par, :], hi,
                                                   ALU.subtract)
                last.then_inc(parts_done, 1)

            def outputs(c):
                for u in range(2):
                    until(dve, residual_ready, c, 1)
                    until(dve, down_ready, c, u + 1)
                    nc.vector.tensor_tensor(y[:, 2 * u:2 * u + 2, :].rearrange("p t d -> p (t d)"),
                                            ffn_bank[u][:, :],
                                            x2[:, 2 * u:2 * u + 2, :].rearrange("p t d -> p (t d)"), ALU.add)\
                        .then_inc(y_done, 1)

            def iteration(b, c, ahead):
                if b is not None:
                    rest_of_banks(b, nT_h, nTh_done, nT_l, nTl_done)
                if c is not None:
                    normalise(c)
                if b is not None:
                    qk_lo(b, 0)
                if c is not None:
                    rest_of_banks(c, cn_h, cTh_done, cn_l, cTl_done)
                if b is not None:
                    values(b)
                    k_stacks(b, 0)
                if c is not None:
                    after_attention(c)
                if b is not None:
                    qk_lo(b, 1)
                    k_stacks(b, 1)
                    head_max(b, 0)
                    head_max(b, 1)
                if c is not None:
                    rest_of_banks(c, cn_h, n2Th_done, cn_l, n2Tl_done)
                if b is not None:
                    for h in range(2, NH):
                        head_max(b, h)
                        if h == 7:
                            max_split(b, 0)
                        if h == 11 and ahead:
                            stats(b + 1)
                    max_split(b, 1)
                if c is not None:
                    outputs(c)

            stats(0)
            iteration(0, None, True)
            with dve.Fori(1, NB - 1) as b:
                iteration(b, b - 1, True)
            iteration(NB - 1, NB - 2, False)
            iteration(None, NB - 1, False)

            dve.sem_inc(p2_nTl, LEAD)
            dve.wait_ge(p2_raw, 32)
            nc.vector.tensor_copy(bias_h.rearrange("p e o -> p (e o)"), bias_raw).then_inc(p2_bias, 1)
            dve.wait_ge(p2_bias, 1)
            nc.vector.tensor_tensor(bias_l.rearrange("p e o -> p (e o)"), bias_raw,
                                    bias_h.rearrange("p e o -> p (e o)").bitcast(F32), ALU.subtract)
            for i in range(NE):
                dve.wait_ge(p2_hi, i + 1)
                part = slice(KD * D * i, KD * D * i + KD * D)
                nc.vector.tensor_tensor(we_l.rearrange("p e k o -> p (e k o)")[:, part], score_bank[i % 4][:, :],
                                        we_h.rearrange("p e k o -> p (e k o)")[:, part].bitcast(F32),
                                        ALU.subtract).then_inc(p2_weights, 1)

            def row_stats(n, half, n0):
                dve.wait_ge(p2_gather[half], (16 * HALF // 2) * n0 + 16 * HALF)
                for s in range(HALF):
                    nc.vector.bn_stats(stats2[:, s, :], rows_in[half][:, s, :]).then_inc(p2_bn, 1)
                dve.wait_ge(p2_norm, LEAD + n)
                for s in range(HALF):
                    dve.wait_ge(p2_bn, HALF * n + s + 1)
                    apart(dve, "DVE")
                    last = nc.vector.bn_aggr(mv2[:, s, :], stats2[:, s, :])
                last.then_inc(p2_mv, 1)

            def two_halves(n0):
                for half in range(2):
                    n = n0 + half
                    row_stats(n, half, n0)
                    for k in range(KD):
                        dve.wait_ge(p2_nTh, KD * n + k + 1)
                        nc.vector.tensor_tensor(p2_T[half][1][:, k, :], mix_bank[k][:, :],
                                                p2_T[half][0][:, k, :].bitcast(F32), ALU.subtract)\
                            .then_inc(p2_nTl, 1)
                    if not isinstance(n0, int):
                        dve.wait_ge(p2_scatter[half], (16 * HALF // 2) * n0)
                    for u in range(2):
                        dve.wait_ge(p2_y, 2 * n + u + 1)
                        nc.vector.tensor_tensor(
                            rows_out[half][:, 2 * u:2 * u + 2, :].rearrange("p t d -> p (t d)"),
                            p2_banks[half][u][:, :],
                            rows_in[half][:, 2 * u:2 * u + 2, :].rearrange("p t d -> p (t d)"), ALU.add)\
                            .then_inc(p2_out, 1)

            two_halves(0)
            with dve.Fori(2, NHALF, 2) as n0:
                two_halves(n0)

        @block.tensor
        def _(pe):
            mm = nc.tensor.matmul

            pe.wait_ge(loaded, 16 * NLOAD)
            for m in range(4):
                for k in range(KD):
                    mm(score_bank[0][:, m:m + 1], wqkv_raw[:, k, P * m:P * m + P], ln_col[:, 1, k:k + 1],
                       start=k == 0, stop=k == KD - 1)
            for m in range(NM):
                for k in range(KD):
                    mm(score_bank[1][:, m:m + 1], w1_raw[:, k, P * m:P * m + P], ln_col[:, 3, k:k + 1],
                       start=k == 0, stop=k == KD - 1)
            pe.wait_ge(sign_done, 1)
            for c in range(NT):
                mm(score_bank[3][:, NE * c:NE * c + NE], const("position_code")[0:DPOS, P * c:P * c + P],
                   route[0:DPOS, NE:2 * NE], start=True, stop=True)
            pe.wait_ge(setup_dve, 1)
            for k in range(KD):
                last = mm(score_bank[2][:, 0:D], b_wide[:, k, :], wqkv_raw[:, k, 2 * D:3 * D],
                          start=k == 0, stop=k == KD - 1)
            last.then_inc(setup_mm, 1)
            pe.wait_ge(setup_dve, 2)
            for c in range(NT):
                for c2 in range(c + 1):
                    mm(score_bank[0][:, NE * c:NE * c + NE], const("before") if c2 == c else const("ones"),
                       r_onehot[:, c2, :], start=c2 == 0, stop=c2 == c)
            for c in range(NT):
                last = mm(score_bank[1][:, 0:NE], const("ones"), r_onehot[:, c, :], start=c == 0, stop=c == NT - 1)
            last.then_inc(setup_mm, 1)
            pe.wait_ge(setup_dve, 3)
            for c in range(NT):
                last = mm(score_bank[2][:, 0:NCOL], r_row[:, c, :], r_group[:, c, :], start=c == 0, stop=c == NT - 1)
            last.then_inc(setup_mm, 1)
            pe.wait_ge(ready, 2)

            def split_product(out, pairs):
                terms = [(a[0], a[2]) for a in pairs] + [(a[1], a[2]) for a in pairs] + [(a[0], a[3]) for a in pairs]
                for i, (lhsT, rhs) in enumerate(terms):
                    last = mm(out, lhsT, rhs, start=i == 0, stop=i == len(terms) - 1)
                return last

            def transpose_rows(src, ready_sem):
                for k in range(KD):
                    for t in range(NT):
                        last = nc.tensor.transpose(mix_bank[k][:, P * t:P * t + P], src[:, t, P * k:P * k + P],
                                                   ident[:, :])
                    last.then_inc(ready_sem, 1)

            def input_transposes(b):
                if not (isinstance(b, int) and b == 0):
                    until(pe, ctx_saved, b - 1, 4)
                until(pe, n1_ready, b, 1)
                transpose_rows(normed, nT_ready)

            def context_to_rows(c):
                until(pe, ctx_saved, c, 4)
                for t in range(NT):
                    for g in range(4):
                        last = nc.tensor.transpose(score_bank[t][:, P * g:P * g + P], ctxT[:, g, P * t:P * t + P],
                                                   ident[:, :])
                    last.then_inc(ctxq_ready, 1)

            def project_qk(b, g):
                if g == 0:
                    until(pe, nTh_done, b, KD)
                    until(pe, nTl_done, b, KD)
                for i in range(2):
                    if g == 1:
                        until(pe, (qsel_done, ksel_done)[i], b, 3)
                    w = slice(D * i + P * g, D * i + P * g + P)
                    split_product(ffn_bank[i][:, :], [
                        (wqkv_h[:, k, w], wqkv_l[:, k, w], nT_h[:, k, :], nT_l[:, k, :]) for k in range(KD)
                    ]).then_inc(qk_ready, 1)

            def context_transposes(c):
                for t in range(NT):
                    until(pe, ctxn_done, c, t + 1)
                    for k in range(KD):
                        last = nc.tensor.transpose(mix_bank[k][:, P * t:P * t + P], ctxn[:, t, P * k:P * k + P],
                                                   ident[:, :])
                        if t == NT - 1:
                            last.then_inc(cT_ready, 1)

            def project_v(b):
                for u in range(2):
                    until(pe, qkl_done, b, u + 1)
                    for s in range(2):
                        c = slice(P * (2 * u + s), P * (2 * u + s) + P)
                        last = split_product(ffn_bank[u][:, D * s:D * s + D], [
                            (nT_h[:, k, c], nT_l[:, k, c], wqkv_h[:, k, 2 * D:], wqkv_l[:, k, 2 * D:])
                            for k in range(KD)])
                    last.then_inc(v_ready, 1)

            def project_out(c):
                until(pe, cTl_done, c, KD)
                for u in range(2):
                    for s in range(2):
                        cols = slice(P * (2 * u + s), P * (2 * u + s) + P)
                        last = split_product(score_bank[2 + u][:, D * s:D * s + D], [
                            (cn_h[:, k, cols], cn_l[:, k, cols], wo_h[:, k, :], wo_l[:, k, :])
                            for k in range(KD)])
                    last.then_inc(attn_ready, 1)

            def stacks(b, g):
                until(pe, qkl_done, b, 2 * g + 2)
                for p in range(4 * g, 4 * g + 4):
                    for i in range(2):
                        n = 2 * p + i
                        if n < 2:
                            until(pe, v_done, b, n + 1)
                        elif n >= 4 and not (g == 1 and p == 4):
                            until(pe, (qsel_done, ksel_done)[i], b, p - 1)
                        h, l = (("sel_qh", "sel_ql"), ("sel_kh", "sel_kl"))[i]
                        mm(select_bank[n % 4][:, :], sel[h][:, p % 4, :], qk_h[:, i, :], start=True, stop=False)
                        mm(select_bank[n % 4][:, :], sel[l][:, p % 4, :], qk_l[:, i, :], start=False, stop=True)\
                            .then_inc(sel_ready, 1)

            def scores(b, h, c):
                if h == 0:
                    until(pe, qsel_done, b, NPAIR)
                    until(pe, ksel_done, b, NPAIR)
                elif h == 1:
                    if c is not None:
                        until(pe, x2_done, c, 2)
                else:
                    until(pe, max_done, b, h - 1)
                p = h // 2
                for t in range(NT):
                    bank = score_bank[2 * (h % 2) + t // 2]
                    c0 = 2 * P * (t % 2)
                    lo = P if t == 0 else 0
                    last = mm(bank[:, c0 + lo:c0 + 2 * P], q_pad[:, p, h % 2, P * t:P * t + P],
                              k_stack[:, p, P * (t - 1) + lo:P * (t + 1)], start=True, stop=True)
                last.then_inc(s_ready, 1)

            def n2_transposes(c):
                until(pe, n2_ready, c, 1)
                transpose_rows(normed, n2T_ready)

            def up(c, m):
                if m == 0:
                    until(pe, n2Tl_done, c, KD)
                elif m >= 2:
                    until(pe, gelu_done, c, m - 1)
                w = slice(P * m, P * m + P)
                split_product(ffn_bank[m % 2][:, :], [
                    (w1_h[:, k, w], w1_l[:, k, w], cn_h[:, k, :], cn_l[:, k, :]) for k in range(KD)
                ]).then_inc(up_ready, 1)

            def max_transposes(b, half):
                until(pe, parts_done, b, half + 1)
                for t in range(NT):
                    last = nc.tensor.transpose(
                        mix_bank[half][0:16, P * t:P * t + P],
                        max_parts[:, t, half, :, :, :].rearrange("p a b c -> p (a b c)"), ident[:, :])
                last.then_inc(maxT_ready, 1)

            def down(c, t):
                if t == 0:
                    until(pe, gelu_done, c, NM)
                for m in range(NM):
                    last = mm(ffn_bank[t // 2][:, D * (t % 2):D * (t % 2) + D], hidden[:, m, P * t:P * t + P],
                              w2[:, m, :], start=m == 0, stop=m == NM - 1)
                if t % 2:
                    last.then_inc(down_ready, 1)

            def scores_T(b, p):
                if p % 4 == 0:
                    until(pe, max_rows[p // 4], b, 64)
                for kc in range(NT):
                    if p == 0:
                        until(pe, max_done, b, NH - 1 + kc // 2)
                    else:
                        until(pe, exp_done, b, NT * (p - 1) + kc + 1)
                    q1 = min(P * (kc + 2), L)
                    n = q1 - P * kc
                    mm(score_bank[kc][:, 0:2 * n].rearrange("p (h q) -> p h q", h=2),
                       k_stack[:, p, P * kc:P * kc + P], q_pad[:, p, :, P * kc:q1],
                       start=True, stop=True).then_inc(sT_ready, 1)

            def context(b, g):
                until(pe, probs_ready, b, 2 * g + 2)
                if g < 2:
                    until(pe, maxT_done, b, g + 1)
                else:
                    until(pe, ctx_saved, b, g - 1)
                for kc in range(NT):
                    n = 2 * P if kc < NT - 1 else P
                    for j in range(4):
                        slot = 2 * (g % 2) + j // 2
                        r0 = 4 * P * kc + n * (j % 2)
                        last = mm(mix_bank[g % 2][32 * j:32 * j + 32, P * kc:P * kc + n],
                                  v_ones[:, kc, VW * (4 * g + j):VW * (4 * g + j) + 32],
                                  probs[:, slot, r0:r0 + n], start=kc == 0, stop=kc == NT - 1,
                                  skip_group_check=True)
                last.then_inc(ctx_ready, 1)

            def iteration(b, c):
                if b is not None:
                    input_transposes(b)
                if c is not None:
                    context_to_rows(c)
                if b is not None:
                    project_qk(b, 0)
                if c is not None:
                    context_transposes(c)
                if b is not None:
                    project_v(b)
                    stacks(b, 0)
                if c is not None:
                    project_out(c)
                if b is not None:
                    project_qk(b, 1)
                    stacks(b, 1)
                    scores(b, 0, c)
                    scores(b, 1, c)
                if c is not None:
                    n2_transposes(c)
                for m in range(NM):
                    if b is not None and m < NM - 1:
                        scores(b, 2 * m + 2, c)
                        scores(b, 2 * m + 3, c)
                    if b is not None and m == 3:
                        max_transposes(b, 0)
                    if c is not None:
                        up(c, m)
                if c is not None:
                    down(c, 0)
                if b is not None:
                    max_transposes(b, 1)
                    for p in range(NPAIR):
                        scores_T(b, p)
                        if c is not None and p in (0, 2, 4):
                            down(c, p // 2 + 1)
                        if p >= 3 and p % 2:
                            context(b, (p - 3) // 2)
                    context(b, 3)
                elif c is not None:
                    for t in range(1, NT):
                        down(c, t)

            iteration(0, None)
            with pe.Fori(1, NB - 1) as b:
                iteration(b, b - 1)
            iteration(NB - 1, NB - 2)
            iteration(None, NB - 1)

            pe.sem_inc(p2_nT, LEAD)
            pe.wait_ge(p2_raw, 32)
            for e in range(NE):
                if e >= 4:
                    pe.wait_ge(p2_weights, e - 3)
                for k in range(KD):
                    for o in range(KD):
                        last = nc.tensor.transpose(score_bank[e % 4][:, D * k + P * o:D * k + P * o + P],
                                                   we_raw[:, e, o, P * k:P * k + P], ident[:, :])
                last.then_inc(p2_tr, 1)
            pe.wait_ge(p2_weights, NE)

            def row_transposes(n):
                pe.wait_ge(p2_nTl, LEAD + KD * n)
                pe.wait_ge(p2_norm, LEAD + n + 1)
                transpose_rows(normed, p2_nT)

            def expert_products(n, half):
                pe.wait_ge(p2_nTl, LEAD + KD * n + KD)
                hi, lo = p2_T[half]
                for s in range(HALF):
                    e = pe.value_load(group_expert[0:1, bass.ds(n * HALF + s, 1)], min_val=0, max_val=NE - 1)
                    dst = p2_banks[half][s // 2][:, D * (s % 2):D * (s % 2) + D]
                    c = slice(P * s, P * s + P)
                    terms = [(a[:, k, c], w[:, bass.ds(e, 1), k, :]) for a, w in ((hi, we_h), (lo, we_h), (hi, we_l))
                             for k in range(KD)]
                    terms += [(one_row[:, :], w[:, bass.ds(e, 1), :]) for w in (bias_h, bias_l)]
                    for i, (lhsT, rhs) in enumerate(terms):
                        last = mm(dst, lhsT, rhs, start=i == 0, stop=i == len(terms) - 1)
                    if s % 2:
                        last.then_inc(p2_y, 1)

            with pe.Fori(0, NHALF, 2) as n:
                row_transposes(n)
                expert_products(n, 0)
                row_transposes(n + 1)
                expert_products(n + 1, 1)


_INS = ["L0_attn_x", "L0_attn_Wq", "L0_attn_bq", "L0_attn_Wk", "L0_attn_bk", "L0_attn_Wv", "L0_attn_bv",
        "L0_attn_Wo", "L0_attn_bo", "L0_attn_W1", "L0_attn_b1", "L0_attn_W2", "L0_attn_b2",
        "L0_attn_ln1_w", "L0_attn_ln1_b", "L0_attn_ln2_w", "L0_attn_ln2_b",
        "L0_ffn_tile_sigs", "L0_ffn_W", "L0_ffn_b"]


def kernel(**inputs):
    import concourse.bacc as bacc
    from concourse.bass_utils import run_bass_kernel_spmd

    nc = bacc.Bacc("TRN2", target_bir_lowering=False, num_devices=1, dynamic_dma_scratch_size=8192)
    arrays, args = {}, []
    for name in _INS:
        a = np.ascontiguousarray(inputs[name])
        arrays[f"in_{name}"] = a
        args.append(nc.dram_tensor(f"in_{name}", a.shape, mybir.dt.from_np(a.dtype), kind="ExternalInput").ap())
    consts, at = shape_constants()
    arrays["shape_constants"] = consts
    cst = nc.dram_tensor("shape_constants", consts.shape, F32, kind="ExternalInput").ap()
    scratch = nc.dram_tensor("attended", (NB * L, D), F32, kind="Internal").ap()
    out = nc.dram_tensor("out_rows", (NB * L, D), F32, kind="ExternalOutput").ap()
    build(nc, *args, cst, at, scratch, out)
    r = run_bass_kernel_spmd(nc, [arrays], core_ids=[0])
    return r.results[0]["out_rows"].reshape(NB, L, D)
```

```python
from contextlib import ExitStack
import math

import numpy as np

import concourse.bass as bass
from concourse import mybir

F32 = mybir.dt.float32
F32R = mybir.dt.float32r
I32 = mybir.dt.int32
U32 = mybir.dt.uint32
ALU = mybir.AluOpType
ACT = mybir.ActivationFunctionType
AX_X = mybir.AxisListType.X

P = 128
NB, L, D = 32, 512, 256
NT = L // P
KD = D // P
NH, HD = 16, 16
NPAIR = NH // 2
DFF = 1024
NM = DFF // P
NE, DPOS = 8, 32
WINDOW = 128
EPS = 1e-5
SCALE = 1.0 / math.sqrt(HD)
MASKED = -3.0e38
LOWEST = float(np.finfo(np.float32).min)
VW = HD + 1

SLOTS = 16
QUADS = P // SLOTS
RUN = NB // QUADS
assert RUN == NT
DEPTH = 4
AHEAD = DEPTH - 1
NUNIT = -(-((L + NE * (SLOTS - 1)) // SLOTS) // DEPTH) * DEPTH
NCOL = NUNIT + 2 * DEPTH
EMPTY = float(1 << 20)

Q_STACK = ("hi", "lo", "hi")
K_STACK = ("hi", "hi", "lo")
MAX_ROW = 3 * HD


def shape_constants():
    r = np.arange(P)
    parts = {}
    parts["ident"] = np.eye(P)
    q, k = r[:, None], r[None, :]
    parts["mask"] = np.concatenate([np.where(k >= q, 0.0, MASKED), np.where(k <= q, 0.0, MASKED)], 1)
    for name, stack, part in (("sel_qh", Q_STACK, "hi"), ("sel_ql", Q_STACK, "lo"),
                              ("sel_kh", K_STACK, "hi"), ("sel_kl", K_STACK, "lo")):
        m = np.zeros((P, NPAIR // KD, P))
        for p in range(NPAIR // KD):
            for par in range(2):
                for c in range(3):
                    if stack[c] == part:
                        for d in range(HD):
                            m[2 * HD * p + HD * par + d, p, 64 * par + HD * c + d] = 1.0
        parts[name] = m.reshape(P, -1)
    kcol = np.zeros((P, 1))
    for par in range(2):
        kcol[64 * par + MAX_ROW:64 * par + MAX_ROW + 2] = -1.0
    parts["minus_one_rows"] = kcol
    parts["before"] = (q < k).astype(np.float32)
    parts["ones"] = np.ones((P, P))
    parts["unit_iota"] = np.broadcast_to(np.arange(NCOL), (P, NCOL))
    parts["slot_of_row"] = np.broadcast_to(r // QUADS, (P, P))
    parts["first_run"] = (r % QUADS - QUADS)[:, None]
    parts["first_row"] = (L * RUN * (r % QUADS))[:, None] + L * np.arange(RUN)[None, :] - 1
    parts["position_plus_1"] = r[:, None] + P * np.arange(NT)[None, :] + 1
    parts["expert_rank"] = np.broadcast_to(NE - np.arange(NE), (P, NT, NE)).reshape(P, -1)
    pos = np.arange(L, dtype=np.float32)[:, None]
    div = np.exp((np.arange(0, DPOS, 2, dtype=np.float32) *
                  np.float32(-math.log(10000.0) / DPOS)).astype(np.float64)).astype(np.float32)
    ang = pos * div
    code = np.zeros((L, DPOS), np.float32)
    code[:, 0::2], code[:, 1::2] = np.sin(ang), np.cos(ang)
    codeT = np.zeros((P, L))
    codeT[:DPOS] = code.T
    parts["position_code"] = codeT
    at, cols = {}, 0
    for name, a in parts.items():
        at[name] = (cols, cols + a.shape[1])
        cols += a.shape[1]
    return np.ascontiguousarray(np.concatenate(list(parts.values()), 1).astype(np.float32)), at


def build(nc, x, Wq, bq, Wk, bk, Wv, bv, Wo, bo, W1, b1, W2, b2, ln1_w, ln1_b, ln2_w, ln2_b,
          sigs, We, be, consts, at, scratch, out):
    ctx = ExitStack()
    with ctx:
        def sb(name, shape, dt=F32):
            return ctx.enter_context(nc.sbuf_tensor(name, shape, dt))

        def sem(name):
            return ctx.enter_context(nc.semaphore(name))

        score_bank = [ctx.enter_context(nc.psum_tensor(f"score_bank{i}", [P, 512], F32)) for i in range(4)]
        ffn_bank = [ctx.enter_context(nc.psum_tensor(f"ffn_bank{i}", [P, 512], F32)) for i in range(2)]
        mix_bank = [ctx.enter_context(nc.psum_tensor(f"mix_bank{i}", [P, 512], F32)) for i in range(2)]
        select_bank = [ffn_bank[0], ffn_bank[1], score_bank[0], score_bank[1]]

        ident = sb("ident", [P, P])
        mask = sb("mask", [P, 2 * P])
        sel = {n: sb(n, [P, NPAIR // KD, P], F32R) for n in ("sel_qh", "sel_ql", "sel_kh", "sel_kl")}
        minus_one_rows = sb("minus_one_rows", [P, 1])
        wqkv_h = sb("wqkv_h", [P, KD, 3 * D], F32R)
        wqkv_l = sb("wqkv_l", [P, KD, 3 * D], F32R)
        wo_h = sb("wo_h", [P, KD, D], F32R)
        wo_l = sb("wo_l", [P, KD, D], F32R)
        w1_h = sb("w1_h", [P, KD, DFF], F32R)
        w1_l = sb("w1_l", [P, KD, DFF], F32R)
        w2 = sb("w2", [P, NM, D])
        qk_bias = sb("qk_bias", [P, 4])
        b1_col = sb("b1_col", [P, NM])
        ln_col = sb("ln_col", [P, 4, KD])
        bv_row = sb("bv_row", [P, D])
        bo_row = sb("bo_row", [P, D])
        b2_row = sb("b2_row", [P, D])
        minus_half = sb("minus_half", [P, NT])

        x_in = sb("x_in", [P, NT, D])
        normed = sb("normed", [P, NT, D])
        x1 = sb("x1", [P, NT, D])
        x_b2 = sb("x_b2", [P, NT, D])
        x2 = sb("x2", [P, NT, D])
        y = sb("y", [P, NT, D])
        ctxn = y
        nT_h = sb("nT_h", [P, KD, L], F32R)
        nT_l = sb("nT_l", [P, KD, L], F32R)
        qk_h = sb("qk_h", [P, 2, L], F32R)
        qk_l = sb("qk_l", [P, 2, L], F32R)
        q_pad = sb("q_pad", [P, NPAIR, 2, L], F32R)
        k_stack = sb("k_stack", [P, NPAIR, L], F32R)
        v_ones = sb("v_ones", [P, NT, NH * VW + HD])
        probs = sb("probs", [P, 4, 7 * 2 * P])
        ctxT = sb("ctxT", [P, 4, L])
        cn_h = sb("cn_h", [P, KD, L], F32R)
        cn_l = sb("cn_l", [P, KD, L], F32R)
        hidden = sb("hidden", [P, NM, L])
        maxT = sb("maxT", [16, L])
        row_max = sb("row_max", [P, NT, NH])
        max_parts = sb("max_parts", [P, NT, 2, 2, 2, 4])
        max_hi = sb("max_hi", [P, NT, 2, 2, 4], F32R)
        inv_sum = sb("inv_sum", [P, NT, NH])
        stats1 = sb("stats1", [P, NT, 6])
        mv1 = sb("mv1", [P, NT, 2])
        stats2 = sb("stats2", [P, NT, 6])
        mv2 = sb("mv2", [P, NT, 2])
        lnt = sb("lnt", [P, 8, NT])
        lnt2 = sb("lnt2", [P, 4, NT])
        row_index = sb("row_index", [P, NCOL, 1 + RUN], I32)
        gather_rows = sb("gather_rows", [P, DEPTH], I32)
        scatter_rows = sb("scatter_rows", [P, 2, RUN], I32)
        unit_expert = sb("unit_expert", [P, NCOL], I32)
        unit_scale = sb("unit_scale", [P, 2, NT])
        unit_std = sb("unit_std", [P, 2, NT])
        eps_col = sb("eps_col", [P, 1])
        unit_shift = sb("unit_shift", [P, 2, NT])
        assert NH * VW + HD >= (NH - 1) * VW + 32

        staged = probs[:, :, :].rearrange("p a b -> p (a b)")
        stage2 = hidden[:, :, :].rearrange("p a b -> p (a b)")
        wqkv_raw = staged[:, 0:KD * 3 * D].rearrange("p (k n) -> p k n", k=KD)
        wo_raw = staged[:, 1536:1536 + KD * D].rearrange("p (k n) -> p k n", k=KD)
        w1_raw = staged[:, 2048:2048 + KD * DFF].rearrange("p (k n) -> p k n", k=KD)
        route = staged[:, 4096:4096 + 1024]
        ncst = consts.shape[1]
        cst = stage2[:, 0:ncst]
        assert ncst <= NM * L

        def const(name):
            return cst[:, at[name][0]:at[name][1]]

        LEAD = 1
        loaded = sem("loaded")
        zeroed = sem("zeroed")
        dve_step = sem("dve_step")
        pool_step = sem("pool_step")
        setup_mm = sem("setup_mm")
        setup_dve = sem("setup_dve")
        ready = sem("ready")
        PER = {}

        def counted(name, n):
            s = sem(name)
            PER[id(s)] = n
            return s

        x_loaded = counted("x_loaded", 16)
        x_used = counted("x_used", 1)
        mv1_ready = counted("mv1_ready", 1)
        n1_ready = counted("n1_ready", 1)
        x1_ready = counted("x1_ready", 1)
        nT_ready = counted("nT_ready", KD)
        nTh_done = counted("nTh_done", KD)
        nTl_done = counted("nTl_done", KD)
        qk_ready = counted("qk_ready", 4)
        qkh_done = counted("qkh_done", 4)
        qkl_done = counted("qkl_done", 4)
        v_ready = counted("v_ready", 2)
        v_done = counted("v_done", 2)
        sel_ready = counted("sel_ready", 2 * NPAIR)
        qsel_done = counted("qsel_done", NPAIR)
        ksel_done = counted("ksel_done", NPAIR)
        s_ready = counted("s_ready", NH)
        max_done = counted("max_done", NH)
        parts_done = counted("parts_done", 2)
        maxT_ready = counted("maxT_ready", 2)
        maxT_done = counted("maxT_done", 2)
        max_rows = [counted(f"max_rows{i}", 64) for i in range(2)]
        sT_ready = counted("sT_ready", NPAIR * NT)
        exp_done = counted("exp_done", NPAIR * NT)
        probs_ready = counted("probs_ready", NPAIR)
        ctx_ready = counted("ctx_ready", 4)
        ctx_saved = counted("ctx_saved", 4)
        ctxq_ready = counted("ctxq_ready", NT)
        ctxn_done = counted("ctxn_done", NT)
        cT_ready = counted("cT_ready", KD)
        cTh_done = counted("cTh_done", KD)
        cTl_done = counted("cTl_done", KD)
        attn_ready = counted("attn_ready", 2)
        x2_done = counted("x2_done", 2)
        mv2_ready = counted("mv2_ready", 1)
        n2_ready = counted("n2_ready", 1)
        residual_ready = counted("residual_ready", 1)
        n2T_ready = counted("n2T_ready", KD)
        n2Th_done = counted("n2Th_done", KD)
        n2Tl_done = counted("n2Tl_done", KD)
        up_ready = counted("up_ready", NM)
        gelu_done = counted("gelu_done", NM)
        down_ready = counted("down_ready", 2)
        y_done = counted("y_done", 2)
        y_stored = counted("y_stored", 16)
        y_free = sem("y_free")
        inv_step = counted("inv_step", NT)
        bn2_step = counted("bn2_step", NT)
        bn1_step = counted("bn1_step", NT)
        maxhi_step = counted("maxhi_step", 4)
        LN1_STEPS, LN2_STEPS, X1_STEPS = 7, 3, 1
        ln1_step = counted("ln1_step", LN1_STEPS)
        ln2_step = counted("ln2_step", LN2_STEPS)
        x1_step = counted("x1_step", X1_STEPS)
        norm_scale = counted("norm_scale", 1)
        sign_done = sem("sign_done")

        def until(eng, s, b, k):
            eng.wait_ge(s, b * PER[id(s)] + k)

        passed = {"DVE": sem("passed_by_dve"), "Pool": sem("passed_by_pool")}

        def apart(eng, name):
            eng.sem_inc(passed[name], 1)

        p2_zeroed = sem("p2_zeroed")
        p2_raw = sem("p2_raw")
        p2_tr = sem("p2_tr")
        p2_hi = sem("p2_hi")
        p2_bias = sem("p2_bias")
        p2_weights = sem("p2_weights")
        p2_gather_rows = sem("p2_gather_rows")
        p2_gather = [sem(f"p2_gather{i}") for i in range(DEPTH)]
        p2_bn = sem("p2_bn")
        p2_mv = sem("p2_mv")
        p2_std = sem("p2_std")
        p2_rstd = sem("p2_rstd")
        p2_scale = sem("p2_scale")
        p2_norm = sem("p2_norm")
        p2_nT = sem("p2_nT")
        p2_nTh = sem("p2_nTh")
        p2_nTl = sem("p2_nTl")
        p2_y = sem("p2_y")
        p2_scatter_rows = sem("p2_scatter_rows")
        p2_out = sem("p2_out")
        p2_scatter = [sem(f"p2_scatter{i}") for i in range(2)]

        HL = NE * KD * D
        we_raw = staged[:, 0:HL].rearrange("p (e o d) -> p e o d", e=NE, o=KD)
        pads = q_pad[:, :, :, :].rearrange("p a b c -> p (a b c)")
        we_h = pads[:, 0:HL].rearrange("p (e k o) -> p e k o", e=NE, k=KD)
        we_l = pads[:, HL:2 * HL].rearrange("p (e k o) -> p e k o", e=NE, k=KD)
        bias_parts = k_stack[:, :, :].rearrange("p a b -> p (a b)")[:, 0:NE * D]
        bias_of = bias_parts.rearrange("p (e o) -> p e o", e=NE)
        bias_raw = staged[:, HL:HL + NE * D]
        BIAS_LO = 32
        all_ones = sb("all_ones", [P, P], F32R)
        rows_all = hidden[:, :, :].rearrange("p m l -> p (m l)")
        rows_in = [rows_all[:, RUN * D * i:RUN * D * i + RUN * D].rearrange("p (j d) -> p j d", j=RUN)
                   for i in range(DEPTH)]
        rows_out = [y, x2]
        unit_normed = [normed, x1]
        p2_banks = [ffn_bank, score_bank[0:2]]
        p2_T = [(nT_h, nT_l), (cn_h, cn_l)]

        b_wide = route[:, 16:16 + KD * P].rearrange("p (k n) -> p k n", k=KD)
        at_small = 16 + KD * P
        r_score, r_cand, r_onehot = (route[:, at_small + i:at_small + i + NT * NE]
                                     .rearrange("p (c e) -> p c e", e=NE) for i in (0, 32, 64))
        r_small = route[:, at_small + 96:at_small + 108].rearrange("p (a c) -> p a c", c=NT)
        r_groups = route[:, at_small + 108:at_small + 116]
        r_start = route[:, at_small + 116:at_small + 124]
        r_gexp = route[:, at_small + 124:at_small + 124 + NCOL]
        r_tmp = route[:, at_small + 272:at_small + 272 + NCOL]
        assert NCOL <= 128
        r_int = sb("r_int", [P, 8], I32)
        r_row = staged[:, 5120:5120 + NT * P].rearrange("p (c n) -> p c n", c=NT)
        r_group = staged[:, 5632:5632 + NT * NCOL].rearrange("p (c n) -> p c n", c=NT)

        def col(v, n):
            return v.rearrange("(m p) -> p m", p=P)

        NLOAD = 19
        x_rows = x.rearrange("b (t p) d -> b p t d", p=P)
        y_rows = scratch.rearrange("(t p) (b d) -> b p t d", t=NT, b=NB)
        scratch_runs = scratch.rearrange("l (q r) -> (l q) r", q=QUADS)

        block = ctx.enter_context(nc.Block())

        @block.sync
        def _(sp):
            sp.dma_start(cst, consts).then_inc(loaded, 16)
            sp.dma_start(wqkv_raw[:, :, 0:D], Wq.rearrange("(k p) n -> p k n", p=P)).then_inc(loaded, 16)
            sp.dma_start(wqkv_raw[:, :, D:2 * D], Wk.rearrange("(k p) n -> p k n", p=P)).then_inc(loaded, 16)
            sp.dma_start(wqkv_raw[:, :, 2 * D:], Wv.rearrange("(k p) n -> p k n", p=P)).then_inc(loaded, 16)
            sp.dma_start(wo_raw, Wo.rearrange("(k p) n -> p k n", p=P)).then_inc(loaded, 16)
            sp.dma_start(w1_raw, W1.rearrange("(k p) n -> p k n", p=P)).then_inc(loaded, 16)
            sp.dma_start(w2[:, :, :], W2.rearrange("(k p) n -> p k n", p=P)).then_inc(loaded, 16)
            sp.dma_start(qk_bias[:, 0:2], col(bq, 2), allow_slow_non_contiguous=True).then_inc(loaded, 16)
            sp.dma_start(qk_bias[:, 2:4], col(bk, 2), allow_slow_non_contiguous=True).then_inc(loaded, 16)
            sp.dma_start(b1_col[:, :], col(b1, NM), allow_slow_non_contiguous=True).then_inc(loaded, 16)
            for i, v in enumerate((ln1_w, ln1_b, ln2_w, ln2_b)):
                sp.dma_start(ln_col[:, i, :], col(v, KD), allow_slow_non_contiguous=True).then_inc(loaded, 16)
            for row, v in ((bv_row, bv), (bo_row, bo), (b2_row, b2)):
                sp.dma_start(row[:, :], v.partition_broadcast(P)).then_inc(loaded, 16)
            sp.dma_start(route[0:DPOS, 0:NE], sigs.rearrange("t p -> p t"), allow_slow_non_contiguous=True).then_inc(loaded, 16)
            sp.dma_start(x_in[:, :, :], x_rows[0]).then_inc(x_loaded, 16)
            sp.dma_start(ident[:, :], consts[:, at["ident"][0]:at["ident"][1]]).then_inc(loaded, 16)

            def attention(b, ahead):
                if ahead:
                    until(sp, x_used, b, 1)
                    sp.dma_start(x_in[:, :, :], x_rows[b + 1]).then_inc(x_loaded, 16)
                for half in range(2):
                    until(sp, maxT_done, b, half + 1)
                    for par in range(2):
                        for part in range(2):
                            row = 64 * par + MAX_ROW + part
                            src = 8 * par + 4 * part
                            sp.dma_start(
                                q_pad[row:row + 1, 4 * half:4 * half + 4, par, :].bitcast(F32),
                                maxT[src:src + 4, :],
                            ).then_inc(max_rows[half], 16)

            def finish(c):
                until(sp, y_done, c, 2)
                sp.dma_start(y_rows[c], y[:, :, :]).then_inc(y_stored, 16)
                until(sp, y_stored, c, 16)
                sp.sem_inc(y_free, 1)

            sp.sem_inc(y_free, LEAD)
            attention(0, True)
            with sp.Fori(1, NB - 1) as b:
                attention(b, True)
                finish(b - 1)
            attention(NB - 1, False)
            finish(NB - 2)

            until(sp, ctx_ready, NB - 1, 4)
            sp.dma_start(staged[:, 0:HL].rearrange("p (e o d) -> p e o d", e=NE, o=KD),
                         We.rearrange("e (o p) d -> p e o d", p=P)).then_inc(p2_raw, 16)
            for part in (0, BIAS_LO):
                sp.dma_start(bias_raw[part:part + 1, :], be.rearrange("(a e) o -> a (e o)", a=1)).then_inc(p2_raw, 16)

            finish(NB - 1)

        @block.gpsimd
        def _(pool):
            nc.gpsimd.memset(v_ones[:, :, :], 0.0).then_inc(pool_step, 1)
            nc.gpsimd.memset(minus_half[:, :], -0.5).then_inc(pool_step, 1)
            nc.gpsimd.memset(eps_col[:, :], EPS).then_inc(pool_step, 1)
            nc.gpsimd.memset(all_ones[:, :].bitcast(F32), 1.0).then_inc(pool_step, 1)
            nc.gpsimd.memset(q_pad[:, :, :, :].bitcast(F32), 0.0).then_inc(pool_step, 1)
            pool.wait_ge(pool_step, 1)
            nc.gpsimd.memset(v_ones[:, :, 0:NH * VW].rearrange("p t (h w) -> p t h w", w=VW)[:, :, :, 0:1],
                             1.0).then_inc(pool_step, 1)
            pool.wait_ge(pool_step, 6)
            nc.gpsimd.memset(lnt2[:, 3, :], 0.0).then_inc(ready, 1)
            pool.wait_ge(loaded, 16 * NLOAD)

            def rsqrt_step(done, dst, src, tmp, step, at_step):
                nc.gpsimd.tensor_scalar(tmp, src, EPS, 1.0, ALU.add, ALU.mult).then_inc(step, 1)
                done(at_step)
                nc.gpsimd.tensor_tensor(dst, tmp, minus_half[:, :], ALU.pow).then_inc(step, 1)
                done(at_step + 1)

            def norm1(b):
                until(pool, mv1_ready, b, 1)
                apart(pool, "Pool")
                if isinstance(b, int) and b == 0:
                    pass
                else:
                    until(pool, nT_ready, b - 1, KD)
                    apart(pool, "Pool")

                def done(k):
                    until(pool, ln1_step, b, k)
                    apart(pool, "Pool")

                neg_mean, r, t, r1 = lnt[:, 0, :], lnt[:, 1, :], lnt[:, 2, :], lnt[:, 3, :]
                var = mv1[:, :, 1]
                nc.gpsimd.tensor_scalar(neg_mean, mv1[:, :, 0], -1.0, 0.0, ALU.mult, ALU.add).then_inc(ln1_step, 1)
                rsqrt_step(done, r, var, lnt[:, 4, :], ln1_step, 2)
                nc.gpsimd.tensor_tensor(t, var, r, ALU.mult).then_inc(ln1_step, 1)
                done(4)
                nc.gpsimd.tensor_tensor(lnt[:, 5, :], t, r, ALU.mult).then_inc(ln1_step, 1)
                done(5)
                nc.gpsimd.tensor_scalar(lnt[:, 6, :], lnt[:, 5, :], EPS, 1.0, ALU.add, ALU.mult).then_inc(ln1_step, 1)
                done(6)
                nc.gpsimd.tensor_tensor(r1, lnt[:, 6, :], minus_half[:, :], ALU.pow).then_inc(ln1_step, 1)
                done(7)
                nc.gpsimd.tensor_tensor(lnt[:, 7, :], r, r1, ALU.mult).then_inc(norm_scale, 1)
                until(pool, norm_scale, b, 1)
                apart(pool, "Pool")
                for t_ in range(NT):
                    last = nc.gpsimd.tensor_scalar(normed[:, t_, :], x_in[:, t_, :], neg_mean[:, t_:t_ + 1],
                                                   lnt[:, 7, t_:t_ + 1], ALU.add, ALU.mult)
                last.then_inc(n1_ready, 1)

            def norm2(c):
                until(pool, mv2_ready, c, 1)
                apart(pool, "Pool")

                def done(k):
                    until(pool, ln2_step, c, k)
                    apart(pool, "Pool")

                neg_mean, r = lnt2[:, 0, :], lnt2[:, 1, :]
                nc.gpsimd.tensor_scalar(neg_mean, mv2[:, :, 0], -1.0, 0.0, ALU.mult, ALU.add).then_inc(ln2_step, 1)
                rsqrt_step(done, r, mv2[:, :, 1], lnt2[:, 2, :], ln2_step, 2)
                for t in range(NT):
                    last = nc.gpsimd.tensor_scalar(normed[:, t, :], x2[:, t, :], neg_mean[:, t:t + 1],
                                                   r[:, t:t + 1], ALU.add, ALU.mult)
                last.then_inc(n2_ready, 1)
                until(pool, n2_ready, c, 1)
                apart(pool, "Pool")
                nc.gpsimd.tensor_tensor(x2[:, :, :], x2[:, :, :], x_b2[:, :, :], ALU.add).then_inc(residual_ready, 1)

            def residuals(b):
                for t in range(NT):
                    last = nc.gpsimd.tensor_scalar(x1[:, t, :], x_in[:, t, :], lnt[:, 0, t:t + 1],
                                                   lnt[:, 1, t:t + 1], ALU.add, ALU.mult)
                last.then_inc(x1_step, 1)
                if not (isinstance(b, int) and b == 0):
                    until(pool, residual_ready, b - 1, 1)
                    apart(pool, "Pool")
                for t in range(NT):
                    last = nc.gpsimd.tensor_tensor(x_b2[:, t, :], x_in[:, t, :], b2_row[:, :], ALU.add)
                last.then_inc(x_used, 1)
                until(pool, x1_step, b, 1)
                apart(pool, "Pool")
                for t in range(NT):
                    last = nc.gpsimd.tensor_tensor(x1[:, t, :], x1[:, t, :], bo_row[:, :], ALU.add)
                last.then_inc(x1_ready, 1)

            def masks(b):
                for p in range(NPAIR):
                    until(pool, exp_done, b, NT * (p + 1))
                    apart(pool, "Pool")
                    blocks = probs[:, p % 4, 0:12 * P].rearrange("p (a h q) -> p a h q", h=2, q=P)
                    same, after = blocks[:, :, 0, :], blocks[:, :, 1, :]
                    last = probs[:, p % 4, 12 * P:14 * P].rearrange("p (a q) -> p a q", q=P)
                    for part, n, sign in ((same, 6, 1), (last, 2, 1), (after, 6, -1)):
                        done = nc.gpsimd.affine_select(
                            out=part, in_=part, compare_op=ALU.is_ge, fill=0.0,
                            base=0 if sign == 1 else WINDOW - P, pattern=[[0, n], [sign, P]],
                            channel_multiplier=-sign)
                    done.then_inc(probs_ready, 1)

            norm1(0)
            residuals(0)
            norm1(1)
            masks(0)
            with pool.Fori(1, NB - 1) as b:
                norm2(b - 1)
                residuals(b)
                norm1(b + 1)
                masks(b)
            norm2(NB - 2)
            residuals(NB - 1)
            masks(NB - 1)
            norm2(NB - 1)

            nc.gpsimd.memset(bias_parts.bitcast(F32), 0.0).then_inc(p2_zeroed, 1)

            def gather(m, i):
                pool.wait_ge(p2_gather_rows, m + 1)
                apart(pool, "Pool")
                nc.gpsimd.indirect_dma_start(
                    rows_in[i].rearrange("p j d -> p (j d)"), None, scratch_runs,
                    bass.IndirectOffsetOnAxis(ap=gather_rows[:, i:i + 1].bitcast(U32), axis=0),
                    bounds_check=L * QUADS - 1, oob_is_err=False).then_inc(p2_gather[i], 16)

            def scatter(n, i):
                pool.wait_ge(p2_scatter_rows, n + 1)
                apart(pool, "Pool")
                pool.wait_ge(p2_out, 2 * n + 2)
                apart(pool, "Pool")
                for j in range(RUN):
                    nc.gpsimd.indirect_dma_start(
                        out, bass.IndirectOffsetOnAxis(ap=scatter_rows[:, i % 2, j:j + 1].bitcast(U32), axis=0),
                        rows_out[i % 2][:, j, :], None,
                        bounds_check=NB * L - 1, oob_is_err=False).then_inc(p2_scatter[i % 2], 16)

            until(pool, y_stored, NB - 1, 16)
            for m in range(AHEAD):
                gather(m, m)
            with pool.Fori(0, NUNIT, DEPTH) as n0:
                for i in range(DEPTH):
                    gather(n0 + (i + AHEAD), (i + AHEAD) % DEPTH)
                    scatter(n0 + i, i)
            for i in range(2):
                pool.wait_ge(p2_scatter[i], 16 * RUN * (NUNIT // 2))
            for i in range(DEPTH):
                pool.wait_ge(p2_gather[i], 16 * (NUNIT // DEPTH + (1 if i < AHEAD else 0)))

        @block.scalar
        def _(act):
            act.wait_ge(loaded, 16 * NLOAD)
            nc.scalar.activation(route[0:DPOS, 8:16], route[0:DPOS, 0:NE], ACT.Sign).then_inc(sign_done, 1)
            act.wait_ge(ready, 2)

            def round_banks(c, ready_sem, dst, done_sem):
                for k in range(KD):
                    until(act, ready_sem, c, k + 1)
                    nc.scalar.activation(dst[:, k, :], mix_bank[k][:, :], ACT.Copy).then_inc(done_sem, 1)

            def qk_hi(b, g):
                for i in range(2):
                    until(act, qk_ready, b, 2 * g + i + 1)
                    nc.scalar.activation(qk_h[:, i, :], ffn_bank[i][:, :], ACT.Identity,
                                         bias=qk_bias[:, 2 * i + g:2 * i + g + 1]).then_inc(qkh_done, 1)

            def q_stacks(b, g):
                for p in range(4 * g, 4 * g + 4):
                    until(act, sel_ready, b, 2 * p + 1)
                    bank = select_bank[(2 * p) % 4]
                    nc.scalar.activation(q_pad[0:64, p, 0, :], bank[0:64, :], ACT.Copy)
                    nc.scalar.activation(q_pad[64:P, p, 1, :], bank[64:P, :], ACT.Copy).then_inc(qsel_done, 1)

            def gelu(c, m):
                until(act, up_ready, c, m + 1)
                nc.scalar.activation(hidden[:, m, :], ffn_bank[m % 2][:, :], ACT.Gelu_apprx_tanh,
                                     bias=b1_col[:, m:m + 1]).then_inc(gelu_done, 1)

            def max_out(b, half):
                until(act, maxT_ready, b, half + 1)
                if half == 1:
                    until(act, max_rows[0], b, 64)
                nc.scalar.activation(maxT[:, :], mix_bank[half][0:16, :], ACT.Copy).then_inc(maxT_done, 1)

            def exps(b, p):
                for kc in range(NT):
                    until(act, sT_ready, b, NT * p + kc + 1)
                    if kc == 0 and p >= 4 and p % 2 == 0:
                        until(act, ctx_ready, b, p // 2 - 1)
                    n = 4 * P if kc < NT - 1 else 2 * P
                    nc.scalar.activation(probs[:, p % 4, 4 * P * kc:4 * P * kc + n], score_bank[kc][:, 0:n],
                                         ACT.Exp, scale=SCALE).then_inc(exp_done, 1)

            def save_ctx(b, g):
                until(act, ctx_ready, b, g + 1)
                nc.scalar.activation(ctxT[:, g, :], mix_bank[g % 2][:, :], ACT.Copy).then_inc(ctx_saved, 1)

            def iteration(b, c):
                if b is not None:
                    round_banks(b, nT_ready, nT_h, nTh_done)
                    qk_hi(b, 0)
                if c is not None:
                    round_banks(c, cT_ready, cn_h, cTh_done)
                if b is not None:
                    q_stacks(b, 0)
                    qk_hi(b, 1)
                    q_stacks(b, 1)
                if c is not None:
                    round_banks(c, n2T_ready, cn_h, n2Th_done)
                for m in range(NM):
                    if c is not None:
                        gelu(c, m)
                    if b is not None and m == 2:
                        max_out(b, 0)
                if b is not None:
                    max_out(b, 1)
                    for p in range(NPAIR):
                        exps(b, p)
                        if p in (4, 6):
                            save_ctx(b, (p - 4) // 2)
                    save_ctx(b, 2)
                    save_ctx(b, 3)

            iteration(0, None)
            with act.Fori(1, NB - 1) as b:
                iteration(b, b - 1)
            iteration(NB - 1, NB - 2)
            iteration(None, NB - 1)

            for i in range(8):
                act.wait_ge(p2_tr, i + 1)
                dst = we_h.rearrange("p e k o -> p (e k o)")[:, 512 * i:512 * i + 512]
                nc.scalar.activation(dst, score_bank[i % 4][:, :], ACT.Copy).then_inc(p2_hi, 1)

            def unit_norm(m, i):
                act.wait_ge(p2_mv, m + 1)
                nc.scalar.activation(unit_std[:, i % 2, :], mv2[:, :, 1], ACT.Sqrt, bias=eps_col[:, :])\
                    .then_inc(p2_std, 1)
                act.wait_ge(p2_scale, m + 1)
                if not (isinstance(m, int) and m < 2):
                    act.wait_ge(p2_nT, (m - 1) * KD)
                for j in range(RUN):
                    last = nc.scalar.activation(unit_normed[i % 2][:, j, :], rows_in[i % DEPTH][:, j, :], ACT.Identity,
                                                bias=unit_shift[:, i % 2, j:j + 1], scale=unit_scale[:, i % 2, j:j + 1])
                last.then_inc(p2_norm, 1)

            def unit_hi(m, i):
                for k in range(KD):
                    act.wait_ge(p2_nT, m * KD + (k + 1))
                    nc.scalar.activation(p2_T[i % 2][0][:, k, :], mix_bank[k][:, :], ACT.Copy).then_inc(p2_nTh, 1)

            unit_norm(0, 0)
            unit_norm(1, 1)
            unit_hi(0, 0)
            with act.Fori(0, NUNIT, DEPTH) as n0:
                for i in range(DEPTH):
                    unit_hi(n0 + (i + 1), i + 1)
                    unit_norm(n0 + (i + 2), i + 2)

        @block.vector
        def _(dve):
            steps = [0]

            def link(ins):
                steps[0] += 1
                ins.then_inc(dve_step, 1)
                dve.wait_ge(dve_step, steps[0])

            dve.wait_ge(loaded, 16 * NLOAD)
            for k in range(KD):
                last = nc.vector.tensor_scalar(b_wide[:, k, :], const("ones"), ln_col[:, 1, k:k + 1], None, ALU.mult)
            last.then_inc(setup_dve, 1)
            for n in sel:
                nc.vector.tensor_copy(sel[n][:, :, :], const(n).rearrange("p (a b) -> p a b", b=P))
            nc.vector.tensor_copy(mask[:, :], const("mask"))
            nc.vector.tensor_copy(minus_one_rows[:, :], const("minus_one_rows"))
            for k in range(KD):
                nc.vector.tensor_scalar(wqkv_h[:, k, :], wqkv_raw[:, k, :], ln_col[:, 0, k:k + 1], None, ALU.mult)
                link(nc.vector.tensor_scalar(w1_h[:, k, :], w1_raw[:, k, :], ln_col[:, 2, k:k + 1], None, ALU.mult))
                nc.vector.scalar_tensor_tensor(wqkv_l[:, k, :], wqkv_raw[:, k, :], ln_col[:, 0, k:k + 1],
                                               wqkv_h[:, k, :].bitcast(F32), ALU.mult, ALU.subtract)
                link(nc.vector.scalar_tensor_tensor(w1_l[:, k, :], w1_raw[:, k, :], ln_col[:, 2, k:k + 1],
                                                    w1_h[:, k, :].bitcast(F32), ALU.mult, ALU.subtract))
            link(nc.vector.tensor_copy(wo_h[:, :, :], wo_raw))
            nc.vector.tensor_tensor(wo_l[:, :, :], wo_raw, wo_h[:, :, :].bitcast(F32), ALU.subtract)
            dve.wait_ge(setup_mm, 1)
            nc.vector.tensor_tensor(qk_bias[:, :], score_bank[0][:, 0:4], qk_bias[:, :], ALU.add)
            nc.vector.tensor_tensor(b1_col[:, :], score_bank[1][:, 0:NM], b1_col[:, :], ALU.add)
            nc.vector.tensor_tensor(bv_row[:, :], score_bank[2][:, 0:D], bv_row[:, :], ALU.add)

            def spread(a):
                return a.unsqueeze(2).broadcast_to([P, NT, NE])

            rank3 = const("expert_rank").rearrange("p (c e) -> p c e", e=NE)
            link(nc.vector.tensor_copy(r_score, score_bank[3][:, 0:NT * NE].rearrange("p (c e) -> p c e", e=NE)))
            link(nc.vector.tensor_reduce(r_small[:, 0, :], r_score, AX_X, ALU.max))
            link(nc.vector.tensor_tensor(r_cand, r_score, spread(r_small[:, 0, :]), ALU.is_equal))
            link(nc.vector.tensor_tensor(r_cand, r_cand, rank3, ALU.mult))
            link(nc.vector.tensor_reduce(r_small[:, 1, :], r_cand, AX_X, ALU.max))
            nc.vector.tensor_tensor(r_onehot, r_cand, spread(r_small[:, 1, :]), ALU.is_equal).then_inc(setup_dve, 1)
            dve.wait_ge(setup_mm, 2)
            nc.vector.tensor_copy(r_score, score_bank[0][:, 0:NT * NE].rearrange("p (c e) -> p c e", e=NE))
            link(nc.vector.tensor_scalar(r_int[:, 0:NE], score_bank[1][:, 0:NE], float(SLOTS - 1), None, ALU.add))
            link(nc.vector.tensor_scalar(r_int[:, 0:NE], r_int[:, 0:NE], SLOTS.bit_length() - 1, None,
                                         ALU.arith_shift_right))
            nc.vector.tensor_copy(r_groups, r_int[:, 0:NE])
            link(nc.vector.memset(r_start, 0.0))
            for e in range(NE - 1):
                link(nc.vector.tensor_tensor(r_start[:, e + 1:e + 2], r_start[:, e:e + 1], r_groups[:, e:e + 1],
                                             ALU.add))
            link(nc.vector.memset(r_gexp, 0.0))
            for e in range(1, NE):
                link(nc.vector.scalar_tensor_tensor(r_gexp, const("unit_iota"), r_start[:, e:e + 1], r_gexp,
                                                    ALU.is_ge, ALU.add))
            nc.vector.tensor_copy(unit_expert[:, :], r_gexp)
            link(nc.vector.tensor_scalar(r_start, r_start, float(SLOTS), None, ALU.mult))
            link(nc.vector.tensor_tensor(r_score, r_score, r_start.unsqueeze(1).broadcast_to([P, NT, NE]), ALU.add))
            link(nc.vector.tensor_tensor(r_score, r_score, r_onehot, ALU.mult))
            link(nc.vector.tensor_reduce(r_small[:, 0, :], r_score, AX_X, ALU.add))
            link(nc.vector.tensor_copy(r_int[:, 0:NT], r_small[:, 0, :]))
            link(nc.vector.tensor_scalar(r_int[:, NT:2 * NT], r_int[:, 0:NT], SLOTS.bit_length() - 1, None,
                                         ALU.arith_shift_right))
            link(nc.vector.tensor_copy(r_small[:, 1, :], r_int[:, NT:2 * NT]))
            link(nc.vector.scalar_tensor_tensor(r_small[:, 2, :], r_small[:, 1, :], -float(SLOTS), r_small[:, 0, :],
                                                ALU.mult, ALU.add))
            for c in range(NT):
                nc.vector.tensor_scalar(r_row[:, c, :], const("slot_of_row"), r_small[:, 2, c:c + 1], None,
                                        ALU.is_equal)
                last = nc.vector.tensor_scalar(r_group[:, c, :], const("unit_iota"), r_small[:, 1, c:c + 1],
                                               const("position_plus_1")[:, c:c + 1], ALU.is_equal, ALU.mult)
            last.then_inc(setup_dve, 1)
            dve.wait_ge(setup_mm, 3)
            nc.vector.tensor_scalar(r_gexp, score_bank[2][:, 0:NCOL], 0.0, EMPTY, ALU.is_equal, ALU.mult)
            link(nc.vector.tensor_scalar(r_tmp, score_bank[2][:, 0:NCOL], float(QUADS), const("first_run"),
                                         ALU.mult, ALU.add))
            link(nc.vector.tensor_tensor(row_index[:, :, 0], r_gexp, r_tmp, ALU.add))
            for j in range(RUN):
                link(nc.vector.scalar_tensor_tensor(row_index[:, :, 1 + j], score_bank[2][:, 0:NCOL],
                                                    const("first_row")[:, j:j + 1], r_gexp, ALU.add, ALU.add))
            nc.vector.memset(max_parts[:, :, :, :, :, :], 0.0).then_inc(ready, 1)
            dve.wait_ge(ready, 2)

            def stats(b):
                until(dve, x_loaded, b, 16)
                for t in range(NT):
                    nc.vector.bn_stats(stats1[:, t, :], x_in[:, t, :]).then_inc(bn1_step, 1)
                if not (isinstance(b, int) and b == 0):
                    until(dve, n1_ready, b - 1, 1)
                for t in range(NT):
                    until(dve, bn1_step, b, t + 1)
                    apart(dve, "DVE")
                    last = nc.vector.bn_aggr(mv1[:, t, :], stats1[:, t, :])
                last.then_inc(mv1_ready, 1)

            def rest_of_banks(c, hi, hi_done, lo, lo_done):
                for k in range(KD):
                    until(dve, hi_done, c, k + 1)
                    nc.vector.tensor_tensor(lo[:, k, :], mix_bank[k][:, :], hi[:, k, :].bitcast(F32), ALU.subtract)\
                        .then_inc(lo_done, 1)

            def normalise(c):
                dve.wait_ge(y_free, LEAD + c)
                for t in range(NT):
                    until(dve, ctxq_ready, c, t + 1)
                    heads = score_bank[t][:, :].rearrange("p (h w) -> p h w", w=32)
                    nc.vector.reciprocal(inv_sum[:, t, :].unsqueeze(2), heads[:, :, 0:1]).then_inc(inv_step, 1)
                for t in range(NT):
                    heads = score_bank[t][:, :].rearrange("p (h w) -> p h w", w=32)
                    until(dve, inv_step, c, t + 1)
                    nc.vector.tensor_tensor(ctxn[:, t, :].rearrange("p (h d) -> p h d", d=HD), heads[:, :, 1:VW],
                                            inv_sum[:, t, :].unsqueeze(2).broadcast_to([P, NH, HD]), ALU.mult)\
                        .then_inc(ctxn_done, 1)

            def qk_lo(b, g):
                for i in range(2):
                    until(dve, qkh_done, b, 2 * g + i + 1)
                    nc.vector.scalar_tensor_tensor(qk_l[:, i, :], ffn_bank[i][:, :],
                                                   qk_bias[:, 2 * i + g:2 * i + g + 1],
                                                   qk_h[:, i, :].bitcast(F32), ALU.add, ALU.subtract)\
                        .then_inc(qkl_done, 1)

            def values(b):
                for u in range(2):
                    until(dve, v_ready, b, u + 1)
                    for s in range(2):
                        t = 2 * u + s
                        dst = v_ones[:, t, 0:NH * VW].rearrange("p (h w) -> p h w", w=VW)[:, :, 1:VW]
                        last = nc.vector.tensor_tensor(
                            dst, ffn_bank[u][:, D * s:D * s + D].rearrange("p (h d) -> p h d", d=HD),
                            bv_row[:, :].rearrange("p (h d) -> p h d", d=HD), ALU.add)
                    last.then_inc(v_done, 1)

            def after_attention(c):
                for u in range(2):
                    until(dve, x1_ready, c, 1)
                    until(dve, attn_ready, c, u + 1)
                    nc.vector.tensor_tensor(x2[:, 2 * u:2 * u + 2, :].rearrange("p t d -> p (t d)"),
                                            score_bank[2 + u][:, :],
                                            x1[:, 2 * u:2 * u + 2, :].rearrange("p t d -> p (t d)"), ALU.add)\
                        .then_inc(x2_done, 1)
                for t in range(NT):
                    until(dve, x2_done, c, t // 2 + 1)
                    nc.vector.bn_stats(stats2[:, t, :], x2[:, t, :]).then_inc(bn2_step, 1)
                for t in range(NT):
                    until(dve, bn2_step, c, t + 1)
                    apart(dve, "DVE")
                    last = nc.vector.bn_aggr(mv2[:, t, :], stats2[:, t, :])
                last.then_inc(mv2_ready, 1)

            def k_stacks(b, g):
                for p in range(4 * g, 4 * g + 4):
                    until(dve, sel_ready, b, 2 * p + 2)
                    nc.vector.tensor_scalar(k_stack[:, p, :], select_bank[(2 * p + 1) % 4][:, :],
                                            minus_one_rows[:, 0:1], None, ALU.add).then_inc(ksel_done, 1)

            def head_max(b, h):
                until(dve, s_ready, b, h + 1)
                apart(dve, "DVE")
                for t in range(NT):
                    bank = score_bank[2 * (h % 2) + t // 2]
                    c0 = 2 * P * (t % 2)
                    lo = P if t == 0 else 0
                    block_ = bank[:, c0 + lo:c0 + 2 * P]
                    last = nc.vector.tensor_tensor_reduce(
                        out=block_, in0=block_, in1=mask[:, lo:2 * P],
                        scale=1.0, scalar=LOWEST, op0=ALU.add, op1=ALU.max, accum_out=row_max[:, t, h:h + 1])
                last.then_inc(max_done, 1)

            def max_split(b, half):
                until(dve, max_done, b, 8 * half + 8)
                src = row_max[:, :, 8 * half:8 * half + 8].rearrange("p t (j a) -> p t a j", a=2)
                for par in range(2):
                    nc.vector.tensor_copy(max_hi[:, :, half, par, :], src[:, :, par, :]).then_inc(maxhi_step, 1)
                for par in range(2):
                    until(dve, maxhi_step, b, 2 * half + par + 1)
                    hi = max_hi[:, :, half, par, :].bitcast(F32)
                    nc.vector.tensor_copy(max_parts[:, :, half, par, 0, :], hi)
                    last = nc.vector.tensor_tensor(max_parts[:, :, half, par, 1, :], src[:, :, par, :], hi,
                                                   ALU.subtract)
                last.then_inc(parts_done, 1)

            def outputs(c):
                for u in range(2):
                    until(dve, residual_ready, c, 1)
                    until(dve, down_ready, c, u + 1)
                    nc.vector.tensor_tensor(y[:, 2 * u:2 * u + 2, :].rearrange("p t d -> p (t d)"),
                                            ffn_bank[u][:, :],
                                            x2[:, 2 * u:2 * u + 2, :].rearrange("p t d -> p (t d)"), ALU.add)\
                        .then_inc(y_done, 1)

            def iteration(b, c, ahead):
                if b is not None:
                    rest_of_banks(b, nT_h, nTh_done, nT_l, nTl_done)
                if c is not None:
                    normalise(c)
                if b is not None:
                    qk_lo(b, 0)
                if c is not None:
                    rest_of_banks(c, cn_h, cTh_done, cn_l, cTl_done)
                if b is not None:
                    values(b)
                    k_stacks(b, 0)
                if c is not None:
                    after_attention(c)
                if b is not None:
                    qk_lo(b, 1)
                    k_stacks(b, 1)
                    head_max(b, 0)
                    head_max(b, 1)
                if c is not None:
                    rest_of_banks(c, cn_h, n2Th_done, cn_l, n2Tl_done)
                if b is not None:
                    for h in range(2, NH):
                        head_max(b, h)
                        if h == 7:
                            max_split(b, 0)
                        if h == 11 and ahead:
                            stats(b + 1)
                    max_split(b, 1)
                if c is not None:
                    outputs(c)

            stats(0)
            iteration(0, None, True)
            with dve.Fori(1, NB - 1) as b:
                iteration(b, b - 1, True)
            iteration(NB - 1, NB - 2, False)
            iteration(None, NB - 1, False)

            dve.wait_ge(p2_raw, 48)
            dve.wait_ge(p2_zeroed, 1)
            for part in (0, BIAS_LO):
                nc.vector.tensor_copy(bias_parts[part:part + 1, :], bias_raw[part:part + 1, :]).then_inc(p2_bias, 1)
            dve.wait_ge(p2_bias, 2)
            lo_row = slice(BIAS_LO, BIAS_LO + 1)
            nc.vector.tensor_tensor(bias_parts[lo_row, :], bias_raw[lo_row, :], bias_parts[lo_row, :].bitcast(F32),
                                    ALU.subtract)
            for i in range(NE):
                dve.wait_ge(p2_hi, i + 1)
                part = slice(KD * D * i, KD * D * i + KD * D)
                nc.vector.tensor_tensor(we_l.rearrange("p e k o -> p (e k o)")[:, part], score_bank[i % 4][:, :],
                                        we_h.rearrange("p e k o -> p (e k o)")[:, part].bitcast(F32),
                                        ALU.subtract).then_inc(p2_weights, 1)

            def gather_table(m, i):
                nc.vector.tensor_copy(gather_rows[:, i % DEPTH:i % DEPTH + 1], row_index[:, bass.ds(m, 1), 0])\
                    .then_inc(p2_gather_rows, 1)

            def row_stats(m, i, n0):
                dve.wait_ge(p2_gather[i % DEPTH], n0 * (16 // DEPTH) + 16 * (i // DEPTH + 1))
                for j in range(RUN):
                    nc.vector.bn_stats(stats2[:, j, :], rows_in[i % DEPTH][:, j, :]).then_inc(p2_bn, 1)
                for j in range(RUN):
                    dve.wait_ge(p2_bn, m * RUN + (j + 1))
                    apart(dve, "DVE")
                    last = nc.vector.bn_aggr(mv2[:, j, :], stats2[:, j, :])
                last.then_inc(p2_mv, 1)

            def scale_shift(m, i):
                if not (isinstance(m, int) and m < 2):
                    dve.wait_ge(p2_norm, m - 1)
                dve.wait_ge(p2_std, m + 1)
                scale, shift = unit_scale[:, i % 2, :], unit_shift[:, i % 2, :]
                nc.vector.reciprocal(scale, unit_std[:, i % 2, :]).then_inc(p2_rstd, 1)
                dve.wait_ge(p2_rstd, m + 1)
                nc.vector.scalar_tensor_tensor(shift, mv2[:, :, 0], -1.0, scale, ALU.mult, ALU.mult)\
                    .then_inc(p2_scale, 1)

            def unit_lo(m, i):
                for k in range(KD):
                    dve.wait_ge(p2_nTh, m * KD + (k + 1))
                    nc.vector.tensor_tensor(p2_T[i % 2][1][:, k, :], mix_bank[k][:, :],
                                            p2_T[i % 2][0][:, k, :].bitcast(F32), ALU.subtract).then_inc(p2_nTl, 1)

            def unit_out(n, i, n0):
                if not (isinstance(n, int) and n < 2):
                    dve.wait_ge(p2_scatter[i % 2], n0 * (16 * RUN // 2) + 16 * RUN * (i // 2))
                nc.vector.tensor_copy(scatter_rows[:, i % 2, :], row_index[:, bass.ds(n, 1), 1:1 + RUN])\
                    .then_inc(p2_scatter_rows, 1)
                for u in range(2):
                    dve.wait_ge(p2_y, 2 * n + (u + 1))
                    nc.vector.tensor_tensor(
                        rows_out[i % 2][:, 2 * u:2 * u + 2, :].rearrange("p t d -> p (t d)"),
                        p2_banks[i % 2][u][:, :],
                        rows_in[i % DEPTH][:, 2 * u:2 * u + 2, :].rearrange("p t d -> p (t d)"), ALU.add)\
                        .then_inc(p2_out, 1)

            def units(n0):
                for i in range(DEPTH):
                    gather_table(n0 + (i + AHEAD), i + AHEAD)
                    row_stats(n0 + (i + 2), i + 2, n0)
                    unit_lo(n0 + (i + 1), i + 1)
                    scale_shift(n0 + (i + 2), i + 2)
                    unit_out(n0 + i, i, n0)

            for m in range(AHEAD):
                gather_table(m, m)
            for m in range(2):
                row_stats(m, m, 0)
                scale_shift(m, m)
            unit_lo(0, 0)
            units(0)
            with dve.Fori(DEPTH, NUNIT, DEPTH) as n0:
                units(n0)

        @block.tensor
        def _(pe):
            mm = nc.tensor.matmul

            pe.wait_ge(loaded, 16 * NLOAD)
            for m in range(4):
                for k in range(KD):
                    mm(score_bank[0][:, m:m + 1], wqkv_raw[:, k, P * m:P * m + P], ln_col[:, 1, k:k + 1],
                       start=k == 0, stop=k == KD - 1)
            for m in range(NM):
                for k in range(KD):
                    mm(score_bank[1][:, m:m + 1], w1_raw[:, k, P * m:P * m + P], ln_col[:, 3, k:k + 1],
                       start=k == 0, stop=k == KD - 1)
            pe.wait_ge(sign_done, 1)
            for c in range(NT):
                mm(score_bank[3][:, NE * c:NE * c + NE], const("position_code")[0:DPOS, P * c:P * c + P],
                   route[0:DPOS, NE:2 * NE], start=True, stop=True)
            pe.wait_ge(setup_dve, 1)
            for k in range(KD):
                last = mm(score_bank[2][:, 0:D], b_wide[:, k, :], wqkv_raw[:, k, 2 * D:3 * D],
                          start=k == 0, stop=k == KD - 1)
            last.then_inc(setup_mm, 1)
            pe.wait_ge(setup_dve, 2)
            for c in range(NT):
                for c2 in range(c + 1):
                    mm(score_bank[0][:, NE * c:NE * c + NE], const("before") if c2 == c else const("ones"),
                       r_onehot[:, c2, :], start=c2 == 0, stop=c2 == c)
            for c in range(NT):
                last = mm(score_bank[1][:, 0:NE], const("ones"), r_onehot[:, c, :], start=c == 0, stop=c == NT - 1)
            last.then_inc(setup_mm, 1)
            pe.wait_ge(setup_dve, 3)
            for c in range(NT):
                last = mm(score_bank[2][:, 0:NCOL], r_row[:, c, :], r_group[:, c, :], start=c == 0, stop=c == NT - 1)
            last.then_inc(setup_mm, 1)
            pe.wait_ge(ready, 2)

            def split_product(out, pairs):
                terms = [(a[0], a[2]) for a in pairs] + [(a[1], a[2]) for a in pairs] + [(a[0], a[3]) for a in pairs]
                for i, (lhsT, rhs) in enumerate(terms):
                    last = mm(out, lhsT, rhs, start=i == 0, stop=i == len(terms) - 1)
                return last

            def transpose_rows(src, ready_sem):
                for k in range(KD):
                    for t in range(NT):
                        last = nc.tensor.transpose(mix_bank[k][:, P * t:P * t + P], src[:, t, P * k:P * k + P],
                                                   ident[:, :])
                    last.then_inc(ready_sem, 1)

            def input_transposes(b):
                if not (isinstance(b, int) and b == 0):
                    until(pe, ctx_saved, b - 1, 4)
                until(pe, n1_ready, b, 1)
                transpose_rows(normed, nT_ready)

            def context_to_rows(c):
                until(pe, ctx_saved, c, 4)
                for t in range(NT):
                    for g in range(4):
                        last = nc.tensor.transpose(score_bank[t][:, P * g:P * g + P], ctxT[:, g, P * t:P * t + P],
                                                   ident[:, :])
                    last.then_inc(ctxq_ready, 1)

            def project_qk(b, g):
                if g == 0:
                    until(pe, nTh_done, b, KD)
                    until(pe, nTl_done, b, KD)
                for i in range(2):
                    if g == 1:
                        until(pe, (qsel_done, ksel_done)[i], b, 3)
                    w = slice(D * i + P * g, D * i + P * g + P)
                    split_product(ffn_bank[i][:, :], [
                        (wqkv_h[:, k, w], wqkv_l[:, k, w], nT_h[:, k, :], nT_l[:, k, :]) for k in range(KD)
                    ]).then_inc(qk_ready, 1)

            def context_transposes(c):
                for t in range(NT):
                    until(pe, ctxn_done, c, t + 1)
                    for k in range(KD):
                        last = nc.tensor.transpose(mix_bank[k][:, P * t:P * t + P], ctxn[:, t, P * k:P * k + P],
                                                   ident[:, :])
                        if t == NT - 1:
                            last.then_inc(cT_ready, 1)

            def project_v(b):
                for u in range(2):
                    until(pe, qkl_done, b, u + 1)
                    for s in range(2):
                        c = slice(P * (2 * u + s), P * (2 * u + s) + P)
                        last = split_product(ffn_bank[u][:, D * s:D * s + D], [
                            (nT_h[:, k, c], nT_l[:, k, c], wqkv_h[:, k, 2 * D:], wqkv_l[:, k, 2 * D:])
                            for k in range(KD)])
                    last.then_inc(v_ready, 1)

            def project_out(c):
                until(pe, cTl_done, c, KD)
                for u in range(2):
                    for s in range(2):
                        cols = slice(P * (2 * u + s), P * (2 * u + s) + P)
                        last = split_product(score_bank[2 + u][:, D * s:D * s + D], [
                            (cn_h[:, k, cols], cn_l[:, k, cols], wo_h[:, k, :], wo_l[:, k, :])
                            for k in range(KD)])
                    last.then_inc(attn_ready, 1)

            def stacks(b, g):
                until(pe, qkl_done, b, 2 * g + 2)
                for p in range(4 * g, 4 * g + 4):
                    for i in range(2):
                        n = 2 * p + i
                        if n < 2:
                            until(pe, v_done, b, n + 1)
                        elif n >= 4 and not (g == 1 and p == 4):
                            until(pe, (qsel_done, ksel_done)[i], b, p - 1)
                        h, l = (("sel_qh", "sel_ql"), ("sel_kh", "sel_kl"))[i]
                        mm(select_bank[n % 4][:, :], sel[h][:, p % 4, :], qk_h[:, i, :], start=True, stop=False)
                        mm(select_bank[n % 4][:, :], sel[l][:, p % 4, :], qk_l[:, i, :], start=False, stop=True)\
                            .then_inc(sel_ready, 1)

            def scores(b, h, c):
                if h == 0:
                    until(pe, qsel_done, b, NPAIR)
                    until(pe, ksel_done, b, NPAIR)
                elif h == 1:
                    if c is not None:
                        until(pe, x2_done, c, 2)
                else:
                    until(pe, max_done, b, h - 1)
                p = h // 2
                for t in range(NT):
                    bank = score_bank[2 * (h % 2) + t // 2]
                    c0 = 2 * P * (t % 2)
                    lo = P if t == 0 else 0
                    last = mm(bank[:, c0 + lo:c0 + 2 * P], q_pad[:, p, h % 2, P * t:P * t + P],
                              k_stack[:, p, P * (t - 1) + lo:P * (t + 1)], start=True, stop=True)
                last.then_inc(s_ready, 1)

            def n2_transposes(c):
                until(pe, n2_ready, c, 1)
                transpose_rows(normed, n2T_ready)

            def up(c, m):
                if m == 0:
                    until(pe, n2Tl_done, c, KD)
                elif m >= 2:
                    until(pe, gelu_done, c, m - 1)
                w = slice(P * m, P * m + P)
                split_product(ffn_bank[m % 2][:, :], [
                    (w1_h[:, k, w], w1_l[:, k, w], cn_h[:, k, :], cn_l[:, k, :]) for k in range(KD)
                ]).then_inc(up_ready, 1)

            def max_transposes(b, half):
                until(pe, parts_done, b, half + 1)
                for t in range(NT):
                    last = nc.tensor.transpose(
                        mix_bank[half][0:16, P * t:P * t + P],
                        max_parts[:, t, half, :, :, :].rearrange("p a b c -> p (a b c)"), ident[:, :])
                last.then_inc(maxT_ready, 1)

            def down(c, t):
                if t == 0:
                    until(pe, gelu_done, c, NM)
                for m in range(NM):
                    last = mm(ffn_bank[t // 2][:, D * (t % 2):D * (t % 2) + D], hidden[:, m, P * t:P * t + P],
                              w2[:, m, :], start=m == 0, stop=m == NM - 1)
                if t % 2:
                    last.then_inc(down_ready, 1)

            def scores_T(b, p):
                if p % 4 == 0:
                    until(pe, max_rows[p // 4], b, 64)
                for kc in range(NT):
                    if p == 0:
                        until(pe, max_done, b, NH - 1 + kc // 2)
                    else:
                        until(pe, exp_done, b, NT * (p - 1) + kc + 1)
                    q1 = min(P * (kc + 2), L)
                    n = q1 - P * kc
                    mm(score_bank[kc][:, 0:2 * n].rearrange("p (h q) -> p h q", h=2),
                       k_stack[:, p, P * kc:P * kc + P], q_pad[:, p, :, P * kc:q1],
                       start=True, stop=True).then_inc(sT_ready, 1)

            def context(b, g):
                until(pe, probs_ready, b, 2 * g + 2)
                if g < 2:
                    until(pe, maxT_done, b, g + 1)
                else:
                    until(pe, ctx_saved, b, g - 1)
                for kc in range(NT):
                    n = 2 * P if kc < NT - 1 else P
                    for j in range(4):
                        slot = 2 * (g % 2) + j // 2
                        r0 = 4 * P * kc + n * (j % 2)
                        last = mm(mix_bank[g % 2][32 * j:32 * j + 32, P * kc:P * kc + n],
                                  v_ones[:, kc, VW * (4 * g + j):VW * (4 * g + j) + 32],
                                  probs[:, slot, r0:r0 + n], start=kc == 0, stop=kc == NT - 1,
                                  skip_group_check=True)
                last.then_inc(ctx_ready, 1)

            def iteration(b, c):
                if b is not None:
                    input_transposes(b)
                if c is not None:
                    context_to_rows(c)
                if b is not None:
                    project_qk(b, 0)
                if c is not None:
                    context_transposes(c)
                if b is not None:
                    project_v(b)
                    stacks(b, 0)
                if c is not None:
                    project_out(c)
                if b is not None:
                    project_qk(b, 1)
                    stacks(b, 1)
                    scores(b, 0, c)
                    scores(b, 1, c)
                if c is not None:
                    n2_transposes(c)
                for m in range(NM):
                    if b is not None and m < NM - 1:
                        scores(b, 2 * m + 2, c)
                        scores(b, 2 * m + 3, c)
                    if b is not None and m == 3:
                        max_transposes(b, 0)
                    if c is not None:
                        up(c, m)
                if c is not None:
                    down(c, 0)
                if b is not None:
                    max_transposes(b, 1)
                    for p in range(NPAIR):
                        scores_T(b, p)
                        if c is not None and p in (0, 2, 4):
                            down(c, p // 2 + 1)
                        if p >= 3 and p % 2:
                            context(b, (p - 3) // 2)
                    context(b, 3)
                elif c is not None:
                    for t in range(1, NT):
                        down(c, t)

            iteration(0, None)
            with pe.Fori(1, NB - 1) as b:
                iteration(b, b - 1)
            iteration(NB - 1, NB - 2)
            iteration(None, NB - 1)

            pe.wait_ge(p2_raw, 48)
            for e in range(NE):
                if e >= 4:
                    pe.wait_ge(p2_weights, e - 3)
                for k in range(KD):
                    for o in range(KD):
                        last = nc.tensor.transpose(score_bank[e % 4][:, D * k + P * o:D * k + P * o + P],
                                                   we_raw[:, e, o, P * k:P * k + P], ident[:, :])
                last.then_inc(p2_tr, 1)
            pe.wait_ge(p2_weights, NE)

            def unit_transposes(m, i):
                if not (isinstance(m, int) and m == 0):
                    pe.wait_ge(p2_nTl, m * KD)
                pe.wait_ge(p2_norm, m + 1)
                transpose_rows(unit_normed[i % 2], p2_nT)

            def unit_products(n, i):
                pe.wait_ge(p2_nTl, n * KD + KD)
                hi, lo = p2_T[i % 2]
                e = pe.value_load(unit_expert[0:1, bass.ds(n, 1)], min_val=0, max_val=NE - 1)
                for j in range(RUN):
                    dst = p2_banks[i % 2][j // 2][:, D * (j % 2):D * (j % 2) + D]
                    c = slice(P * j, P * j + P)
                    terms = [(a[:, k, c], w[:, bass.ds(e, 1), k, :]) for a, w in ((hi, we_h), (lo, we_h), (hi, we_l))
                             for k in range(KD)]
                    terms.append((all_ones[:, :], bias_of[:, bass.ds(e, 1), :]))
                    for t, (lhsT, rhs) in enumerate(terms):
                        last = mm(dst, lhsT, rhs, start=t == 0, stop=t == len(terms) - 1)
                    if j % 2:
                        last.then_inc(p2_y, 1)

            unit_transposes(0, 0)
            with pe.Fori(0, NUNIT, DEPTH) as n0:
                for i in range(DEPTH):
                    unit_transposes(n0 + (i + 1), i + 1)
                    unit_products(n0 + i, i)


_INS = ["L0_attn_x", "L0_attn_Wq", "L0_attn_bq", "L0_attn_Wk", "L0_attn_bk", "L0_attn_Wv", "L0_attn_bv",
        "L0_attn_Wo", "L0_attn_bo", "L0_attn_W1", "L0_attn_b1", "L0_attn_W2", "L0_attn_b2",
        "L0_attn_ln1_w", "L0_attn_ln1_b", "L0_attn_ln2_w", "L0_attn_ln2_b",
        "L0_ffn_tile_sigs", "L0_ffn_W", "L0_ffn_b"]


def kernel(**inputs):
    import concourse.bacc as bacc
    from concourse.bass_utils import run_bass_kernel_spmd

    nc = bacc.Bacc("TRN2", target_bir_lowering=False, num_devices=1, dynamic_dma_scratch_size=8192)
    arrays, args = {}, []
    for name in _INS:
        a = np.ascontiguousarray(inputs[name])
        arrays[f"in_{name}"] = a
        args.append(nc.dram_tensor(f"in_{name}", a.shape, mybir.dt.from_np(a.dtype), kind="ExternalInput").ap())
    consts, at = shape_constants()
    arrays["shape_constants"] = consts
    cst = nc.dram_tensor("shape_constants", consts.shape, F32, kind="ExternalInput").ap()
    scratch = nc.dram_tensor("attended", (L, NB * D), F32, kind="Internal").ap()
    out = nc.dram_tensor("out_rows", (NB * L, D), F32, kind="ExternalOutput").ap()
    build(nc, *args, cst, at, scratch, out)
    r = run_bass_kernel_spmd(nc, [arrays], core_ids=[0])
    return r.results[0]["out_rows"].reshape(NB, L, D)
```

```python
from contextlib import ExitStack
import math

import numpy as np

import concourse.bass as bass
from concourse import mybir

F32 = mybir.dt.float32
F32R = mybir.dt.float32r
I32 = mybir.dt.int32
U32 = mybir.dt.uint32
ALU = mybir.AluOpType
ACT = mybir.ActivationFunctionType
AX_X = mybir.AxisListType.X

P = 128
NB, L, D = 32, 512, 256
NT = L // P
KD = D // P
NH, HD = 16, 16
NPAIR = NH // 2
DFF = 1024
NM = DFF // P
NE, DPOS = 8, 32
WINDOW = 128
EPS = 1e-5
SCALE = 1.0 / math.sqrt(HD)
MASKED = -3.0e38
LOWEST = float(np.finfo(np.float32).min)
VW = HD + 1

MAX_AT = 6
SCORES_AT = ((0, 0), (0, 1), (0, 2), (0, 3), (1, 0))
STATS_AT = 5
DOWN_AT = (0, 0, 1, 2, 2, 4, 6, 7)
ACT_K = (4,)

SLOTS = 16
QUADS = P // SLOTS
RUN = NB // QUADS
assert RUN == NT
DEPTH = 8
AHEAD = 4
NUNIT = -(-((L + NE * (SLOTS - 1)) // SLOTS) // DEPTH) * DEPTH
NCOL = NUNIT + 2 * DEPTH
EMPTY = float(1 << 20)

Q_STACK = ("hi", "lo", "hi")
K_STACK = ("hi", "hi", "lo")
MAX_ROW = 3 * HD


def shape_constants():
    r = np.arange(P)
    parts = {}
    parts["ident"] = np.eye(P)
    q, k = r[:, None], r[None, :]
    parts["mask"] = np.concatenate([np.where(k >= q, 0.0, MASKED), np.where(k <= q, 0.0, MASKED)], 1)
    for name, stack, part in (("sel_qh", Q_STACK, "hi"), ("sel_ql", Q_STACK, "lo"),
                              ("sel_kh", K_STACK, "hi"), ("sel_kl", K_STACK, "lo")):
        m = np.zeros((P, NPAIR // KD, P))
        for p in range(NPAIR // KD):
            for par in range(2):
                for c in range(3):
                    if stack[c] == part:
                        for d in range(HD):
                            m[2 * HD * p + HD * par + d, p, 64 * par + HD * c + d] = 1.0
        parts[name] = m.reshape(P, -1)
    kcol = np.zeros((P, 1))
    for par in range(2):
        kcol[64 * par + MAX_ROW:64 * par + MAX_ROW + 2] = -1.0
    parts["minus_one_rows"] = kcol
    parts["before"] = (q < k).astype(np.float32)
    parts["ones"] = np.ones((P, P))
    parts["unit_iota"] = np.broadcast_to(np.arange(NCOL), (P, NCOL))
    parts["slot_of_row"] = np.broadcast_to(r // QUADS, (P, P))
    parts["first_run"] = (r % QUADS - QUADS)[:, None]
    parts["first_row"] = (L * RUN * (r % QUADS))[:, None] + L * np.arange(RUN)[None, :] - 1
    parts["position_plus_1"] = r[:, None] + P * np.arange(NT)[None, :] + 1
    parts["expert_rank"] = np.broadcast_to(NE - np.arange(NE), (P, NT, NE)).reshape(P, -1)
    pos = np.arange(L, dtype=np.float32)[:, None]
    div = np.exp((np.arange(0, DPOS, 2, dtype=np.float32) *
                  np.float32(-math.log(10000.0) / DPOS)).astype(np.float64)).astype(np.float32)
    ang = pos * div
    code = np.zeros((L, DPOS), np.float32)
    code[:, 0::2], code[:, 1::2] = np.sin(ang), np.cos(ang)
    codeT = np.zeros((P, L))
    codeT[:DPOS] = code.T
    parts["position_code"] = codeT
    at, cols = {}, 0
    for name, a in parts.items():
        at[name] = (cols, cols + a.shape[1])
        cols += a.shape[1]
    return np.ascontiguousarray(np.concatenate(list(parts.values()), 1).astype(np.float32)), at


def build(nc, x, Wq, bq, Wk, bk, Wv, bv, Wo, bo, W1, b1, W2, b2, ln1_w, ln1_b, ln2_w, ln2_b,
          sigs, We, be, consts, at, scratch, out):
    ctx = ExitStack()
    with ctx:
        def sb(name, shape, dt=F32):
            return ctx.enter_context(nc.sbuf_tensor(name, shape, dt))

        def sem(name):
            return ctx.enter_context(nc.semaphore(name))

        score_bank = [ctx.enter_context(nc.psum_tensor(f"score_bank{i}", [P, 512], F32)) for i in range(4)]
        ffn_bank = [ctx.enter_context(nc.psum_tensor(f"ffn_bank{i}", [P, 512], F32)) for i in range(2)]
        mix_bank = [ctx.enter_context(nc.psum_tensor(f"mix_bank{i}", [P, 512], F32)) for i in range(2)]
        input_bank = score_bank[0:2]
        select_bank = [score_bank[0:2] + ffn_bank, ffn_bank + score_bank[2:4]]

        ident = sb("ident", [P, P])
        mask = sb("mask", [P, 2 * P])
        sel = {n: sb(n, [P, NPAIR // KD, P], F32R) for n in ("sel_qh", "sel_ql", "sel_kh", "sel_kl")}
        minus_one_rows = sb("minus_one_rows", [P, 1])
        wqkv_h = sb("wqkv_h", [P, KD, 3 * D], F32R)
        wqkv_l = sb("wqkv_l", [P, KD, 3 * D], F32R)
        wo_h = sb("wo_h", [P, KD, D], F32R)
        wo_l = sb("wo_l", [P, KD, D], F32R)
        w1_h = sb("w1_h", [P, KD, DFF], F32R)
        w1_l = sb("w1_l", [P, KD, DFF], F32R)
        w2 = sb("w2", [P, NM, D])
        qkv_bias = sb("qkv_bias", [P, 6])
        b1_col = sb("b1_col", [P, NM])
        ln_col = sb("ln_col", [P, 4, KD])
        bo_row = sb("bo_row", [P, D])
        b2_row = sb("b2_row", [P, D])
        minus_half = sb("minus_half", [P, 2, NT])

        x_in = sb("x_in", [P, NT, D])
        normed = sb("normed", [P, NT, D])
        x1 = sb("x1", [P, NT, D])
        x_b2 = sb("x_b2", [P, NT, D])
        x2 = sb("x2", [P, NT, D])
        y = sb("y", [P, NT, D])
        ctxn = normed
        nT_h = sb("nT_h", [P, KD, L], F32R)
        nT_l = sb("nT_l", [P, KD, L], F32R)
        qk_h = sb("qk_h", [P, 2, L], F32R)
        qk_l = sb("qk_l", [P, 2, L], F32R)
        q_pad = sb("q_pad", [P, NPAIR, 2, L], F32R)
        k_stack = sb("k_stack", [P, NPAIR, L], F32R)
        v_ones = sb("v_ones", [P, NT, NH * VW + HD])
        probs = sb("probs", [P, 4, 7 * 2 * P])
        ctxT = sb("ctxT", [P, 4, L])
        cn_h = sb("cn_h", [P, KD, L], F32R)
        cn_l = sb("cn_l", [P, KD, L], F32R)
        hidden = sb("hidden", [P, NM, L])
        maxT = sb("maxT", [16, L])
        row_max = sb("row_max", [P, NT, NH])
        max_parts = sb("max_parts", [P, NT, 2, 2, 2, 4])
        max_hi = sb("max_hi", [P, NT, 2, 2, 4], F32R)
        inv_sum = sb("inv_sum", [P, NT, NH])
        stats1 = sb("stats1", [P, NT, 6])
        mv1 = sb("mv1", [P, NT, 2])
        stats2 = sb("stats2", [P, NT, 6])
        mv2 = sb("mv2", [P, NT, 2])
        var1 = sb("var1", [P, 2, NT])
        scale1 = sb("scale1", [P, 2, NT])
        minus_mean1 = sb("minus_mean1", [P, NT])
        minus_mean2 = sb("minus_mean2", [P, NT])
        var2 = sb("var2", [P, NT])
        scale2 = sb("scale2", [P, NT])
        row_index = sb("row_index", [P, NCOL, 1 + RUN], I32)
        gather_rows = sb("gather_rows", [P, DEPTH], I32)
        scatter_rows = sb("scatter_rows", [P, 2, RUN], I32)
        unit_expert = sb("unit_expert", [P, NCOL], I32)
        unit_scale = sb("unit_scale", [P, 2, NT])
        unit_std = sb("unit_std", [P, 2, NT])
        eps_col = sb("eps_col", [P, 1])
        unit_shift = sb("unit_shift", [P, 2, NT])
        assert NH * VW + HD >= (NH - 1) * VW + 32

        staged = probs[:, :, :].rearrange("p a b -> p (a b)")
        stage2 = hidden[:, :, :].rearrange("p a b -> p (a b)")
        wqkv_raw = staged[:, 0:KD * 3 * D].rearrange("p (k n) -> p k n", k=KD)
        wo_raw = staged[:, 1536:1536 + KD * D].rearrange("p (k n) -> p k n", k=KD)
        w1_raw = staged[:, 2048:2048 + KD * DFF].rearrange("p (k n) -> p k n", k=KD)
        route = staged[:, 4096:4096 + 1024]
        ncst = consts.shape[1]
        cst = stage2[:, 0:ncst]
        assert ncst <= NM * L

        def const(name):
            return cst[:, at[name][0]:at[name][1]]

        LEAD = 1
        loaded = sem("loaded")
        dve_step = sem("dve_step")
        pool_step = sem("pool_step")
        setup_mm = sem("setup_mm")
        setup_dve = sem("setup_dve")
        ready = sem("ready")
        PER = {}

        def counted(name, n):
            s = sem(name)
            PER[id(s)] = n
            return s

        x_loaded = counted("x_loaded", 16)
        x_used = counted("x_used", 1)
        mv1_ready = counted("mv1_ready", 1)
        n1_ready = counted("n1_ready", 1)
        x1_ready = counted("x1_ready", 1)
        nT_ready = counted("nT_ready", KD)
        nTh_done = counted("nTh_done", KD)
        nTl_done = counted("nTl_done", KD)
        qk_ready = counted("qk_ready", 4)
        qkh_done = counted("qkh_done", 4)
        qkl_done = counted("qkl_done", 4)
        v_ready = counted("v_ready", 2)
        v_done = counted("v_done", 2)
        sel_ready = counted("sel_ready", 2 * NPAIR)
        qsel_done = counted("qsel_done", NPAIR)
        ksel_done = counted("ksel_done", NPAIR - len(ACT_K))
        ksel_by_act = counted("ksel_by_act", len(ACT_K))
        s_ready = counted("s_ready", NH)
        max_done = counted("max_done", NH)
        parts_done = counted("parts_done", 2)
        maxT_ready = counted("maxT_ready", 2)
        maxT_done = counted("maxT_done", 2)
        max_rows = [counted(f"max_rows{i}", 64) for i in range(2)]
        sT_ready = counted("sT_ready", NPAIR * NT)
        exp_done = counted("exp_done", NPAIR * NT)
        probs_ready = counted("probs_ready", NPAIR)
        ctx_ready = counted("ctx_ready", 4)
        ctx_saved = counted("ctx_saved", 4)
        ctxq_ready = counted("ctxq_ready", NT)
        ctxn_done = counted("ctxn_done", NT)
        cT_ready = counted("cT_ready", KD)
        cTh_done = counted("cTh_done", KD)
        cTl_done = counted("cTl_done", KD)
        attn_ready = counted("attn_ready", 2)
        x2_done = counted("x2_done", 2)
        mv2_ready = counted("mv2_ready", 1)
        n2_ready = counted("n2_ready", NT)
        residual_ready = counted("residual_ready", 1)
        n2T_ready = counted("n2T_ready", KD)
        n2Th_done = counted("n2Th_done", KD)
        n2Tl_done = counted("n2Tl_done", KD)
        up_ready = counted("up_ready", NM)
        gelu_done = counted("gelu_done", NM)
        down_ready = counted("down_ready", 2)
        y_done = counted("y_done", 2)
        y_stored = counted("y_stored", 16)
        y_free = sem("y_free")
        inv_step = counted("inv_step", NT)
        bn2_step = counted("bn2_step", NT)
        bn1_step = counted("bn1_step", NT)
        maxhi_step = counted("maxhi_step", 4)
        scale1_step = counted("scale1_step", 1)
        scale2_step = counted("scale2_step", 1)
        aggr1_step = counted("aggr1_step", 1)
        aggr2_step = counted("aggr2_step", 1)
        sign_done = sem("sign_done")

        def until(eng, s, b, k):
            eng.wait_ge(s, b * PER[id(s)] + k)

        passed = {"DVE": sem("passed_by_dve"), "Pool": sem("passed_by_pool")}

        def apart(eng, name):
            eng.sem_inc(passed[name], 1)

        p2_zeroed = sem("p2_zeroed")
        p2_raw = sem("p2_raw")
        p2_tr = sem("p2_tr")
        p2_hi = sem("p2_hi")
        p2_bias = sem("p2_bias")
        p2_weights = sem("p2_weights")
        p2_gather_rows = sem("p2_gather_rows")
        p2_gather = [sem(f"p2_gather{i}") for i in range(DEPTH)]
        p2_bn = sem("p2_bn")
        p2_mv = sem("p2_mv")
        p2_std = sem("p2_std")
        p2_rstd = sem("p2_rstd")
        p2_scale = sem("p2_scale")
        p2_norm = sem("p2_norm")
        p2_nT = sem("p2_nT")
        p2_nTh = sem("p2_nTh")
        p2_nTl = sem("p2_nTl")
        p2_y = sem("p2_y")
        p2_scatter_rows = sem("p2_scatter_rows")
        p2_out = sem("p2_out")
        p2_scatter = [sem(f"p2_scatter{i}") for i in range(2)]

        HL = NE * KD * D
        we_raw = staged[:, 0:HL].rearrange("p (e o d) -> p e o d", e=NE, o=KD)
        pads = q_pad[:, :, :, :].rearrange("p a b c -> p (a b c)")
        we_h = pads[:, 0:HL].rearrange("p (e k o) -> p e k o", e=NE, k=KD)
        we_l = pads[:, HL:2 * HL].rearrange("p (e k o) -> p e k o", e=NE, k=KD)
        bias_parts = k_stack[:, :, :].rearrange("p a b -> p (a b)")[:, 0:NE * D]
        bias_of = bias_parts.rearrange("p (e o) -> p e o", e=NE)
        bias_raw = staged[:, HL:HL + NE * D]
        BIAS_LO = 32
        all_ones = sb("all_ones", [P, P], F32R)
        rows_in = [(stage2, staged)[i // AHEAD][:, RUN * D * (i % AHEAD):RUN * D * (i % AHEAD + 1)]
                   .rearrange("p (j d) -> p j d", j=RUN) for i in range(DEPTH)]
        rows_out = [y, x2]
        unit_normed = [normed, x1]
        p2_banks = [ffn_bank, score_bank[0:2]]
        p2_T = [(nT_h, nT_l), (cn_h, cn_l)]

        b_wide = route[:, 16:16 + KD * P].rearrange("p (k n) -> p k n", k=KD)
        at_small = 16 + KD * P
        r_score, r_cand, r_onehot = (route[:, at_small + i:at_small + i + NT * NE]
                                     .rearrange("p (c e) -> p c e", e=NE) for i in (0, 32, 64))
        r_small = route[:, at_small + 96:at_small + 108].rearrange("p (a c) -> p a c", c=NT)
        r_groups = route[:, at_small + 108:at_small + 116]
        r_start = route[:, at_small + 116:at_small + 124]
        r_gexp = route[:, at_small + 124:at_small + 124 + NCOL]
        r_tmp = route[:, at_small + 272:at_small + 272 + NCOL]
        assert NCOL <= 128
        r_int = sb("r_int", [P, 8], I32)
        r_row = staged[:, 5120:5120 + NT * P].rearrange("p (c n) -> p c n", c=NT)
        r_group = staged[:, 5632:5632 + NT * NCOL].rearrange("p (c n) -> p c n", c=NT)

        def col(v, n):
            return v.rearrange("(m p) -> p m", p=P)

        NLOAD = 19
        x_rows = x.rearrange("b (t p) d -> b p t d", p=P)
        y_rows = scratch.rearrange("(t p) (b d) -> b p t d", t=NT, b=NB)
        scratch_runs = scratch.rearrange("l (q r) -> (l q) r", q=QUADS)

        block = ctx.enter_context(nc.Block())

        @block.sync
        def _(sp):
            sp.dma_start(x_in[:, :, :], x_rows[0]).then_inc(x_loaded, 16)
            sp.dma_start(cst, consts).then_inc(loaded, 16)
            sp.dma_start(wqkv_raw[:, :, 0:D], Wq.rearrange("(k p) n -> p k n", p=P)).then_inc(loaded, 16)
            sp.dma_start(wqkv_raw[:, :, D:2 * D], Wk.rearrange("(k p) n -> p k n", p=P)).then_inc(loaded, 16)
            sp.dma_start(wqkv_raw[:, :, 2 * D:], Wv.rearrange("(k p) n -> p k n", p=P)).then_inc(loaded, 16)
            sp.dma_start(wo_raw, Wo.rearrange("(k p) n -> p k n", p=P)).then_inc(loaded, 16)
            sp.dma_start(w1_raw, W1.rearrange("(k p) n -> p k n", p=P)).then_inc(loaded, 16)
            sp.dma_start(w2[:, :, :], W2.rearrange("(k p) n -> p k n", p=P)).then_inc(loaded, 16)
            sp.dma_start(qkv_bias[:, 0:2], col(bq, 2), allow_slow_non_contiguous=True).then_inc(loaded, 16)
            sp.dma_start(qkv_bias[:, 2:4], col(bk, 2), allow_slow_non_contiguous=True).then_inc(loaded, 16)
            sp.dma_start(qkv_bias[:, 4:6], col(bv, 2), allow_slow_non_contiguous=True).then_inc(loaded, 16)
            sp.dma_start(b1_col[:, :], col(b1, NM), allow_slow_non_contiguous=True).then_inc(loaded, 16)
            for i, v in enumerate((ln1_w, ln1_b, ln2_w, ln2_b)):
                sp.dma_start(ln_col[:, i, :], col(v, KD), allow_slow_non_contiguous=True).then_inc(loaded, 16)
            for row, v in ((bo_row, bo), (b2_row, b2)):
                sp.dma_start(row[:, :], v.partition_broadcast(P)).then_inc(loaded, 16)
            sp.dma_start(route[0:DPOS, 0:NE], sigs.rearrange("t p -> p t"), allow_slow_non_contiguous=True).then_inc(loaded, 16)
            sp.dma_start(ident[:, :], consts[:, at["ident"][0]:at["ident"][1]]).then_inc(loaded, 16)

            def attention(b, ahead):
                if ahead:
                    until(sp, x_used, b, 1)
                    sp.dma_start(x_in[:, :, :], x_rows[b + 1]).then_inc(x_loaded, 16)
                for half in range(2):
                    until(sp, maxT_done, b, half + 1)
                    for par in range(2):
                        for part in range(2):
                            row = 64 * par + MAX_ROW + part
                            src = 8 * par + 4 * part
                            sp.dma_start(
                                q_pad[row:row + 1, 4 * half:4 * half + 4, par, :].bitcast(F32),
                                maxT[src:src + 4, :],
                            ).then_inc(max_rows[half], 16)

            def finish(c):
                until(sp, y_done, c, 2)
                sp.dma_start(y_rows[c], y[:, :, :]).then_inc(y_stored, 16)
                until(sp, y_stored, c, 16)
                sp.sem_inc(y_free, 1)

            sp.sem_inc(y_free, LEAD)
            attention(0, True)
            with sp.Fori(1, NB - 1) as b:
                attention(b, True)
                finish(b - 1)
            attention(NB - 1, False)
            finish(NB - 2)

            until(sp, ctx_ready, NB - 1, 4)
            sp.dma_start(staged[:, 0:HL].rearrange("p (e o d) -> p e o d", e=NE, o=KD),
                         We.rearrange("e (o p) d -> p e o d", p=P)).then_inc(p2_raw, 16)
            for part in (0, BIAS_LO):
                sp.dma_start(bias_raw[part:part + 1, :], be.rearrange("(a e) o -> a (e o)", a=1)).then_inc(p2_raw, 16)

            finish(NB - 1)

        @block.gpsimd
        def _(pool):
            nc.gpsimd.memset(v_ones[:, :, :], 0.0).then_inc(pool_step, 1)
            nc.gpsimd.memset(minus_half[:, :, :], -0.5).then_inc(pool_step, 1)
            nc.gpsimd.memset(eps_col[:, :], EPS).then_inc(pool_step, 1)
            nc.gpsimd.memset(all_ones[:, :].bitcast(F32), 1.0).then_inc(pool_step, 1)
            nc.gpsimd.memset(q_pad[:, :, :, :].bitcast(F32), 0.0).then_inc(pool_step, 1)
            pool.wait_ge(pool_step, 1)
            nc.gpsimd.memset(v_ones[:, :, 0:NH * VW].rearrange("p t (h w) -> p t h w", w=VW)[:, :, :, 0:1],
                             1.0).then_inc(pool_step, 1)
            pool.wait_ge(pool_step, 6)
            nc.gpsimd.memset(scale2[:, :], 0.0).then_inc(ready, 1)

            def norm1(b):
                until(pool, mv1_ready, b, 1)
                apart(pool, "Pool")
                nc.gpsimd.tensor_tensor(scale1[:, :, :], var1[:, :, :], minus_half[:, :, :], ALU.pow)\
                    .then_inc(scale1_step, 1)
                if isinstance(b, int) and b < 2:
                    if b == 1:
                        until(pool, nT_ready, 0, KD)
                else:
                    until(pool, n2T_ready, b - 2, KD)
                    apart(pool, "Pool")
                until(pool, scale1_step, b, 1)
                apart(pool, "Pool")
                for t in range(NT):
                    last = nc.gpsimd.tensor_scalar(normed[:, t, :], x_in[:, t, :], minus_mean1[:, t:t + 1],
                                                   scale1[:, 1, t:t + 1], ALU.add, ALU.mult)
                last.then_inc(n1_ready, 1)

            def norm2(c):
                until(pool, mv2_ready, c, 1)
                apart(pool, "Pool")
                nc.gpsimd.tensor_tensor(scale2[:, :], var2[:, :], minus_half[:, 0, :], ALU.pow)\
                    .then_inc(scale2_step, 1)
                until(pool, scale2_step, c, 1)
                apart(pool, "Pool")
                for t in range(NT):
                    nc.gpsimd.tensor_scalar(normed[:, t, :], x2[:, t, :], minus_mean2[:, t:t + 1], scale2[:, t:t + 1],
                                            ALU.add, ALU.mult).then_inc(n2_ready, 1)

            def residual2(c):
                until(pool, n2_ready, c, NT)
                apart(pool, "Pool")
                nc.gpsimd.tensor_tensor(x2[:, :, :], x2[:, :, :], x_b2[:, :, :], ALU.add).then_inc(residual_ready, 1)

            def residuals(b):
                if not (isinstance(b, int) and b == 0):
                    until(pool, residual_ready, b - 1, 1)
                    apart(pool, "Pool")
                for t in range(NT):
                    nc.gpsimd.tensor_tensor(x_b2[:, t, :], x_in[:, t, :], b2_row[:, :], ALU.add)
                for t in range(NT):
                    last = nc.gpsimd.tensor_scalar(x1[:, t, :], x_in[:, t, :], minus_mean1[:, t:t + 1],
                                                   scale1[:, 0, t:t + 1], ALU.add, ALU.mult)
                last.then_inc(x_used, 1)
                until(pool, x_used, b, 1)
                apart(pool, "Pool")
                for t in range(NT):
                    last = nc.gpsimd.tensor_tensor(x1[:, t, :], x1[:, t, :], bo_row[:, :], ALU.add)
                last.then_inc(x1_ready, 1)

            def masks(b):
                for p in range(NPAIR):
                    until(pool, exp_done, b, NT * (p + 1))
                    apart(pool, "Pool")
                    blocks = probs[:, p % 4, 0:12 * P].rearrange("p (a h q) -> p a h q", h=2, q=P)
                    same, after = blocks[:, :, 0, :], blocks[:, :, 1, :]
                    last = probs[:, p % 4, 12 * P:14 * P].rearrange("p (a q) -> p a q", q=P)
                    for part, n, sign in ((same, 6, 1), (last, 2, 1), (after, 6, -1)):
                        done = nc.gpsimd.affine_select(
                            out=part, in_=part, compare_op=ALU.is_ge, fill=0.0,
                            base=0 if sign == 1 else WINDOW - P, pattern=[[0, n], [sign, P]],
                            channel_multiplier=-sign)
                    done.then_inc(probs_ready, 1)

            pool.wait_ge(pool_step, 6)
            norm1(0)
            pool.wait_ge(ready, 2)
            residuals(0)
            norm1(1)
            masks(0)
            with pool.Fori(1, NB - 1) as b:
                norm2(b - 1)
                residual2(b - 1)
                residuals(b)
                norm1(b + 1)
                masks(b)
            norm2(NB - 2)
            residual2(NB - 2)
            residuals(NB - 1)
            masks(NB - 1)
            nc.gpsimd.memset(bias_parts.bitcast(F32), 0.0).then_inc(p2_zeroed, 1)
            norm2(NB - 1)
            residual2(NB - 1)


            def gather(m, i):
                pool.wait_ge(p2_gather_rows, m + 1)
                apart(pool, "Pool")
                nc.gpsimd.indirect_dma_start(
                    rows_in[i].rearrange("p j d -> p (j d)"), None, scratch_runs,
                    bass.IndirectOffsetOnAxis(ap=gather_rows[:, i:i + 1].bitcast(U32), axis=0),
                    bounds_check=L * QUADS - 1, oob_is_err=False).then_inc(p2_gather[i], 16)

            def scatter(n, i):
                pool.wait_ge(p2_scatter_rows, n + 1)
                apart(pool, "Pool")
                pool.wait_ge(p2_out, 2 * n + 2)
                apart(pool, "Pool")
                for j in range(RUN):
                    nc.gpsimd.indirect_dma_start(
                        out, bass.IndirectOffsetOnAxis(ap=scatter_rows[:, i % 2, j:j + 1].bitcast(U32), axis=0),
                        rows_out[i % 2][:, j, :], None,
                        bounds_check=NB * L - 1, oob_is_err=False).then_inc(p2_scatter[i % 2], 16)

            until(pool, y_stored, NB - 1, 16)
            for m in range(AHEAD):
                gather(m, m)
            pool.wait_ge(p2_tr, NE)
            apart(pool, "Pool")
            with pool.Fori(0, NUNIT, DEPTH) as n0:
                for i in range(DEPTH):
                    gather(n0 + (i + AHEAD), (i + AHEAD) % DEPTH)
                    scatter(n0 + i, i)
            for i in range(2):
                pool.wait_ge(p2_scatter[i], 16 * RUN * (NUNIT // 2))
            for i in range(DEPTH):
                pool.wait_ge(p2_gather[i], 16 * (NUNIT // DEPTH + (1 if i < AHEAD else 0)))

        @block.scalar
        def _(act):
            act.wait_ge(loaded, 16 * NLOAD)
            nc.scalar.activation(route[0:DPOS, 8:16], route[0:DPOS, 0:NE], ACT.Sign).then_inc(sign_done, 1)
            act.wait_ge(ready, 2)

            def round_banks(c, ready_sem, banks, dst, done_sem):
                for k in range(KD):
                    until(act, ready_sem, c, k + 1)
                    nc.scalar.activation(dst[:, k, :], banks[k][:, :], ACT.Copy).then_inc(done_sem, 1)

            def qk_hi(b, g):
                for i in range(2):
                    until(act, qk_ready, b, 2 * g + i + 1)
                    nc.scalar.activation(qk_h[:, i, :], ffn_bank[i][:, :], ACT.Identity,
                                         bias=qkv_bias[:, 2 * i + g:2 * i + g + 1]).then_inc(qkh_done, 1)

            def values(b):
                for u in range(2):
                    until(act, v_ready, b, u + 1)
                    dst = v_ones[:, 2 * u:2 * u + 2, 0:NH * VW].rearrange("p t (h w) -> p t h w", w=VW)[:, :, :, 1:VW]
                    nc.scalar.activation(dst, ffn_bank[u][:, :].rearrange("p (t h d) -> p t h d", t=2, d=HD),
                                         ACT.Copy).then_inc(v_done, 1)

            def stacks_out(b, pairs):
                for p in pairs:
                    until(act, sel_ready, b, 2 * p + 1)
                    bank = select_bank[p // 4][(2 * p) % 4]
                    nc.scalar.activation(q_pad[0:64, p, 0, :], bank[0:64, :], ACT.Copy)
                    nc.scalar.activation(q_pad[64:P, p, 1, :], bank[64:P, :], ACT.Copy).then_inc(qsel_done, 1)
                    if p in ACT_K:
                        until(act, sel_ready, b, 2 * p + 2)
                        nc.scalar.activation(k_stack[:, p, :], select_bank[p // 4][(2 * p + 1) % 4][:, :], ACT.Identity,
                                             bias=minus_one_rows[:, 0:1]).then_inc(ksel_by_act, 1)

            def gelu(c, m):
                until(act, up_ready, c, m + 1)
                nc.scalar.activation(hidden[:, m, :], ffn_bank[m % 2][:, :], ACT.Gelu_apprx_tanh,
                                     bias=b1_col[:, m:m + 1]).then_inc(gelu_done, 1)

            def max_out(b, half):
                until(act, maxT_ready, b, half + 1)
                if half == 1:
                    until(act, max_rows[0], b, 64)
                nc.scalar.activation(maxT[:, :], mix_bank[half][0:16, :], ACT.Copy).then_inc(maxT_done, 1)

            def exps(b, p):
                for kc in range(NT):
                    until(act, sT_ready, b, NT * p + kc + 1)
                    if kc == 0 and p >= 4 and p % 2 == 0:
                        until(act, ctx_ready, b, p // 2 - 1)
                    n = 4 * P if kc < NT - 1 else 2 * P
                    nc.scalar.activation(probs[:, p % 4, 4 * P * kc:4 * P * kc + n], score_bank[kc][:, 0:n],
                                         ACT.Exp, scale=SCALE).then_inc(exp_done, 1)

            def weights_hi():
                for i in range(NE):
                    act.wait_ge(p2_tr, i + 1)
                    dst = we_h.rearrange("p e k o -> p (e k o)")[:, 512 * i:512 * i + 512]
                    nc.scalar.activation(dst, score_bank[i % 4][:, :], ACT.Copy).then_inc(p2_hi, 1)

            def iteration(b, c, ahead):
                if b is not None:
                    qk_hi(b, 0)
                    values(b)
                if c is not None:
                    round_banks(c, cT_ready, mix_bank, cn_h, cTh_done)
                if b is None:
                    weights_hi()
                if b is not None:
                    stacks_out(b, range(0, 4))
                    qk_hi(b, 1)
                if c is not None:
                    round_banks(c, n2T_ready, mix_bank, cn_h, n2Th_done)
                if b is not None:
                    stacks_out(b, range(4, NPAIR))
                for m in range(NM):
                    if c is not None:
                        gelu(c, m)
                    if b is not None and m == MAX_AT:
                        max_out(b, 0)
                if b is not None:
                    for p in range(NPAIR):
                        exps(b, p)
                        if p == 0:
                            max_out(b, 1)
                if ahead:
                    round_banks(b + 1, nT_ready, input_bank, nT_h, nTh_done)

            round_banks(0, nT_ready, input_bank, nT_h, nTh_done)
            iteration(0, None, True)
            with act.Fori(1, NB - 1) as b:
                iteration(b, b - 1, True)
            iteration(NB - 1, NB - 2, False)
            iteration(None, NB - 1, False)


            def unit_norm(m, i):
                act.wait_ge(p2_mv, m + 1)
                nc.scalar.activation(unit_std[:, i % 2, :], mv2[:, :, 1], ACT.Sqrt, bias=eps_col[:, :])\
                    .then_inc(p2_std, 1)
                act.wait_ge(p2_scale, m + 1)
                if not (isinstance(m, int) and m < 2):
                    act.wait_ge(p2_nT, (m - 1) * KD)
                for j in range(RUN):
                    last = nc.scalar.activation(unit_normed[i % 2][:, j, :], rows_in[i % DEPTH][:, j, :], ACT.Identity,
                                                bias=unit_shift[:, i % 2, j:j + 1], scale=unit_scale[:, i % 2, j:j + 1])
                last.then_inc(p2_norm, 1)

            def unit_hi(m, i):
                for k in range(KD):
                    act.wait_ge(p2_nT, m * KD + (k + 1))
                    nc.scalar.activation(p2_T[i % 2][0][:, k, :], mix_bank[k][:, :], ACT.Copy).then_inc(p2_nTh, 1)

            unit_norm(0, 0)
            unit_norm(1, 1)
            unit_hi(0, 0)
            with act.Fori(0, NUNIT, DEPTH) as n0:
                for i in range(DEPTH):
                    unit_hi(n0 + (i + 1), i + 1)
                    unit_norm(n0 + (i + 2), i + 2)

        @block.vector
        def _(dve):
            steps = [0]

            def link(ins):
                steps[0] += 1
                ins.then_inc(dve_step, 1)
                dve.wait_ge(dve_step, steps[0])

            def stats(b):
                until(dve, x_loaded, b, 16)
                for t in range(NT):
                    nc.vector.bn_stats(stats1[:, t, :], x_in[:, t, :]).then_inc(bn1_step, 1)
                for t in range(NT):
                    until(dve, bn1_step, b, t + 1)
                    apart(dve, "DVE")
                    last = nc.vector.bn_aggr(mv1[:, t, :], stats1[:, t, :])
                last.then_inc(aggr1_step, 1)
                until(dve, aggr1_step, b, 1)
                nc.vector.tensor_scalar(minus_mean1[:, :], mv1[:, :, 0], -1.0, None, ALU.mult)
                nc.vector.tensor_scalar(var1[:, 0, :], mv1[:, :, 1], EPS, None, ALU.add)
                nc.vector.tensor_scalar(var1[:, 1, :], mv1[:, :, 1], 1.0 + EPS, EPS * EPS, ALU.mult, ALU.add)\
                    .then_inc(mv1_ready, 1)

            stats(0)

            dve.wait_ge(loaded, 16 * NLOAD)
            for n in sel:
                nc.vector.tensor_copy(sel[n][:, :, :], const(n).rearrange("p (a b) -> p a b", b=P))
            nc.vector.tensor_copy(mask[:, :], const("mask"))
            nc.vector.tensor_copy(minus_one_rows[:, :], const("minus_one_rows"))
            for k in range(KD):
                nc.vector.tensor_scalar(wqkv_h[:, k, :], wqkv_raw[:, k, :], ln_col[:, 0, k:k + 1], None, ALU.mult)
                link(nc.vector.tensor_scalar(w1_h[:, k, :], w1_raw[:, k, :], ln_col[:, 2, k:k + 1], None, ALU.mult))
                nc.vector.scalar_tensor_tensor(wqkv_l[:, k, :], wqkv_raw[:, k, :], ln_col[:, 0, k:k + 1],
                                               wqkv_h[:, k, :].bitcast(F32), ALU.mult, ALU.subtract)
                link(nc.vector.scalar_tensor_tensor(w1_l[:, k, :], w1_raw[:, k, :], ln_col[:, 2, k:k + 1],
                                                    w1_h[:, k, :].bitcast(F32), ALU.mult, ALU.subtract))
            link(nc.vector.tensor_copy(wo_h[:, :, :], wo_raw))
            nc.vector.tensor_tensor(wo_l[:, :, :], wo_raw, wo_h[:, :, :].bitcast(F32), ALU.subtract)
            dve.wait_ge(setup_mm, 1)
            link(nc.vector.tensor_tensor(qkv_bias[:, :], score_bank[0][:, 0:6], qkv_bias[:, :], ALU.add))
            for k in range(KD):
                last = nc.vector.tensor_scalar(b_wide[:, k, :], const("ones"), qkv_bias[:, 4 + k:5 + k], None, ALU.mult)
            last.then_inc(setup_dve, 1)
            nc.vector.tensor_tensor(b1_col[:, :], score_bank[1][:, 0:NM], b1_col[:, :], ALU.add)

            def spread(a):
                return a.unsqueeze(2).broadcast_to([P, NT, NE])

            rank3 = const("expert_rank").rearrange("p (c e) -> p c e", e=NE)
            link(nc.vector.tensor_copy(r_score, score_bank[3][:, 0:NT * NE].rearrange("p (c e) -> p c e", e=NE)))
            link(nc.vector.tensor_reduce(r_small[:, 0, :], r_score, AX_X, ALU.max))
            link(nc.vector.tensor_tensor(r_cand, r_score, spread(r_small[:, 0, :]), ALU.is_equal))
            link(nc.vector.tensor_tensor(r_cand, r_cand, rank3, ALU.mult))
            link(nc.vector.tensor_reduce(r_small[:, 1, :], r_cand, AX_X, ALU.max))
            nc.vector.tensor_tensor(r_onehot, r_cand, spread(r_small[:, 1, :]), ALU.is_equal).then_inc(setup_dve, 1)
            dve.wait_ge(setup_mm, 3)
            nc.vector.tensor_tensor(bo_row[:, :], score_bank[2][:, 0:D], bo_row[:, :], ALU.add)
            nc.vector.tensor_copy(r_score, score_bank[0][:, 0:NT * NE].rearrange("p (c e) -> p c e", e=NE))
            link(nc.vector.tensor_scalar(r_int[:, 0:NE], score_bank[1][:, 0:NE], float(SLOTS - 1), None, ALU.add))
            link(nc.vector.tensor_scalar(r_int[:, 0:NE], r_int[:, 0:NE], SLOTS.bit_length() - 1, None,
                                         ALU.arith_shift_right))
            nc.vector.tensor_copy(r_groups, r_int[:, 0:NE])
            link(nc.vector.memset(r_start, 0.0))
            for e in range(NE - 1):
                link(nc.vector.tensor_tensor(r_start[:, e + 1:e + 2], r_start[:, e:e + 1], r_groups[:, e:e + 1],
                                             ALU.add))
            link(nc.vector.memset(r_gexp, 0.0))
            for e in range(1, NE):
                link(nc.vector.scalar_tensor_tensor(r_gexp, const("unit_iota"), r_start[:, e:e + 1], r_gexp,
                                                    ALU.is_ge, ALU.add))
            nc.vector.tensor_copy(unit_expert[:, :], r_gexp)
            link(nc.vector.tensor_scalar(r_start, r_start, float(SLOTS), None, ALU.mult))
            link(nc.vector.tensor_tensor(r_score, r_score, r_start.unsqueeze(1).broadcast_to([P, NT, NE]), ALU.add))
            link(nc.vector.tensor_tensor(r_score, r_score, r_onehot, ALU.mult))
            link(nc.vector.tensor_reduce(r_small[:, 0, :], r_score, AX_X, ALU.add))
            link(nc.vector.tensor_copy(r_int[:, 0:NT], r_small[:, 0, :]))
            link(nc.vector.tensor_scalar(r_int[:, NT:2 * NT], r_int[:, 0:NT], SLOTS.bit_length() - 1, None,
                                         ALU.arith_shift_right))
            link(nc.vector.tensor_copy(r_small[:, 1, :], r_int[:, NT:2 * NT]))
            link(nc.vector.scalar_tensor_tensor(r_small[:, 2, :], r_small[:, 1, :], -float(SLOTS), r_small[:, 0, :],
                                                ALU.mult, ALU.add))
            for c in range(NT):
                nc.vector.tensor_scalar(r_row[:, c, :], const("slot_of_row"), r_small[:, 2, c:c + 1], None,
                                        ALU.is_equal)
                last = nc.vector.tensor_scalar(r_group[:, c, :], const("unit_iota"), r_small[:, 1, c:c + 1],
                                               const("position_plus_1")[:, c:c + 1], ALU.is_equal, ALU.mult)
            last.then_inc(setup_dve, 1)
            dve.wait_ge(setup_mm, 4)
            nc.vector.tensor_scalar(r_gexp, score_bank[2][:, 0:NCOL], 0.0, EMPTY, ALU.is_equal, ALU.mult)
            link(nc.vector.tensor_scalar(r_tmp, score_bank[2][:, 0:NCOL], float(QUADS), const("first_run"),
                                         ALU.mult, ALU.add))
            link(nc.vector.tensor_tensor(row_index[:, :, 0], r_gexp, r_tmp, ALU.add))
            for j in range(RUN):
                link(nc.vector.scalar_tensor_tensor(row_index[:, :, 1 + j], score_bank[2][:, 0:NCOL],
                                                    const("first_row")[:, j:j + 1], r_gexp, ALU.add, ALU.add))
            nc.vector.memset(max_parts[:, :, :, :, :, :], 0.0).then_inc(ready, 1)
            dve.wait_ge(ready, 2)

            def rest_of_bank(c, k, banks, hi, hi_done, lo, lo_done):
                until(dve, hi_done, c, k + 1)
                nc.vector.tensor_tensor(lo[:, k, :], banks[k][:, :], hi[:, k, :].bitcast(F32), ALU.subtract)\
                    .then_inc(lo_done, 1)

            def rest_of_banks(c, banks, hi, hi_done, lo, lo_done):
                for k in range(KD):
                    rest_of_bank(c, k, banks, hi, hi_done, lo, lo_done)

            def normalise(c):
                for t in range(NT):
                    until(dve, ctxq_ready, c, t + 1)
                    heads = score_bank[t][:, :].rearrange("p (h w) -> p h w", w=32)
                    nc.vector.reciprocal(inv_sum[:, t, :].unsqueeze(2), heads[:, :, 0:1]).then_inc(inv_step, 1)
                for t in range(NT):
                    heads = score_bank[t][:, :].rearrange("p (h w) -> p h w", w=32)
                    until(dve, inv_step, c, t + 1)
                    nc.vector.tensor_tensor(ctxn[:, t, :].rearrange("p (h d) -> p h d", d=HD), heads[:, :, 1:VW],
                                            inv_sum[:, t, :].unsqueeze(2).broadcast_to([P, NH, HD]), ALU.mult)\
                        .then_inc(ctxn_done, 1)

            def qk_lo(b, g, i):
                until(dve, qkh_done, b, 2 * g + i + 1)
                nc.vector.scalar_tensor_tensor(qk_l[:, i, :], ffn_bank[i][:, :],
                                               qkv_bias[:, 2 * i + g:2 * i + g + 1],
                                               qk_h[:, i, :].bitcast(F32), ALU.add, ALU.subtract)\
                    .then_inc(qkl_done, 1)

            def after_attention(c, u):
                until(dve, x1_ready, c, 1)
                until(dve, attn_ready, c, u + 1)
                nc.vector.tensor_tensor(x2[:, 2 * u:2 * u + 2, :].rearrange("p t d -> p (t d)"),
                                        score_bank[2 + u][:, :],
                                        x1[:, 2 * u:2 * u + 2, :].rearrange("p t d -> p (t d)"), ALU.add)\
                    .then_inc(x2_done, 1)
                until(dve, x2_done, c, u + 1)
                for t in range(2 * u, 2 * u + 2):
                    nc.vector.bn_stats(stats2[:, t, :], x2[:, t, :]).then_inc(bn2_step, 1)

            def aggregate2(c):
                for t in range(NT):
                    until(dve, bn2_step, c, t + 1)
                    apart(dve, "DVE")
                    last = nc.vector.bn_aggr(mv2[:, t, :], stats2[:, t, :])
                last.then_inc(aggr2_step, 1)
                until(dve, aggr2_step, c, 1)
                nc.vector.tensor_scalar(minus_mean2[:, :], mv2[:, :, 0], -1.0, None, ALU.mult)
                nc.vector.tensor_scalar(var2[:, :], mv2[:, :, 1], EPS, None, ALU.add).then_inc(mv2_ready, 1)

            def k_stack_of(b, p):
                if p in ACT_K:
                    return
                until(dve, sel_ready, b, 2 * p + 2)
                nc.vector.tensor_scalar(k_stack[:, p, :], select_bank[p // 4][(2 * p + 1) % 4][:, :],
                                        minus_one_rows[:, 0:1], None, ALU.add).then_inc(ksel_done, 1)

            def head_max(b, h):
                until(dve, s_ready, b, h + 1)
                apart(dve, "DVE")
                for t in range(NT):
                    bank = score_bank[2 * (h % 2) + t // 2]
                    c0 = 2 * P * (t % 2)
                    lo = P if t == 0 else 0
                    block_ = bank[:, c0 + lo:c0 + 2 * P]
                    last = nc.vector.tensor_tensor_reduce(
                        out=block_, in0=block_, in1=mask[:, lo:2 * P],
                        scale=1.0, scalar=LOWEST, op0=ALU.add, op1=ALU.max, accum_out=row_max[:, t, h:h + 1])
                last.then_inc(max_done, 1)

            def max_split(b, half):
                until(dve, max_done, b, 8 * half + 8)
                src = row_max[:, :, 8 * half:8 * half + 8].rearrange("p t (j a) -> p t a j", a=2)
                for par in range(2):
                    nc.vector.tensor_copy(max_hi[:, :, half, par, :], src[:, :, par, :]).then_inc(maxhi_step, 1)
                for par in range(2):
                    until(dve, maxhi_step, b, 2 * half + par + 1)
                    hi = max_hi[:, :, half, par, :].bitcast(F32)
                    nc.vector.tensor_copy(max_parts[:, :, half, par, 0, :], hi)
                    last = nc.vector.tensor_tensor(max_parts[:, :, half, par, 1, :], src[:, :, par, :], hi,
                                                   ALU.subtract)
                last.then_inc(parts_done, 1)

            def outputs(c, u):
                if u == 0:
                    until(dve, residual_ready, c, 1)
                    dve.wait_ge(y_free, LEAD + c)
                until(dve, down_ready, c, u + 1)
                nc.vector.tensor_tensor(y[:, 2 * u:2 * u + 2, :].rearrange("p t d -> p (t d)"),
                                        ffn_bank[u][:, :],
                                        x2[:, 2 * u:2 * u + 2, :].rearrange("p t d -> p (t d)"), ALU.add)\
                    .then_inc(y_done, 1)

            def save_ctx(b, g):
                until(dve, ctx_ready, b, g + 1)
                nc.vector.tensor_copy(ctxT[:, g, :], mix_bank[g % 2][:, :]).then_inc(ctx_saved, 1)

            def weights_lo():
                dve.wait_ge(p2_raw, 48)
                dve.wait_ge(p2_zeroed, 1)
                for part in (0, BIAS_LO):
                    nc.vector.tensor_copy(bias_parts[part:part + 1, :], bias_raw[part:part + 1, :]).then_inc(p2_bias, 1)
                dve.wait_ge(p2_bias, 2)
                lo_row = slice(BIAS_LO, BIAS_LO + 1)
                nc.vector.tensor_tensor(bias_parts[lo_row, :], bias_raw[lo_row, :], bias_parts[lo_row, :].bitcast(F32),
                                        ALU.subtract)
                for i in range(NE):
                    dve.wait_ge(p2_hi, i + 1)
                    part = slice(KD * D * i, KD * D * i + KD * D)
                    nc.vector.tensor_tensor(we_l.rearrange("p e k o -> p (e k o)")[:, part], score_bank[i % 4][:, :],
                                            we_h.rearrange("p e k o -> p (e k o)")[:, part].bitcast(F32),
                                            ALU.subtract).then_inc(p2_weights, 1)

            def iteration(b, c, ahead):
                if b is not None:
                    qk_lo(b, 0, 0)
                    qk_lo(b, 0, 1)
                if c is not None:
                    normalise(c)
                if c is not None:
                    rest_of_banks(c, mix_bank, cn_h, cTh_done, cn_l, cTl_done)
                if b is not None:
                    k_stack_of(b, 0)
                    k_stack_of(b, 1)
                if c is not None:
                    after_attention(c, 0)
                if b is not None:
                    k_stack_of(b, 2)
                if c is not None:
                    after_attention(c, 1)
                    aggregate2(c)
                if b is not None:
                    k_stack_of(b, 3)
                else:
                    weights_lo()
                if b is not None:
                    head_max(b, 0)
                    qk_lo(b, 1, 0)
                    qk_lo(b, 1, 1)
                    head_max(b, 1)
                    head_max(b, 2)
                for k in range(KD):
                    if b is not None:
                        k_stack_of(b, 4 + k)
                    if c is not None:
                        rest_of_bank(c, k, mix_bank, cn_h, n2Th_done, cn_l, n2Tl_done)
                if b is not None:
                    for p in range(4 + KD, NPAIR):
                        k_stack_of(b, p)
                    for h in range(3, NH):
                        head_max(b, h)
                        if h == 7:
                            max_split(b, 0)
                        if h == STATS_AT and ahead:
                            stats(b + 1)
                    max_split(b, 1)
                if c is not None:
                    outputs(c, 0)
                if b is not None:
                    save_ctx(b, 0)
                    save_ctx(b, 1)
                if c is not None:
                    outputs(c, 1)
                if b is not None:
                    save_ctx(b, 2)
                    if ahead:
                        rest_of_banks(b + 1, input_bank, nT_h, nTh_done, nT_l, nTl_done)
                    save_ctx(b, 3)

            rest_of_banks(0, input_bank, nT_h, nTh_done, nT_l, nTl_done)
            iteration(0, None, True)
            with dve.Fori(1, NB - 1) as b:
                iteration(b, b - 1, True)
            iteration(NB - 1, NB - 2, False)
            iteration(None, NB - 1, False)

            def gather_table(m, i):
                nc.vector.tensor_copy(gather_rows[:, i % DEPTH:i % DEPTH + 1], row_index[:, bass.ds(m, 1), 0])\
                    .then_inc(p2_gather_rows, 1)

            def row_stats(m, i, n0):
                dve.wait_ge(p2_gather[i % DEPTH], n0 * (16 // DEPTH) + 16 * (i // DEPTH + 1))
                for j in range(RUN):
                    nc.vector.bn_stats(stats2[:, j, :], rows_in[i % DEPTH][:, j, :]).then_inc(p2_bn, 1)
                for j in range(RUN):
                    dve.wait_ge(p2_bn, m * RUN + (j + 1))
                    apart(dve, "DVE")
                    last = nc.vector.bn_aggr(mv2[:, j, :], stats2[:, j, :])
                last.then_inc(p2_mv, 1)

            def scale_shift(m, i):
                if not (isinstance(m, int) and m < 2):
                    dve.wait_ge(p2_norm, m - 1)
                dve.wait_ge(p2_std, m + 1)
                scale, shift = unit_scale[:, i % 2, :], unit_shift[:, i % 2, :]
                nc.vector.reciprocal(scale, unit_std[:, i % 2, :]).then_inc(p2_rstd, 1)
                dve.wait_ge(p2_rstd, m + 1)
                nc.vector.scalar_tensor_tensor(shift, mv2[:, :, 0], -1.0, scale, ALU.mult, ALU.mult)\
                    .then_inc(p2_scale, 1)

            def unit_lo(m, i):
                for k in range(KD):
                    dve.wait_ge(p2_nTh, m * KD + (k + 1))
                    nc.vector.tensor_tensor(p2_T[i % 2][1][:, k, :], mix_bank[k][:, :],
                                            p2_T[i % 2][0][:, k, :].bitcast(F32), ALU.subtract).then_inc(p2_nTl, 1)

            def unit_out(n, i, n0):
                if not (isinstance(n, int) and n < 2):
                    dve.wait_ge(p2_scatter[i % 2], n0 * (16 * RUN // 2) + 16 * RUN * (i // 2))
                nc.vector.tensor_copy(scatter_rows[:, i % 2, :], row_index[:, bass.ds(n, 1), 1:1 + RUN])\
                    .then_inc(p2_scatter_rows, 1)
                for u in range(2):
                    dve.wait_ge(p2_y, 2 * n + (u + 1))
                    nc.vector.tensor_tensor(
                        rows_out[i % 2][:, 2 * u:2 * u + 2, :].rearrange("p t d -> p (t d)"),
                        p2_banks[i % 2][u][:, :],
                        rows_in[i % DEPTH][:, 2 * u:2 * u + 2, :].rearrange("p t d -> p (t d)"), ALU.add)\
                        .then_inc(p2_out, 1)

            def units(n0):
                for i in range(DEPTH):
                    gather_table(n0 + (i + AHEAD), i + AHEAD)
                    row_stats(n0 + (i + 2), i + 2, n0)
                    unit_lo(n0 + (i + 1), i + 1)
                    scale_shift(n0 + (i + 2), i + 2)
                    unit_out(n0 + i, i, n0)

            for m in range(AHEAD):
                gather_table(m, m)
            for m in range(2):
                row_stats(m, m, 0)
                scale_shift(m, m)
            unit_lo(0, 0)
            units(0)
            with dve.Fori(DEPTH, NUNIT, DEPTH) as n0:
                units(n0)

        @block.tensor
        def _(pe):
            mm = nc.tensor.matmul

            pe.wait_ge(loaded, 16 * NLOAD)
            for m in range(6):
                for k in range(KD):
                    mm(score_bank[0][:, m:m + 1], wqkv_raw[:, k, P * m:P * m + P], ln_col[:, 1, k:k + 1],
                       start=k == 0, stop=k == KD - 1)
            for m in range(NM):
                for k in range(KD):
                    mm(score_bank[1][:, m:m + 1], w1_raw[:, k, P * m:P * m + P], ln_col[:, 3, k:k + 1],
                       start=k == 0, stop=k == KD - 1)
            pe.wait_ge(sign_done, 1)
            for c in range(NT):
                last = mm(score_bank[3][:, NE * c:NE * c + NE], const("position_code")[0:DPOS, P * c:P * c + P],
                   route[0:DPOS, NE:2 * NE], start=True, stop=True)
            last.then_inc(setup_mm, 1)
            pe.wait_ge(setup_dve, 1)
            for k in range(KD):
                last = mm(score_bank[2][:, 0:D], b_wide[:, k, :], wo_raw[:, k, :],
                          start=k == 0, stop=k == KD - 1)
            last.then_inc(setup_mm, 1)
            pe.wait_ge(setup_dve, 2)
            for c in range(NT):
                for c2 in range(c + 1):
                    mm(score_bank[0][:, NE * c:NE * c + NE], const("before") if c2 == c else const("ones"),
                       r_onehot[:, c2, :], start=c2 == 0, stop=c2 == c)
            for c in range(NT):
                last = mm(score_bank[1][:, 0:NE], const("ones"), r_onehot[:, c, :], start=c == 0, stop=c == NT - 1)
            last.then_inc(setup_mm, 1)
            pe.wait_ge(setup_dve, 3)
            for c in range(NT):
                last = mm(score_bank[2][:, 0:NCOL], r_row[:, c, :], r_group[:, c, :], start=c == 0, stop=c == NT - 1)
            last.then_inc(setup_mm, 1)
            pe.wait_ge(ready, 2)

            def split_product(out, pairs):
                terms = [(a[0], a[2]) for a in pairs] + [(a[1], a[2]) for a in pairs] + [(a[0], a[3]) for a in pairs]
                for i, (lhsT, rhs) in enumerate(terms):
                    last = mm(out, lhsT, rhs, start=i == 0, stop=i == len(terms) - 1)
                return last

            def transpose_rows(src, banks, ready_sem):
                for k in range(KD):
                    for t in range(NT):
                        last = nc.tensor.transpose(banks[k][:, P * t:P * t + P], src[:, t, P * k:P * k + P],
                                                   ident[:, :])
                    last.then_inc(ready_sem, 1)

            def input_transposes(b):
                if not (isinstance(b, int) and b == 0):
                    until(pe, exp_done, b - 1, NT * (NPAIR - 1) + 2)
                until(pe, n1_ready, b, 1)
                transpose_rows(normed, input_bank, nT_ready)

            def context_to_rows(c):
                until(pe, ctx_saved, c, 4)
                for t in range(NT):
                    for g in range(4):
                        last = nc.tensor.transpose(score_bank[t][:, P * g:P * g + P], ctxT[:, g, P * t:P * t + P],
                                                   ident[:, :])
                    last.then_inc(ctxq_ready, 1)

            def until_stacks(b, i, n):
                by_act = sum(p < n for p in ACT_K)
                if i == 0:
                    until(pe, qsel_done, b, n)
                else:
                    until(pe, ksel_done, b, n - by_act)
                    if by_act:
                        until(pe, ksel_by_act, b, by_act)

            def project_qk(b, g):
                if g == 0:
                    until(pe, nTh_done, b, KD)
                    until(pe, nTl_done, b, KD)
                for i in range(2):
                    if g == 1:
                        until_stacks(b, i, 4)
                    w = slice(D * i + P * g, D * i + P * g + P)
                    split_product(ffn_bank[i][:, :], [
                        (wqkv_h[:, k, w], wqkv_l[:, k, w], nT_h[:, k, :], nT_l[:, k, :]) for k in range(KD)
                    ]).then_inc(qk_ready, 1)

            def context_transposes(c):
                for t in range(NT):
                    until(pe, ctxn_done, c, t + 1)
                    for k in range(KD):
                        last = nc.tensor.transpose(mix_bank[k][:, P * t:P * t + P], ctxn[:, t, P * k:P * k + P],
                                                   ident[:, :])
                        if t == NT - 1:
                            last.then_inc(cT_ready, 1)

            def project_v(b):
                for u in range(2):
                    until(pe, qkl_done, b, u + 1)
                    for s in range(2):
                        c = slice(P * (2 * u + s), P * (2 * u + s) + P)
                        last = split_product(ffn_bank[u][:, D * s:D * s + D], [
                            (nT_h[:, k, c], nT_l[:, k, c], wqkv_h[:, k, 2 * D:], wqkv_l[:, k, 2 * D:])
                            for k in range(KD)])
                    last.then_inc(v_ready, 1)

            def project_out(c, u):
                until(pe, cTl_done, c, KD)
                for s in range(2):
                    cols = slice(P * (2 * u + s), P * (2 * u + s) + P)
                    last = split_product(score_bank[2 + u][:, D * s:D * s + D], [
                        (cn_h[:, k, cols], cn_l[:, k, cols], wo_h[:, k, :], wo_l[:, k, :]) for k in range(KD)])
                last.then_inc(attn_ready, 1)

            def stacks(b, p):
                if p % 4 == 0:
                    until(pe, qkl_done, b, p // 2 + 2)
                elif p == 1:
                    until(pe, v_done, b, 2)
                elif p == 5:
                    until(pe, max_done, b, 2)
                for i in range(2):
                    if p % 4 >= 2:
                        until_stacks(b, i, p - 1)
                    bank = select_bank[p // 4][(2 * p + i) % 4]
                    h, l = (("sel_qh", "sel_ql"), ("sel_kh", "sel_kl"))[i]
                    mm(bank[:, :], sel[h][:, p % 4, :], qk_h[:, i, :], start=True, stop=False)
                    mm(bank[:, :], sel[l][:, p % 4, :], qk_l[:, i, :], start=False, stop=True)\
                        .then_inc(sel_ready, 1)

            def scores(b, h, c):
                if h == 0 or h == 3:
                    until_stacks(b, 0, NPAIR if h else 3)
                    until_stacks(b, 1, NPAIR if h else 3)
                if h == 1:
                    if c is not None:
                        until(pe, x2_done, c, 2)
                elif h >= 2:
                    until(pe, max_done, b, h - 1)
                p = h // 2
                for t in range(NT):
                    bank = score_bank[2 * (h % 2) + t // 2]
                    c0 = 2 * P * (t % 2)
                    lo = P if t == 0 else 0
                    last = mm(bank[:, c0 + lo:c0 + 2 * P], q_pad[:, p, h % 2, P * t:P * t + P],
                              k_stack[:, p, P * (t - 1) + lo:P * (t + 1)], start=True, stop=True)
                last.then_inc(s_ready, 1)

            def n2_transposes(c):
                for t in range(NT):
                    until(pe, n2_ready, c, t + 1)
                    for k in range(KD):
                        last = nc.tensor.transpose(mix_bank[k][:, P * t:P * t + P], normed[:, t, P * k:P * k + P],
                                                   ident[:, :])
                        if t == NT - 1:
                            last.then_inc(n2T_ready, 1)

            def up(c, m, b):
                if m == 0:
                    until(pe, n2Tl_done, c, KD)
                    if b is not None:
                        until_stacks(b, 0, NPAIR - 1)
                        until_stacks(b, 1, NPAIR - 1)
                elif m >= 2:
                    until(pe, gelu_done, c, m - 1)
                w = slice(P * m, P * m + P)
                split_product(ffn_bank[m % 2][:, :], [
                    (w1_h[:, k, w], w1_l[:, k, w], cn_h[:, k, :], cn_l[:, k, :]) for k in range(KD)
                ]).then_inc(up_ready, 1)

            def max_transposes(b, half):
                until(pe, parts_done, b, half + 1)
                for t in range(NT):
                    last = nc.tensor.transpose(
                        mix_bank[half][0:16, P * t:P * t + P],
                        max_parts[:, t, half, :, :, :].rearrange("p a b c -> p (a b c)"), ident[:, :])
                last.then_inc(maxT_ready, 1)

            def down(c, t, part):
                if t == 0 and part == 0:
                    until(pe, gelu_done, c, NM)
                for m in range(NM // 4 * part, NM // 4 * (part + 1)):
                    last = mm(ffn_bank[t // 2][:, D * (t % 2):D * (t % 2) + D], hidden[:, m, P * t:P * t + P],
                              w2[:, m, :], start=m == 0, stop=m == NM - 1)
                if t % 2 and part == 3:
                    last.then_inc(down_ready, 1)

            def scores_T(b, p):
                if p % 4 == 0:
                    until(pe, max_rows[p // 4], b, 64)
                for kc in range(NT):
                    if p == 0:
                        until(pe, max_done, b, NH - 1 + kc // 2)
                    else:
                        until(pe, exp_done, b, NT * (p - 1) + kc + 1)
                    q1 = min(P * (kc + 2), L)
                    n = q1 - P * kc
                    mm(score_bank[kc][:, 0:2 * n].rearrange("p (h q) -> p h q", h=2),
                       k_stack[:, p, P * kc:P * kc + P], q_pad[:, p, :, P * kc:q1],
                       start=True, stop=True).then_inc(sT_ready, 1)

            def context(b, g):
                until(pe, probs_ready, b, 2 * g + 2)
                if g < 2:
                    until(pe, maxT_done, b, g + 1)
                else:
                    until(pe, ctx_saved, b, g - 1)
                for kc in range(NT):
                    n = 2 * P if kc < NT - 1 else P
                    for j in range(4):
                        slot = 2 * (g % 2) + j // 2
                        r0 = 4 * P * kc + n * (j % 2)
                        last = mm(mix_bank[g % 2][32 * j:32 * j + 32, P * kc:P * kc + n],
                                  v_ones[:, kc, VW * (4 * g + j):VW * (4 * g + j) + 32],
                                  probs[:, slot, r0:r0 + n], start=kc == 0, stop=kc == NT - 1,
                                  skip_group_check=True)
                last.then_inc(ctx_ready, 1)

            def weights():
                pe.wait_ge(p2_raw, 48)
                for e in range(NE):
                    if e == 2:
                        until(pe, x2_done, NB - 1, 2)
                    if e >= 4:
                        pe.wait_ge(p2_weights, e - 3)
                    for k in range(KD):
                        for o in range(KD):
                            last = nc.tensor.transpose(score_bank[e % 4][:, D * k + P * o:D * k + P * o + P],
                                                       we_raw[:, e, o, P * k:P * k + P], ident[:, :])
                    last.then_inc(p2_tr, 1)

            def iteration(b, c, ahead):
                if b is not None:
                    project_qk(b, 0)
                if c is not None:
                    context_to_rows(c)
                if b is not None:
                    project_v(b)
                if c is not None:
                    context_transposes(c)
                if b is not None:
                    stacks(b, 0)
                    stacks(b, 1)
                for u in range(2):
                    if c is not None:
                        project_out(c, u)
                    if b is not None:
                        stacks(b, 2 + u)
                if b is None:
                    weights()
                if b is not None:
                    scores(b, 0, c)
                    scores(b, 1, c)
                    project_qk(b, 1)
                    scores(b, 2, c)
                if c is not None:
                    n2_transposes(c)
                if b is not None:
                    for p in range(4, NPAIR):
                        stacks(b, p)
                for m in range(NM):
                    if c is not None:
                        up(c, m, b)
                    if b is not None:
                        scores(b, 3 + m, c)
                    if b is not None and m == MAX_AT:
                        max_transposes(b, 0)
                for t in range(2):
                    for part in range(4):
                        if b is not None and (t, part) in SCORES_AT:
                            scores(b, 11 + SCORES_AT.index((t, part)), c)
                        if c is not None:
                            down(c, t, part)
                if b is not None:
                    for p in range(NPAIR):
                        scores_T(b, p)
                        if p == 0:
                            max_transposes(b, 1)
                        for i, at_pair in enumerate(DOWN_AT):
                            if c is not None and p == at_pair:
                                down(c, 2 + i // 4, i % 4)
                        if p >= 3 and p % 2:
                            context(b, (p - 3) // 2)
                    if ahead:
                        input_transposes(b + 1)
                    context(b, 3)
                elif c is not None:
                    for i in range(8):
                        down(c, 2 + i // 4, i % 4)

            input_transposes(0)
            iteration(0, None, True)
            with pe.Fori(1, NB - 1) as b:
                iteration(b, b - 1, True)
            iteration(NB - 1, NB - 2, False)
            iteration(None, NB - 1, False)

            def unit_transposes(m, i):
                if not (isinstance(m, int) and m == 0):
                    pe.wait_ge(p2_nTl, m * KD)
                pe.wait_ge(p2_norm, m + 1)
                transpose_rows(unit_normed[i % 2], mix_bank, p2_nT)

            def unit_products(n, i):
                pe.wait_ge(p2_nTl, n * KD + KD)
                hi, lo = p2_T[i % 2]
                e = pe.value_load(unit_expert[0:1, bass.ds(n, 1)], min_val=0, max_val=NE - 1)
                for j in range(RUN):
                    dst = p2_banks[i % 2][j // 2][:, D * (j % 2):D * (j % 2) + D]
                    c = slice(P * j, P * j + P)
                    terms = [(a[:, k, c], w[:, bass.ds(e, 1), k, :]) for a, w in ((hi, we_h), (lo, we_h), (hi, we_l))
                             for k in range(KD)]
                    terms.append((all_ones[:, :], bias_of[:, bass.ds(e, 1), :]))
                    for t, (lhsT, rhs) in enumerate(terms):
                        last = mm(dst, lhsT, rhs, start=t == 0, stop=t == len(terms) - 1)
                    if j % 2:
                        last.then_inc(p2_y, 1)

            pe.wait_ge(p2_weights, NE)
            unit_transposes(0, 0)
            with pe.Fori(0, NUNIT, DEPTH) as n0:
                for i in range(DEPTH):
                    unit_transposes(n0 + (i + 1), i + 1)
                    unit_products(n0 + i, i)


_INS = ["L0_attn_x", "L0_attn_Wq", "L0_attn_bq", "L0_attn_Wk", "L0_attn_bk", "L0_attn_Wv", "L0_attn_bv",
        "L0_attn_Wo", "L0_attn_bo", "L0_attn_W1", "L0_attn_b1", "L0_attn_W2", "L0_attn_b2",
        "L0_attn_ln1_w", "L0_attn_ln1_b", "L0_attn_ln2_w", "L0_attn_ln2_b",
        "L0_ffn_tile_sigs", "L0_ffn_W", "L0_ffn_b"]


def kernel(**inputs):
    import concourse.bacc as bacc
    from concourse.bass_utils import run_bass_kernel_spmd

    nc = bacc.Bacc("TRN2", target_bir_lowering=False, num_devices=1, dynamic_dma_scratch_size=8192)
    arrays, args = {}, []
    for name in _INS:
        a = np.ascontiguousarray(inputs[name])
        arrays[f"in_{name}"] = a
        args.append(nc.dram_tensor(f"in_{name}", a.shape, mybir.dt.from_np(a.dtype), kind="ExternalInput").ap())
    consts, at = shape_constants()
    arrays["shape_constants"] = consts
    cst = nc.dram_tensor("shape_constants", consts.shape, F32, kind="ExternalInput").ap()
    scratch = nc.dram_tensor("attended", (L, NB * D), F32, kind="Internal").ap()
    out = nc.dram_tensor("out_rows", (NB * L, D), F32, kind="ExternalOutput").ap()
    build(nc, *args, cst, at, scratch, out)
    r = run_bass_kernel_spmd(nc, [arrays], core_ids=[0])
    return r.results[0]["out_rows"].reshape(NB, L, D)
```
